# Optimizing a Trainium2 kernel written in Bass

```python
import numpy as np
import jax
import jax.numpy as jnp

def _softmax(x, axis=-1):
    return jax.nn.softmax(x, axis=axis)

def _gelu(x):
    return jax.nn.gelu(x, approximate=True)

def _silu(x):
    return jax.nn.silu(x)

def _sigmoid(x):
    return jax.nn.sigmoid(x)

def _layernorm(x, axis=-1, eps=1e-05):
    m = jnp.mean(x, axis=axis, keepdims=True)
    v = jnp.var(x, axis=axis, keepdims=True)
    return (x - m) / jnp.sqrt(v + eps)

def _scatter_add(tgt, idx, src, axis=0):
    return tgt.at[idx].add(src)

def _segment_sum(src, seg, n):
    return jax.ops.segment_sum(src, seg, n)
kernel_name = 'mk_sandwich_d2_jaxref_r8_82e15a'

def setup_inputs(seed: int=0):
    np.random.seed(seed)
    _w = jnp.asarray

    def _L0_attn_setup():
        import jax, jax.numpy as jnp
        import numpy as np
        EMB = 128
        HEADS = 16
        HEAD_DIM = EMB // HEADS
        ROPE_BASE = 10000.0

        def rotate_half(x):
            x1 = x[..., ::2]
            x2 = x[..., 1::2]
            return jnp.stack((-x2, x1), axis=-1).reshape(x.shape)

        def rope_cos_sin(seq_len, head_dim):
            inv_freq = 1.0 / ROPE_BASE ** (jnp.arange(0, head_dim, 2, dtype=jnp.float32) / head_dim)
            pos = jnp.arange(seq_len, dtype=jnp.float32)
            freqs = jnp.outer(pos, inv_freq)
            emb = jnp.concatenate([freqs, freqs], -1)
            return (jnp.cos(emb)[None, None], jnp.sin(emb)[None, None])
        key = jax.random.key(seed)
        ks = jax.random.split(key, 5)
        B, S = (2, 256)
        x = jax.random.normal(ks[0], (B, S, EMB), dtype=jnp.float32)
        scale = EMB ** (-0.5)
        Wq = jax.random.normal(ks[1], (EMB, EMB), dtype=jnp.float32) * scale
        Wk = jax.random.normal(ks[2], (EMB, EMB), dtype=jnp.float32) * scale
        Wv = jax.random.normal(ks[3], (EMB, EMB), dtype=jnp.float32) * scale
        Wo = jax.random.normal(ks[4], (EMB, EMB), dtype=jnp.float32) * scale
        return {'x': x, 'Wq': Wq, 'Wk': Wk, 'Wv': Wv, 'Wo': Wo}
    _L0_attn_in = _L0_attn_setup()

    def _L0_ffn_setup():
        import jax, jax.numpy as jnp
        import numpy as np
        E, D, F = (8, 128, 512)
        B, S = (4, 256)

        def _layernorm(x, g, b, eps=1e-05):
            mu = jnp.mean(x, axis=-1, keepdims=True)
            var = jnp.var(x, axis=-1, keepdims=True)
            return (x - mu) * jax.lax.rsqrt(var + eps) * g + b
        key = jax.random.key(seed)
        ks = jax.random.split(key, 5)
        return {'input_features': jax.random.normal(ks[0], (B, S, D), jnp.float32), 'centroids': jax.random.normal(ks[1], (E, D), jnp.float32) * 0.1, 'ln_g': jnp.ones((E, D), jnp.float32), 'ln_b': jnp.zeros((E, D), jnp.float32), 'w1': jax.random.normal(ks[2], (E, F, D), jnp.float32) * (1.0 / np.sqrt(D).astype(np.float32)), 'b1': jnp.zeros((E, F), jnp.float32), 'w2': jax.random.normal(ks[3], (E, D, F), jnp.float32) * (1.0 / np.sqrt(F).astype(np.float32)), 'b2': jnp.zeros((E, D), jnp.float32)}
    _L0_ffn_in = _L0_ffn_setup()

    def _L1_attn_setup():
        import jax, jax.numpy as jnp
        import numpy as np
        SPS_AMPLIFY = 1.5
        SPS_DAMPEN = 0.3
        SPS_DEEP_QUESTION = 0.1
        SPS_EXCLAIM = 0.85
        SPS_QUESTION = 0.25
        SPS_SUPER_EXCLAIM = 0.95
        B, S, D = (4, 256, 128)
        NUM_HEADS = 16
        HEAD_DIM = D // NUM_HEADS
        SCALE = HEAD_DIM ** (-0.5)

        def sps_pro(x):
            xn = jax.nn.sigmoid(x)
            mult = jnp.where(xn > SPS_SUPER_EXCLAIM, 2.0, jnp.where(xn > SPS_EXCLAIM, SPS_AMPLIFY, jnp.where(xn < SPS_DEEP_QUESTION, 0.1, jnp.where(xn < SPS_QUESTION, SPS_DAMPEN, 1.0))))
            return x * mult
        key = jax.random.key(seed)
        k0, k1, k2, k3, k4 = jax.random.split(key, 5)
        s = 1.0 / np.sqrt(D)
        return {'x': jax.random.normal(k0, (B, S, D), dtype=jnp.float32), 'W_qkv': jax.random.uniform(k1, (D, 3 * D), dtype=jnp.float32, minval=-s, maxval=s), 'b_qkv': jax.random.uniform(k2, (3 * D,), dtype=jnp.float32, minval=-s, maxval=s), 'W_proj': jax.random.uniform(k3, (D, D), dtype=jnp.float32, minval=-s, maxval=s), 'b_proj': jax.random.uniform(k4, (D,), dtype=jnp.float32, minval=-s, maxval=s)}
    _L1_attn_in = _L1_attn_setup()

    def _L1_ffn_setup():
        import jax, jax.numpy as jnp
        import numpy as np
        MICRO_BATCHES = 2
        TOP_K = 2
        NUM_EXPERTS = 8
        B, S, D = (4, 512, 128)
        H = 4 * D
        key = jax.random.key(seed)
        ks = jax.random.split(key, 8)
        s = 0.02
        return {'x': jax.random.normal(ks[0], (B, S, D), jnp.float32), 'ln_scale': jnp.ones((D,), jnp.float32), 'ln_bias': jnp.zeros((D,), jnp.float32), 'attn_w': jax.random.normal(ks[1], (D, D), jnp.float32) * s, 'attn_b': jnp.zeros((D,), jnp.float32), 'gate_w': jax.random.normal(ks[2], (NUM_EXPERTS, D), jnp.float32) * s, 'w1': jax.random.normal(ks[3], (NUM_EXPERTS, D, H), jnp.float32) * s, 'b1': jnp.zeros((NUM_EXPERTS, H), jnp.float32), 'w2': jax.random.normal(ks[4], (NUM_EXPERTS, H, D), jnp.float32) * s, 'b2': jnp.zeros((NUM_EXPERTS, D), jnp.float32), 'next_w': jax.random.normal(ks[5], (D, D), jnp.float32) * s, 'next_b': jnp.zeros((D,), jnp.float32)}
    _L1_ffn_in = _L1_ffn_setup()
    _d = {'L0_attn_x': _L0_attn_in['x'], 'L0_attn_Wq': _L0_attn_in['Wq'], 'L0_attn_Wk': _L0_attn_in['Wk'], 'L0_attn_Wv': _L0_attn_in['Wv'], 'L0_attn_Wo': _L0_attn_in['Wo'], 'L0_ffn_centroids': _L0_ffn_in['centroids'], 'L0_ffn_ln_g': _L0_ffn_in['ln_g'], 'L0_ffn_ln_b': _L0_ffn_in['ln_b'], 'L0_ffn_w1': _L0_ffn_in['w1'], 'L0_ffn_b1': _L0_ffn_in['b1'], 'L0_ffn_w2': _L0_ffn_in['w2'], 'L0_ffn_b2': _L0_ffn_in['b2'], 'L1_attn_W_qkv': _L1_attn_in['W_qkv'], 'L1_attn_b_qkv': _L1_attn_in['b_qkv'], 'L1_attn_W_proj': _L1_attn_in['W_proj'], 'L1_attn_b_proj': _L1_attn_in['b_proj'], 'L1_ffn_ln_scale': _L1_ffn_in['ln_scale'], 'L1_ffn_ln_bias': _L1_ffn_in['ln_bias'], 'L1_ffn_attn_w': _L1_ffn_in['attn_w'], 'L1_ffn_attn_b': _L1_ffn_in['attn_b'], 'L1_ffn_gate_w': _L1_ffn_in['gate_w'], 'L1_ffn_w1': _L1_ffn_in['w1'], 'L1_ffn_b1': _L1_ffn_in['b1'], 'L1_ffn_w2': _L1_ffn_in['w2'], 'L1_ffn_b2': _L1_ffn_in['b2'], 'L1_ffn_next_w': _L1_ffn_in['next_w'], 'L1_ffn_next_b': _L1_ffn_in['next_b']}
    _x0 = _d['L0_attn_x']
    _d['L0_attn_x'] = jax.random.normal(jax.random.fold_in(jax.random.key(seed), 1), (4, 1024, 128), dtype=_x0.dtype)
    del _x0
    return _d

def reference(L0_attn_x, L0_attn_Wq, L0_attn_Wk, L0_attn_Wv, L0_attn_Wo, L0_ffn_centroids, L0_ffn_ln_g, L0_ffn_ln_b, L0_ffn_w1, L0_ffn_b1, L0_ffn_w2, L0_ffn_b2, L1_attn_W_qkv, L1_attn_b_qkv, L1_attn_W_proj, L1_attn_b_proj, L1_ffn_ln_scale, L1_ffn_ln_bias, L1_ffn_attn_w, L1_ffn_attn_b, L1_ffn_gate_w, L1_ffn_w1, L1_ffn_b1, L1_ffn_w2, L1_ffn_b2, L1_ffn_next_w, L1_ffn_next_b):

    def _L0_attn_ref(x, Wq, Wk, Wv, Wo):
        import jax, jax.numpy as jnp
        import numpy as np
        EMB = 128
        HEADS = 16
        HEAD_DIM = EMB // HEADS
        ROPE_BASE = 10000.0

        def rotate_half(x):
            x1 = x[..., ::2]
            x2 = x[..., 1::2]
            return jnp.stack((-x2, x1), axis=-1).reshape(x.shape)

        def rope_cos_sin(seq_len, head_dim):
            inv_freq = 1.0 / ROPE_BASE ** (jnp.arange(0, head_dim, 2, dtype=jnp.float32) / head_dim)
            pos = jnp.arange(seq_len, dtype=jnp.float32)
            freqs = jnp.outer(pos, inv_freq)
            emb = jnp.concatenate([freqs, freqs], -1)
            return (jnp.cos(emb)[None, None], jnp.sin(emb)[None, None])
        B, S, E = x.shape

        def shape_heads(t):
            return t.reshape(B, S, HEADS, HEAD_DIM).transpose(0, 2, 1, 3)
        q = shape_heads(x @ Wq.T)
        k = shape_heads(x @ Wk.T)
        v = shape_heads(x @ Wv.T)
        cos, sin = rope_cos_sin(S, HEAD_DIM)
        q = q * cos + rotate_half(q) * sin
        k = k * cos + rotate_half(k) * sin
        scale = HEAD_DIM ** (-0.5)
        scores = jnp.einsum('bhqd,bhkd->bhqk', q, k) * scale
        causal = jnp.triu(jnp.ones((S, S), dtype=bool), k=1)
        scores = jnp.where(causal, -jnp.inf, scores)
        attn = jax.nn.softmax(scores, axis=-1)
        out = jnp.einsum('bhqk,bhkd->bhqd', attn, v)
        out = out.transpose(0, 2, 1, 3).reshape(B, S, E)
        return out @ Wo.T

    def _L0_ffn_ref(input_features, centroids, ln_g, ln_b, w1, b1, w2, b2):
        import jax, jax.numpy as jnp
        import numpy as np
        E, D, F = (8, 128, 512)
        B, S = (4, 256)

        def _layernorm(x, g, b, eps=1e-05):
            mu = jnp.mean(x, axis=-1, keepdims=True)
            var = jnp.var(x, axis=-1, keepdims=True)
            return (x - mu) * jax.lax.rsqrt(var + eps) * g + b
        Bf, Sf, Df = input_features.shape
        x = input_features.reshape(-1, Df)
        aff = x @ centroids.T
        assign = jnp.argmax(aff, axis=1)
        order = jnp.argsort(assign)
        xs = x[order]
        es = assign[order]
        alpha = jax.nn.sigmoid(jnp.take_along_axis(aff[order], es[:, None], axis=1))
        nE = centroids.shape[0]
        y = jnp.zeros_like(xs)
        for e in range(nE):
            h = _layernorm(xs, ln_g[e], ln_b[e])
            h = jax.nn.relu(h @ w1[e].T + b1[e])
            ye = xs + h @ w2[e].T + b2[e]
            y = y + jnp.where((es == e)[:, None], ye, 0.0)
        out_sorted = alpha * y + (1.0 - alpha) * xs
        inv = jnp.argsort(order)
        return out_sorted[inv].reshape(Bf, Sf, Df)

    def _L1_attn_ref(x, W_qkv, b_qkv, W_proj, b_proj):
        import jax, jax.numpy as jnp
        import numpy as np
        SPS_AMPLIFY = 1.5
        SPS_DAMPEN = 0.3
        SPS_DEEP_QUESTION = 0.1
        SPS_EXCLAIM = 0.85
        SPS_QUESTION = 0.25
        SPS_SUPER_EXCLAIM = 0.95
        B, S, D = (4, 256, 128)
        NUM_HEADS = 16
        HEAD_DIM = D // NUM_HEADS
        SCALE = HEAD_DIM ** (-0.5)

        def sps_pro(x):
            xn = jax.nn.sigmoid(x)
            mult = jnp.where(xn > SPS_SUPER_EXCLAIM, 2.0, jnp.where(xn > SPS_EXCLAIM, SPS_AMPLIFY, jnp.where(xn < SPS_DEEP_QUESTION, 0.1, jnp.where(xn < SPS_QUESTION, SPS_DAMPEN, 1.0))))
            return x * mult
        qkv = jnp.einsum('bsd,de->bse', x, W_qkv) + b_qkv
        q, k, v = jnp.split(qkv, 3, axis=-1)
        attn = jnp.einsum('bsd,btd->bst', q, k) * SCALE
        attn = sps_pro(attn)
        attn = jax.nn.softmax(attn, axis=-1)
        out = jnp.einsum('bst,btd->bsd', attn, v)
        out = jnp.einsum('bsd,de->bse', out, W_proj) + b_proj
        return out

    def _L1_ffn_ref(x, ln_scale, ln_bias, attn_w, attn_b, gate_w, w1, b1, w2, b2, next_w, next_b):
        import jax, jax.numpy as jnp
        import numpy as np
        MICRO_BATCHES = 2
        TOP_K = 2
        NUM_EXPERTS = 8
        B, S, D = (4, 512, 128)
        H = 4 * D
        b, s, d = x.shape
        flat = x.reshape(b * s, d)
        mu = jnp.mean(flat, axis=-1, keepdims=True)
        var = jnp.mean((flat - mu) ** 2, axis=-1, keepdims=True)
        xn = (flat - mu) * jax.lax.rsqrt(var + 1e-05) * ln_scale + ln_bias
        x_attn = xn @ attn_w.T + attn_b + flat
        logits = x_attn @ gate_w.T
        _vals, _idx = jax.lax.top_k(logits, TOP_K)
        e = w1.shape[0]
        n = b * s // (MICRO_BATCHES * e)
        xe = x_attn.reshape(MICRO_BATCHES, e, n, d)
        h = jax.nn.gelu(jnp.einsum('mend,edh->menh', xe, w1) + b1[None, :, None, :], approximate=False)
        eo = jnp.einsum('menh,ehd->mend', h, w2) + b2[None, :, None, :]
        eo = eo.reshape(b * s, d)
        out = jax.nn.gelu(eo @ next_w.T + next_b, approximate=False)
        return out.reshape(b, s, d)
    x = L0_attn_x
    x = x + _layernorm(_L0_attn_ref(_layernorm(x, axis=-1), L0_attn_Wq, L0_attn_Wk, L0_attn_Wv, L0_attn_Wo), axis=-1)
    x = x + _layernorm(_L0_ffn_ref(_layernorm(x, axis=-1), L0_ffn_centroids, L0_ffn_ln_g, L0_ffn_ln_b, L0_ffn_w1, L0_ffn_b1, L0_ffn_w2, L0_ffn_b2), axis=-1)
    x = x + _layernorm(_L1_attn_ref(_layernorm(x, axis=-1), L1_attn_W_qkv, L1_attn_b_qkv, L1_attn_W_proj, L1_attn_b_proj), axis=-1)
    x = x + _layernorm(_L1_ffn_ref(_layernorm(x, axis=-1), L1_ffn_ln_scale, L1_ffn_ln_bias, L1_ffn_attn_w, L1_ffn_attn_b, L1_ffn_gate_w, L1_ffn_w1, L1_ffn_b1, L1_ffn_w2, L1_ffn_b2, L1_ffn_next_w, L1_ffn_next_b), axis=-1)
    return x

_drawn_inputs = setup_inputs


def setup_inputs(seed=0):
    import zlib

    import numpy as np

    out = dict(_drawn_inputs(seed))
    spreads = {'L0_ffn_ln_g': (1.0, 0.2),
     'L0_ffn_ln_b': (0.0, 0.272),
     'L0_ffn_b1': (0.0, 0.281),
     'L0_ffn_b2': (0.0, 0.1),
     'L1_ffn_ln_scale': (1.0, 0.6),
     'L1_ffn_ln_bias': (0.0, 0.8),
     'L1_ffn_attn_b': (0.0, 0.8),
     'L1_ffn_b1': (0.0, 0.383),
     'L1_ffn_b2': (0.0, 0.1),
     'L1_ffn_next_b': (0.0, 0.1)}
    factors = {'L1_ffn_attn_w': 4.912}
    for name, (base, spread) in spreads.items():
        noise = np.random.default_rng([zlib.crc32(name.encode()), seed]).standard_normal(out[name].shape)
        drawn = base * np.exp(spread * noise) if base else spread * noise
        out[name] = jnp.asarray(drawn.astype(out[name].dtype))
    for name, factor in factors.items():
        out[name] = (out[name] * factor).astype(out[name].dtype)
    return out
```

```python
from contextlib import ExitStack

import concourse.bass as bass
import numpy as np
from concourse import mybir

P = 128
D = 128
B, S = 4, 1024
TB = S // P
T = B * TB
H, HD = 16, 8
GH = 4
G = H // GH
E0, F0 = 8, 512
FC = F0 // P
EPS = 1e-5
SCALE = HD ** -0.5
LOW = -3.0e38

F32 = mybir.dt.float32
BF16 = mybir.dt.bfloat16
I32 = mybir.dt.int32
U32 = mybir.dt.uint32
ALU = mybir.AluOpType
ACT = mybir.ActivationFunctionType
AX = mybir.AxisListType


class Scope:

    def __init__(self, nc, ctx, phase=""):
        self.nc, self.ctx, self.phase = nc, ctx, phase

    def sb(self, name, shape, dt=F32):
        return self.ctx.enter_context(self.nc.sbuf_tensor(self.phase + name, shape, dt))

    def ps(self, name, shape, dt=F32):
        return self.ctx.enter_context(self.nc.psum_tensor(self.phase + name, shape, dt))

    def sem(self, name):
        return self.ctx.enter_context(self.nc.semaphore(self.phase + name))


def project_heads(nc, io, keep):
    X, ident, Q4, K4, Vg = keep["X"], keep["ident"], keep["Q4"], keep["K4"], keep["Vg"]
    tri = keep["tri"]
    with ExitStack() as ctx:
        m = Scope(nc, ctx, "p1_")
        W = m.sb("l0_w", [P, 5, D])
        rope = m.sb("rope", [P, 2, S])
        stats = m.sb("stats", [P, TB, 6])
        mv = m.sb("mv", [P, TB, 2])
        var, inv_var = m.sb("var", [P, TB]), m.sb("inv_var", [P, TB])
        rstd = m.sb("rstd", [P, TB])
        xn = m.sb("xn", [P, TB, D])
        xnT = m.sb("xnT", [P, S])
        part_c = m.sb("part_c", [P, 2, S])
        part_s = m.sb("part_s", [P, 2, S])
        rot = m.sb("rot", [P, 2, S])
        rest = m.sb("rest", [P, 2, 2, S])
        split = m.sb("split", [P, 2, 3, S], BF16)
        bank = [m.ps(f"proj{i}", [P, S]) for i in range(4)]

        s_x, s_w = m.sem("x_loaded"), m.sem("w_loaded")
        s_ident = m.sem("ident_done")
        s_var = m.sem("inv_var_steps")
        s_stat, s_agg, s_rstd, s_xn = m.sem("stats_done"), m.sem("mean_var_done"), m.sem("rstd_done"), m.sem("xn_ready")
        s_tr, s_xnT = m.sem("xn_transposed"), m.sem("xnT_ready")
        s_proj, s_v = m.sem("projected"), m.sem("v_projected")
        s_c, s_s, s_rot = m.sem("cos_part_done"), m.sem("sin_part_done"), m.sem("rotated")
        s_p1, s_r1, s_p2, s_r2, s_p3 = (m.sem(n) for n in ("part1", "rest1", "part2", "rest2", "part3"))
        s_vout = m.sem("v_kept")
        s_out = m.sem("splits_stored")
        s_z = m.sem("zeroed")
        apart = keep["apart"]
        block = ctx.enter_context(nc.Block())

        @block.sync
        def _(sp):
            sp.dma_start(X[:, :, :], io["x"].rearrange("b (t p) d -> p (b t) d", p=P)).then_inc(s_x, 16)
            sp.dma_start(W[:, :, :], io["l0_w"].rearrange("e j o -> e j o")[:, 0:5, :]).then_inc(s_w, 16)
            sp.dma_start(rope[:, :, :], io["rope"]).then_inc(s_w, 16)
            with sp.Fori(0, B) as b:
                sp.wait_ge(s_p3, 2 * b + 2)
                sp.wait_ge(s_p2, 2 * b + 2)
                sp.dma_start(io["q_parts"][:, bass.ds(b, 1), :, :].rearrange("i b r s -> r (b i) s"),
                             split[:, 0, :, :]).then_inc(s_out, 16)
                sp.dma_start(io["k_parts"][:, bass.ds(b, 1), :, :].rearrange("i b r s -> r (b i) s"),
                             split[:, 1, :, :]).then_inc(s_out, 16)
            sp.wait_ge(s_out, 32 * B)

        @block.gpsimd
        def _(pool):
            pool.memset(ident[:, :], 0.0).then_inc(s_ident, 1)
            pool.wait_ge(s_ident, 1)
            pool.affine_select(out=ident[:, :], in_=ident[:, :], compare_op=ALU.not_equal, fill=1.0, base=0,
                               pattern=[[-1, P]], channel_multiplier=1).then_inc(s_ident, 1)
            pool.memset(tri[:, :], 0.0).then_inc(s_z, 1)
            pool.wait_ge(s_z, 1)
            pool.affine_select(out=tri[:, 3 * P:4 * P], in_=tri[:, 3 * P:4 * P], compare_op=ALU.is_ge, fill=LOW,
                               base=0, pattern=[[-1, P]], channel_multiplier=1).then_inc(s_z, 1)
            pool.wait_ge(s_z, 2)
            pool.memset(Q4[64:P, :, :, :].bitcast(F32), 0.0).then_inc(s_z, 1)
            pool.memset(K4[64:P, :, :, :].bitcast(F32), 0.0).then_inc(s_z, 1)
            pool.wait_ge(s_z, 4)
            pool.memset(K4[96:99, :, :, :], 1.0).then_inc(s_z, 1)
            pool.wait_ge(s_z, 5)
            with pool.Fori(0, B) as b:
                for w in range(2):
                    pool.wait_ge(s_rot, 2 * b + w + 1)
                    pool.wait_ge(s_p1, 2 * b + w + 1)
                    pool.tensor_tensor(rest[:, w, 0, :], rot[:, w, :], split[:, w, 0, :], ALU.subtract).then_inc(s_r1, 1)
                    pool.wait_ge(s_p2, 2 * b + w + 1)
                    pool.tensor_tensor(rest[:, w, 1, :], rest[:, w, 0, :], split[:, w, 1, :], ALU.subtract).then_inc(s_r2, 1)
                    pool.wait_ge(s_r2, 2 * b + w + 1)
                    pool.sem_inc(apart["pool"], 1)
                    pool.tensor_copy(split[:, w, 2, :], rest[:, w, 1, :]).then_inc(s_p3, 1)
                    pool.wait_ge(s_p3, 2 * b + w + 1)

        @block.vector
        def _(dve):
            dve.memset(keep["Vone"][:, :, :, :, :], 0.0).then_inc(s_stat, 1)
            dve.wait_ge(s_stat, 1)
            dve.memset(keep["Vone"][:, :, :, :, HD:HD + 1], 1.0).then_inc(s_stat, 1)
            dve.wait_ge(s_x, 16)
            dve.wait_ge(s_w, 32)
            with dve.Fori(0, B) as b:
                for t in range(TB):
                    dve.bn_stats(stats[:, t, :], X[:, bass.ds(b * TB + t, 1), :].rearrange("p a d -> p (a d)")).then_inc(s_stat, 1)
                dve.wait_ge(s_stat, TB * b + TB + 2)
                dve.sem_inc(apart["dve"], 1)
                for t in range(TB):
                    dve.bn_aggr(mv[:, t, :], stats[:, t, :]).then_inc(s_agg, 1)
                dve.wait_ge(s_agg, TB * b + TB)
                dve.tensor_scalar(var[:, :], mv[:, :, 1], EPS, None, ALU.add).then_inc(s_var, 1)
                dve.wait_ge(s_var, 2 * b + 1)
                dve.reciprocal(inv_var[:, :], var[:, :]).then_inc(s_var, 1)
                dve.wait_ge(s_rstd, b + 1)
                for t in range(TB):
                    dve.tensor_scalar(xn[:, t, :], X[:, bass.ds(b * TB + t, 1), :].rearrange("p a d -> p (a d)"),
                                      mv[:, t, 0:1], rstd[:, t:t + 1], ALU.subtract, ALU.mult).then_inc(s_xn, 1)
                for w in range(2):
                    dve.wait_ge(s_proj, 4 * b + 2 * w + 1)
                    dve.tensor_tensor(part_c[:, w, :], bank[(1, 3)[w]][:, :], rope[:, 0, :], ALU.mult).then_inc(s_c, 1)
                    dve.wait_ge(s_proj, 4 * b + 2 * w + 2)
                    dve.tensor_tensor(part_s[:, w, :], bank[(2, 0)[w]][:, :], rope[:, 1, :], ALU.mult).then_inc(s_s, 1)
                    dve.wait_ge(s_s, 2 * b + w + 1)
                    dve.wait_ge(s_c, 2 * b + w + 1)
                    dve.tensor_tensor(rot[:, w, :], part_c[:, w, :], part_s[:, w, :], ALU.add).then_inc(s_rot, 1)
                dve.wait_ge(s_r1, 2 * b + 2)

        @block.scalar
        def _(act):
            with act.Fori(0, B) as b:
                act.wait_ge(s_var, 2 * b + 2)
                act.activation(rstd[:, :], inv_var[:, :], ACT.Sqrt).then_inc(s_rstd, 1)
                act.wait_ge(s_tr, b + 1)
                act.activation(xnT[:, :], bank[0][:, :], ACT.Copy).then_inc(s_xnT, 1)
                for w in range(2):
                    act.wait_ge(s_rot, 2 * b + w + 1)
                    act.activation(split[:, w, 0, :], rot[:, w, :], ACT.Copy).then_inc(s_p1, 1)
                    act.wait_ge(s_r1, 2 * b + w + 1)
                    act.activation(split[:, w, 1, :], rest[:, w, 0, :], ACT.Copy).then_inc(s_p2, 1)
                act.wait_ge(s_v, b + 1)
                for g in range(G):
                    act.activation(Vg[:, bass.ds(b * G + g, 1), :, :].rearrange("p a t r -> p (a t) r"),
                                   bank[1][:, :].rearrange("p (t g r) -> p t g r", t=TB, g=G)[:, :, g, :],
                                   ACT.Copy).then_inc(s_vout, 1)
                act.wait_ge(s_p3, 2 * b + 2)
                act.wait_ge(s_out, 32 * b + 32)

        @block.tensor
        def _(pe):
            pe.wait_ge(s_ident, 2)
            pe.wait_ge(s_w, 32)
            pe.wait_ge(s_stat, 2)
            with pe.Fori(0, B) as b:
                pe.wait_ge(s_xn, TB * b + TB)
                for t in range(TB):
                    tr = pe.transpose(bank[0][:, t * P:(t + 1) * P], xn[:, t, :], ident[:, :])
                tr.then_inc(s_tr, 1)
                pe.wait_ge(s_xnT, b + 1)
                for j, k in ((0, 1), (1, 2), (2, 3), (3, 0)):
                    for c in range(2):
                        mm = pe.matmul(bank[k][:, c * 512:(c + 1) * 512], W[:, j, :], xnT[:, c * 512:(c + 1) * 512],
                                       start=True, stop=True)
                    mm.then_inc(s_proj, 1)
                pe.wait_ge(s_c, 2 * b + 1)
                for t in range(TB):
                    mm = pe.matmul(bank[1][:, t * P:(t + 1) * P], xnT[:, t * P:(t + 1) * P], W[:, 4, :],
                                   start=True, stop=True)
                mm.then_inc(s_v, 1)
                pe.wait_ge(s_vout, G * b + G)
                pe.wait_ge(s_s, 2 * b + 2)


STEPS = [(0, kb) for kb in range(4)] + [(1, kb) for kb in range(8)]
NS = len(STEPS)
ST_LEAD, MAX_LEAD = 2, 21
MAX_STEPS = [
    [(0, 0, 128, "only"), (1, 0, 256, "only"), (2, 0, 384, "only"), (3, 0, 512, "only")],
    [(4, 0, 512, "first"), (5, 0, 512, "first"), (4, 512, 128, "last"), (5, 512, 256, "last")],
    [(6, 0, 512, "first"), (7, 0, 512, "first"), (6, 512, 384, "last"), (7, 512, 512, "last")],
]


def span(step):
    c, kb = STEPS[step]
    q0 = max(c * 512, kb * P)
    return q0, (c + 1) * 512 - q0


def causal_attention(nc, io, keep):
    ident, Q4, K4, Vg, Vone, tri = (keep[k] for k in ("ident", "Q4", "K4", "Vg", "Vone", "tri"))
    NB = G * NS
    with ExitStack() as ctx:
        m = Scope(nc, ctx, "p2_")
        PT = m.sb("probs", [P, 3, GH, 512])
        rowmax = m.sb("rowmax", [P, 2, GH, TB])
        half_max = m.sb("half_max", [P, 2, GH, 4])
        negmax = m.sb("negmax", [GH * TB, P])
        max_rest = m.sb("max_rest", [GH * TB, 2, P])
        max_parts = m.sb("max_parts", [GH * TB, 3, P], BF16)
        o_sb = m.sb("o_sb", [P, 2, 512])
        st = [m.ps(f"st{i}", [P, 2, 512]) for i in range(2)]
        sq = [m.ps(f"sq{i}", [P, 512]) for i in range(2)]
        o_ps = m.ps("o_ps", [P, 512])
        mt = m.ps("mt", [P, 512])

        s_ops = [m.sem(f"operands_loaded{g}") for g in range(G)]
        s_st, s_exp = m.sem("scores_ready"), m.sem("exps_done")
        s_diag = m.sem("diagonal_masked")
        s_pv = m.sem("pv_done")
        s_sq, s_max = m.sem("score_rows_ready"), m.sem("maxima_done")
        s_mt, s_neg = m.sem("maxima_transposed"), m.sem("maxima_negated")
        s_sp = m.sem("maxima_split_steps")
        s_row = m.sem("maxima_rows_stored")
        s_v = m.sem("v_group_ready")
        s_o = m.sem("o_evacuated")
        s_oout = [m.sem(f"o_stored{c}") for c in range(2)]
        apart = keep["apart"]
        block = ctx.enter_context(nc.Block())

        def batches(eng, body):
            with eng.Fori(0, B - 1) as b:
                body(b, False)
            body(B - 1, True)

        def load(sp, b, g):
            n = b * G + g
            for i in range(3):
                for j in range(3):
                    r = 24 * i + 8 * j
                    for dst, src, part in ((Q4, io["q_parts"], i), (K4, io["k_parts"], j)):
                        rows = src.rearrange("i b (g h d) s -> i d (b g) h s", g=G, h=GH)[part, :, bass.ds(n, 1), :, :]
                        sp.dma_start(dst[r:r + 8, g, :, :], rows.rearrange("d a h s -> d (a h) s")).then_inc(s_ops[g], 16)

        OPS = 18 * 16

        @block.sync
        def _(sp):
            for c in range(2):
                sp.sem_inc(s_oout[c], 16)
            for g in range(G):
                load(sp, 0, g)

            def max_rows(n, buf):
                sp.wait_ge(s_sp, 5 * n + 10)
                for i in range(3):
                    sp.dma_start(Q4[96 + i:97 + i, buf, :, :].rearrange("a h (t q) -> a (h t) q", q=P),
                                 max_parts[:, i, :]).then_inc(s_row, 16)

            def store_o(b, g, c):
                sp.wait_ge(s_o, 2 * (G * b + g) + c + 2)
                sp.dma_start(io["heads_out"][bass.ds(b * G + g, 1), :, c * 512:(c + 1) * 512].rearrange("a r s -> r (a s)"),
                             o_sb[:, c, :]).then_inc(s_oout[c], 16)

            max_rows(0, 0)

            def body(b, last):
                for g in range(G):
                    if not (last and g == G - 1):
                        max_rows(b * G + g + 1, (g + 1) % G)
                    store_o(b, g, 0)
                    if not last:
                        sp.wait_ge(s_st, 2 * NS * (b * G + g + 1))
                        load(sp, b + 1, g)
                    store_o(b, g, 1)

            batches(sp, body)
            for c in range(2):
                sp.wait_ge(s_oout[c], 16 * (B * G + 1))

        @block.tensor
        def _(pe):
            def scores(b, i):
                g, s = i // NS % G, i % NS
                b = b + i // NB
                c, kb = STEPS[s]
                q0, w = span(s)
                if s == 0:
                    pe.wait_ge(s_row, 48 * (b * G + g + 1))
                def tile(hp):
                    u = 2 * ((b * G + g) * NS + s) + hp
                    pe.wait_ge(s_exp, u + 1)
                    for h in (0, 1):
                        mm = pe.matmul(st[hp][:, h, 0:w], K4[:, g, 2 * hp + h, kb * P:(kb + 1) * P],
                                       Q4[:, g, 2 * hp + h, q0:q0 + w], start=True, stop=True)
                    mm.then_inc(s_st, 1)
                return [lambda: tile(0), lambda: tile(1)]

            def maxima(b, i):
                g, ms = i // NS % G, i % NS
                b = b + i // NB
                h = ms // 3
                if ms == 0:
                    pe.wait_ge(s_ops[g], OPS * (b + 1))
                def tile(j):
                    qb, k0, w, _ = MAX_STEPS[ms % 3][j]
                    n = 4 * ((b * G + g) * NS + ms) + j
                    pe.wait_ge(s_max, n + 1)
                    pe.matmul(sq[j % 2][:, 0:w], Q4[0:96, g, h, qb * P:(qb + 1) * P], K4[0:96, g, h, k0:k0 + w],
                              start=True, stop=True).then_inc(s_sq, 1)
                return [lambda j=j: tile(j) for j in range(4)]

            def transpose_max(n, par):
                pe.wait_ge(s_max, 4 * NS * (n + 1) + 2)
                pe.wait_ge(s_neg, n + 1)
                pe.matmul(mt[0:GH * TB, 0:P], rowmax[:, par, :, :].rearrange("p h t -> p (h t)"), ident[:, :],
                          is_transpose=True, start=True, stop=True).then_inc(s_mt, 1)

            def pv(b, i):
                g, s = i // NS, i % NS
                c, kb = STEPS[s]
                q0, w = span(s)
                n = b * G + g
                if s == 0:
                    pe.wait_ge(s_v, n + 1)
                if kb == 0:
                    pe.wait_ge(s_o, 2 * n + c + 1)
                if kb >= 4 * c:
                    pe.wait_ge(s_diag, TB * n + kb + 1)
                else:
                    pe.wait_ge(s_exp, 2 * (n * NS + s) + 4)
                for j in range(GH):
                    mm = pe.matmul(o_ps[32 * j:32 * j + 32, q0 - c * 512:512], Vone[:, g % 2, kb, j, :],
                                   PT[:, s % 3, j, 0:w], start=(kb == 0), stop=(kb == 4 * c + 3))
                mm.then_inc(s_pv, 1)

            for i in range(MAX_LEAD):
                for t in maxima(0, i):
                    t()
                if i == NS + 1:
                    transpose_max(0, 0)
            for i in range(ST_LEAD):
                for t in scores(0, i):
                    t()

            def body(b, last):
                for i in range(NB):
                    sc = scores(b, i + ST_LEAD) if not (last and i + ST_LEAD >= NB) else []
                    mx = maxima(b, i + MAX_LEAD) if not (last and i + MAX_LEAD >= NB) else []
                    for k in range(2):
                        for t in sc[k:k + 1] + mx[2 * k:2 * k + 2]:
                            t()
                    if i % NS == 4 and not (last and i // NS == G - 1):
                        transpose_max(b * G + i // NS + 1, (i // NS + 1) % 2)
                    pv(b, i)

            batches(pe, body)

        @block.vector
        def _(dve):
            def maxima(b, i):
                g, ms = i // NS % G, i % NS
                b = b + i // NB
                h = ms // 3
                n0 = 4 * ((b * G + g) * NS + ms)
                if ms == 0:
                    dve.wait_ge(s_mt, b * G + g + 1)
                for j, (qb, k0, w, how) in enumerate(MAX_STEPS[ms % 3]):
                    dve.wait_ge(s_sq, n0 + j + 1)
                    out = rowmax[:, g % 2, h, qb:qb + 1]
                    part = half_max[:, g % 2, h, qb - 4:qb - 3] if qb >= 4 else None
                    if how == "first":
                        dve.tensor_reduce(part, sq[j % 2][:, 0:w], AX.X, ALU.max).then_inc(s_max, 1)
                        continue
                    if how == "last":
                        dve.wait_ge(s_max, n0 + j + 1)
                    dve.sem_inc(apart["dve"], 1)
                    dve.tensor_tensor_reduce(out=sq[j % 2][:, 0:w], in0=sq[j % 2][:, 0:w], in1=tri[:, 512 - w:512], scale=1.0,
                                             scalar=(LOW if how == "only" else part), op0=ALU.add, op1=ALU.max,
                                             accum_out=out).then_inc(s_max, 1)

            dve.sem_inc(s_max, 2)
            dve.sem_inc(s_mt, 2)
            for i in range(MAX_LEAD):
                maxima(0, i)

            def body(b, last):
                for i in range(NB):
                    if not (last and i + MAX_LEAD >= NB):
                        maxima(b, i + MAX_LEAD)

            batches(dve, body)

        @block.scalar
        def _(act):
            def exps(b, i):
                s = i % NS
                _, w = span(s)
                n = (b * G) * NS + i
                act.wait_ge(s_pv, n + 1)
                for hp in range(2):
                    act.wait_ge(s_st, 2 * n + hp + 1)
                    act.activation(PT[:, s % 3, 2 * hp:2 * hp + 2, 0:w], st[hp][:, :, 0:w], ACT.Exp,
                                   scale=SCALE).then_inc(s_exp, 1)

            def negate(n):
                act.wait_ge(s_mt, n + 3)
                act.wait_ge(s_sp, 5 * n + 5)
                act.activation(negmax[:, :], mt[0:GH * TB, 0:P], ACT.Copy, scale=-1.0).then_inc(s_neg, 1)

            act.sem_inc(s_exp, 2)
            act.sem_inc(s_o, 1)
            act.sem_inc(s_neg, 1)
            negate(0)
            for i in range(ST_LEAD):
                exps(0, i)

            def body(b, last):
                for i in range(NB):
                    g, s = i // NS, i % NS
                    if not (last and i + ST_LEAD >= NB):
                        exps(b, i + ST_LEAD)
                    if s == 4 and not (last and g == G - 1):
                        negate(b * G + g + 1)
                    if s in (3, NS - 1):
                        c = int(s > 3)
                        n = b * G + g
                        act.wait_ge(s_pv, b * NB + i + 4)
                        act.wait_ge(s_oout[c], 16 * n + 16)
                        act.activation(o_sb[:, c, :], o_ps[:, :], ACT.Copy).then_inc(s_o, 1)

            batches(act, body)

        @block.gpsimd
        def _(pool):
            def v_group(n, par):
                pool.wait_ge(s_pv, NS * n - NS + 3)
                pool.sem_inc(apart["pool"], 1)
                pool.tensor_copy(Vone[:, par, :, :, 0:HD],
                                 Vg[:, bass.ds(n, 1), :, :].rearrange("p a t (h d) -> p (a t) h d", h=GH)).then_inc(s_v, 1)
                pool.wait_ge(s_v, n + 1)

            def split_max(n, first=False):
                pool.wait_ge(s_neg, n + 2)
                if not first:
                    pool.wait_ge(s_row, 48 * n)
                src = negmax[:, :]
                for i in range(3):
                    pool.sem_inc(apart["pool"], 1)
                    pool.tensor_copy(max_parts[:, i, :], src).then_inc(s_sp, 1)
                    pool.wait_ge(s_sp, 5 * n + 2 * i + 6)
                    if i < 2:
                        pool.tensor_tensor(max_rest[:, i, :], src, max_parts[:, i, :], ALU.subtract).then_inc(s_sp, 1)
                        pool.wait_ge(s_sp, 5 * n + 2 * i + 7)
                        src = max_rest[:, i, :]

            def mask(b, i):
                s = i % NS
                c, kb = STEPS[s]
                if kb < 4 * c:
                    return
                pool.wait_ge(s_exp, 2 * (b * NB + i) + 4)
                pool.sem_inc(apart["pool"], 1)
                part = PT[:, s % 3, :, 0:P]
                pool.affine_select(out=part, in_=part, compare_op=ALU.is_ge, fill=0.0, base=0,
                                   pattern=[[0, GH], [1, P]], channel_multiplier=-1).then_inc(s_diag, 1)
                pool.wait_ge(s_diag, TB * G * b + TB * (i // NS) + kb + 1)

            pool.sem_inc(s_pv, 3)
            pool.sem_inc(s_sp, 5)
            pool.tensor_copy(Vone[:, 0, :, :, 0:HD], Vg[:, 0, :, :].rearrange("p t (h d) -> p t h d", h=GH)).then_inc(s_v, 1)
            pool.wait_ge(s_v, 1)
            split_max(0, first=True)
            for i in range(ST_LEAD):
                mask(0, i)

            def body(b, last):
                for i in range(NB):
                    g, s = i // NS, i % NS
                    if not (last and i + ST_LEAD >= NB):
                        mask(b, i + ST_LEAD)
                    if not (last and g == G - 1):
                        if s == 3:
                            v_group(b * G + g + 1, (g + 1) % 2)
                        if s == 5:
                            split_max(b * G + g + 1)

            batches(pool, body)


RING = 4
MAXTILES = -(-(T + E0 - 1) // RING) * RING


def merge_heads(nc, io, keep):
    X, ident, XN, XH = keep["X"], keep["ident"], keep["XN"], keep["XH"]
    with ExitStack() as ctx:
        m = Scope(nc, ctx, "p3_")
        Wo = m.sb("wo", [P, D])
        C = m.sb("centroids", [P, E0])
        att = m.sb("att", [P, B, S])
        sums = m.sb("sums", [P, B, S])
        recip = m.sb("recip", [P, S])
        attT = m.sb("attT", [P, S])
        stats = m.sb("stats", [P, 2, TB, 6])
        mv = m.sb("mv", [P, 2, TB, 2])
        var, inv, rstd = m.sb("var", [P, 3, TB]), m.sb("inv", [P, 3, TB]), m.sb("rstd", [P, 3, TB])
        yn = m.sb("yn", [P, TB, D])
        xn = m.sb("xn", [P, TB, D])
        xnT = m.sb("xnT", [P, S])
        y_ps = m.ps("y_ps", [P, TB, D])
        t_ps = m.ps("t_ps", [P, S])
        a_ps = m.ps("a_ps", [P, TB, E0])

        s_w = m.sem("w_loaded")
        s_att = m.sem("att_loaded")
        s_rc, s_attT, s_y = m.sem("sums_inverted"), m.sem("attT_ready"), m.sem("y_ready")
        s_st = m.sem("ln_steps")
        s_in, s_rt = m.sem("inverse_variance_ready"), m.sem("rstd_ready")
        s_yn, s_x = m.sem("y_normed"), m.sem("x_updated")
        s_xn, s_xh = m.sem("xn_ready"), m.sem("xh_ready")
        s_kept = m.sem("xn_kept")
        s_tr, s_xnT, s_a, s_af = m.sem("xn_transposed"), m.sem("xnT_ready"), m.sem("affinity_ready"), m.sem("affinity_kept")
        apart = keep["apart"]
        block = ctx.enter_context(nc.Block())

        @block.sync
        def _(sp):
            sp.dma_start(Wo[:, :], io["l0_w"][:, 5, :]).then_inc(s_w, 16)
            sp.dma_start(C[:, :], io["centroids"]).then_inc(s_w, 16)
            for b in range(B):
                for g in range(G):
                    rows = io["heads_out"][b * G + g, :, :].rearrange("(j r) s -> j r s", j=GH)
                    for j in range(GH):
                        p0 = 32 * g + HD * j
                        sp.dma_start(att[p0:p0 + HD, b, :], rows[j, 0:HD, :]).then_inc(s_att, 16)
                        sp.dma_start(sums[p0:p0 + HD, b, :], rows[j, HD:HD + 1, :].broadcast_to([HD, S])).then_inc(s_att, 16)

        @block.vector
        def _(dve):
            dve.wait_ge(s_att, 16 * 2 * B * H)
            with dve.Fori(0, B) as b:
                dve.reciprocal(recip[:, :], sums[:, bass.ds(b, 1), :].rearrange("p a s -> p (a s)")).then_inc(s_rc, 1)
                dve.wait_ge(s_rc, b + 1)
                dve.tensor_tensor(attT[:, :], att[:, bass.ds(b, 1), :].rearrange("p a s -> p (a s)"), recip[:, :],
                                  ALU.mult).then_inc(s_attT, 1)
                dve.wait_ge(s_y, b + 1)
                for t in range(TB):
                    dve.bn_stats(stats[:, 0, t, :], y_ps[:, t, :]).then_inc(s_st, 1)
                k = b * (4 * TB + 4)
                dve.wait_ge(s_st, k + TB)
                dve.sem_inc(apart["dve"], 1)
                for t in range(TB):
                    dve.bn_aggr(mv[:, 0, t, :], stats[:, 0, t, :]).then_inc(s_st, 1)
                dve.wait_ge(s_st, k + 2 * TB)
                dve.tensor_scalar(var[:, 0, :], mv[:, 0, :, 1], EPS, None, ALU.add).then_inc(s_st, 1)
                dve.wait_ge(s_st, k + 2 * TB + 1)
                dve.reciprocal(inv[:, 0, :], var[:, 0, :]).then_inc(s_in, 1)
                dve.wait_ge(s_rt, 3 * b + 1)
                for t in range(TB):
                    dve.tensor_scalar(yn[:, t, :], y_ps[:, t, :], mv[:, 0, t, 0:1], rstd[:, 0, t:t + 1],
                                      ALU.subtract, ALU.mult).then_inc(s_yn, 1)
                dve.wait_ge(s_yn, TB * b + TB)
                rows = X[:, bass.ds(b * TB, TB), :]
                dve.tensor_tensor(rows, rows, yn[:, :, :], ALU.add).then_inc(s_x, 1)
                dve.wait_ge(s_x, b + 1)
                dve.sem_inc(apart["dve"], 1)
                for t in range(TB):
                    dve.bn_stats(stats[:, 1, t, :], X[:, bass.ds(b * TB + t, 1), :].rearrange("p a d -> p (a d)")).then_inc(s_st, 1)
                dve.wait_ge(s_st, k + 3 * TB + 1)
                dve.sem_inc(apart["dve"], 1)
                for t in range(TB):
                    dve.bn_aggr(mv[:, 1, t, :], stats[:, 1, t, :]).then_inc(s_st, 1)
                dve.wait_ge(s_st, k + 4 * TB + 1)
                dve.tensor_scalar(var[:, 1, :], mv[:, 1, :, 1], EPS, None, ALU.add).then_inc(s_st, 1)
                dve.wait_ge(s_st, k + 4 * TB + 2)
                dve.reciprocal(inv[:, 1, :], var[:, 1, :]).then_inc(s_in, 1)
                dve.wait_ge(s_in, 3 * b + 2)
                dve.tensor_tensor(var[:, 2, :], mv[:, 1, :, 1], inv[:, 1, :], ALU.mult).then_inc(s_st, 1)
                dve.wait_ge(s_st, k + 4 * TB + 3)
                dve.tensor_scalar(rstd[:, 2, :], var[:, 2, :], EPS, None, ALU.add).then_inc(s_st, 1)
                dve.wait_ge(s_st, k + 4 * TB + 4)
                dve.reciprocal(inv[:, 2, :], rstd[:, 2, :]).then_inc(s_in, 1)
                dve.wait_ge(s_rt, 3 * b + 3)
                for t in range(TB):
                    dve.tensor_scalar(xn[:, t, :], X[:, bass.ds(b * TB + t, 1), :].rearrange("p a d -> p (a d)"),
                                      mv[:, 1, t, 0:1], rstd[:, 1, t:t + 1], ALU.subtract, ALU.mult).then_inc(s_xn, 1)
                dve.wait_ge(s_xn, TB * b + TB)
                for t in range(TB):
                    dve.tensor_scalar(XH[:, bass.ds(b * TB + t, 1), :].rearrange("p a d -> p (a d)"), xn[:, t, :],
                                      rstd[:, 2, t:t + 1], None, ALU.mult).then_inc(s_xh, 1)
                dve.wait_ge(s_a, b + 1)
                dve.tensor_copy(keep["aff"][:, bass.ds(b * TB, TB), :], a_ps[:, :, :]).then_inc(s_af, 1)
                dve.wait_ge(s_af, b + 1)
                dve.wait_ge(s_xh, TB * b + TB)
                dve.wait_ge(s_kept, b + 1)

        @block.scalar
        def _(act):
            with act.Fori(0, B) as b:
                for k in range(3):
                    act.wait_ge(s_in, 3 * b + k + 1)
                    act.activation(rstd[:, k, :], inv[:, k, :], ACT.Sqrt).then_inc(s_rt, 1)
                act.wait_ge(s_tr, b + 1)
                act.activation(xnT[:, :], t_ps[:, :], ACT.Copy).then_inc(s_xnT, 1)

        @block.gpsimd
        def _(pool):
            with pool.Fori(0, B) as b:
                pool.wait_ge(s_xn, TB * b + TB)
                pool.sem_inc(apart["pool"], 1)
                pool.tensor_copy(XN[:, bass.ds(b * TB, TB), :], xn[:, :, :]).then_inc(s_kept, 1)
                pool.wait_ge(s_kept, b + 1)

        @block.tensor
        def _(pe):
            pe.wait_ge(s_w, 32)
            with pe.Fori(0, B) as b:
                pe.wait_ge(s_attT, b + 1)
                for t in range(TB):
                    mm = pe.matmul(y_ps[:, t, :], attT[:, t * P:(t + 1) * P], Wo[:, :], start=True, stop=True)
                mm.then_inc(s_y, 1)
                pe.wait_ge(s_xn, TB * b + TB)
                for t in range(TB):
                    mm = pe.transpose(t_ps[:, t * P:(t + 1) * P], xn[:, t, :], ident[:, :])
                mm.then_inc(s_tr, 1)
                pe.wait_ge(s_xnT, b + 1)
                for t in range(TB):
                    mm = pe.matmul(a_ps[:, t, :], xnT[:, t * P:(t + 1) * P], C[:, :], start=True, stop=True)
                mm.then_inc(s_a, 1)


def route(nc, io, keep):
    XH, aff, pos, gate, tile_expert = keep["XH"], keep["aff"], keep["pos"], keep["gate"], keep["tile_expert"]
    NE = T * E0
    with ExitStack() as ctx:
        m = Scope(nc, ctx, "p4_")
        top = m.sb("top", [P, T])
        tied = m.sb("tied", [P, T, E0])
        early = m.sb("early", [P, E0])
        score = m.sb("score", [P, T, E0])
        best = m.sb("best", [P, T])
        chosen = m.sb("chosen", [P, T, E0])
        chosen_bf = m.sb("chosen_bf", [P, T, E0], BF16)
        before = m.sb("before", [P, P], BF16)
        ones = m.sb("ones", [P, P], BF16)
        scan = m.sb("scan", [P, 6, T, E0])
        steps = m.sb("steps", [P, T])
        over = m.sb("over", [P, E0, T])
        tiles = m.sb("tiles", [P, E0])
        lower = m.sb("lower", [P, E0, E0])
        prod = m.sb("prod", [P, E0, E0])
        first = m.sb("first", [P, E0])
        last = m.sb("last", [P, E0])
        index = m.sb("index", [P, MAXTILES])
        past = m.sb("past", [P, MAXTILES, E0])
        owner = m.sb("owner", [P, MAXTILES])
        place = m.sb("place", [P, T, E0])
        start = m.sb("start", [P, E0])
        at = m.sb("at", [P, T])
        e_neg = m.sb("e_neg", [P, T])
        zeros = m.sb("zeros", [P, MAXTILES, D])
        rank_ps = m.ps("rank_ps", [P, NE])
        count_ps = m.ps("count_ps", [P, NE])

        s_c, s_z = m.sem("constants"), m.sem("zeros_stored")
        s_zm = m.sem("zeros_made")
        s_d, s_oh, s_cnt, s_e = m.sem("router_steps"), m.sem("chosen_ready"), m.sem("counts_ready"), m.sem("gate_exp")
        s_pos, s_sc = m.sem("places_ready"), m.sem("rows_placed")
        block = ctx.enter_context(nc.Block())

        @block.sync
        def _(sp):
            sp.wait_ge(s_zm, 1)
            sp.dma_start(io["sorted_in"].rearrange("(n p) d -> p n d", p=P), zeros[:, :, :]).then_inc(s_z, 16)

        @block.gpsimd
        def _(pool):
            n = 0
            def step(ins):
                nonlocal n
                n += 1
                ins.then_inc(s_c, 1)
                pool.wait_ge(s_c, n)
            step(pool.iota(early[:, :], [[-1, E0]], base=E0, channel_multiplier=0, allow_small_or_imprecise_dtypes=True))
            step(pool.iota(steps[:, :], [[P, T]], base=0, channel_multiplier=0, allow_small_or_imprecise_dtypes=True))
            step(pool.iota(index[:, :], [[1, MAXTILES]], base=0, channel_multiplier=0, allow_small_or_imprecise_dtypes=True))
            step(pool.memset(ones[:, :], 1.0))
            step(pool.memset(lower[:, :, :], 1.0))
            step(pool.affine_select(out=before[:, :], in_=ones[:, :], compare_op=ALU.is_gt, fill=0.0, base=0,
                                    pattern=[[1, P]], channel_multiplier=-1))
            step(pool.affine_select(out=lower[:, :, :], in_=lower[:, :, :], compare_op=ALU.is_gt, fill=0.0, base=0,
                                    pattern=[[1, E0], [-1, E0]], channel_multiplier=0))
            pool.wait_ge(s_pos, 1)
            pool.wait_ge(s_z, 16)
            for t in range(T):
                pool.indirect_dma_start(io["sorted_in"], bass.IndirectOffsetOnAxis(ap=pos[:, t:t + 1], axis=0),
                                        XH[:, t, :], None).then_inc(s_sc, 16)
            pool.wait_ge(s_sc, 16 * T)

        @block.tensor
        def _(pe):
            pe.wait_ge(s_c, 7)
            pe.wait_ge(s_oh, 1)
            oh = chosen_bf[:, :, :].rearrange("p t e -> p (t e)")
            pe.matmul(rank_ps[:, :], before[:, :], oh, start=True, stop=True).then_inc(s_cnt, 1)
            pe.matmul(count_ps[:, :], ones[:, :], oh, start=True, stop=True).then_inc(s_cnt, 1)

        @block.scalar
        def _(act):
            act.wait_ge(s_d, 1)
            act.activation(e_neg[:, :], top[:, :], ACT.Exp, scale=-1.0).then_inc(s_e, 1)

        @block.vector
        def _(dve):
            n = 0
            def step(ins):
                nonlocal n
                n += 1
                ins.then_inc(s_d, 1)
                dve.wait_ge(s_d, n)
            def over_e(x):
                return x.unsqueeze(2).broadcast_to([P, T, E0])
            step(dve.tensor_reduce(top[:, :], aff[:, :, :], AX.X, ALU.max))
            dve.memset(zeros[:, :, :], 0.0).then_inc(s_zm, 1)
            step(dve.tensor_tensor(tied[:, :, :], aff[:, :, :], over_e(top[:, :]), ALU.is_equal))
            dve.wait_ge(s_c, 7)
            step(dve.tensor_tensor(score[:, :, :], tied[:, :, :], early[:, :].unsqueeze(1).broadcast_to([P, T, E0]), ALU.mult))
            step(dve.tensor_reduce(best[:, :], score[:, :, :], AX.X, ALU.max))
            step(dve.tensor_tensor(chosen[:, :, :], score[:, :, :], over_e(best[:, :]), ALU.is_equal))
            dve.tensor_copy(chosen_bf[:, :, :], chosen[:, :, :]).then_inc(s_oh, 1)
            dve.wait_ge(s_e, 1)
            step(dve.tensor_scalar(at[:, :], e_neg[:, :], 1.0, None, ALU.add))
            step(dve.reciprocal(gate[:, :], at[:, :]))
            dve.wait_ge(s_cnt, 2)
            step(dve.tensor_copy(scan[:, 0, :, :], count_ps[:, :].rearrange("p (t e) -> p t e", t=T)))
            for k in range(5):
                r = 1 << k
                step(dve.tensor_copy(scan[:, k + 1, 0:r, :], scan[:, k, 0:r, :]))
                step(dve.tensor_tensor(scan[:, k + 1, r:T, :], scan[:, k, r:T, :], scan[:, k, 0:T - r, :], ALU.add))
            total = scan[:, 5, T - 1, :]
            step(dve.tensor_tensor(over[:, :, :], total.unsqueeze(2).broadcast_to([P, E0, T]),
                                   steps[:, :].unsqueeze(1).broadcast_to([P, E0, T]), ALU.is_gt))
            step(dve.tensor_reduce(tiles[:, :], over[:, :, :], AX.X, ALU.add))
            step(dve.tensor_tensor(prod[:, :, :], lower[:, :, :], tiles[:, :].unsqueeze(1).broadcast_to([P, E0, E0]), ALU.mult))
            step(dve.tensor_reduce(first[:, :], prod[:, :, :], AX.X, ALU.add))
            step(dve.tensor_tensor(last[:, :], first[:, :], tiles[:, :], ALU.add))
            M = MAXTILES
            step(dve.tensor_tensor(past[:, :, :], index[:, :].unsqueeze(2).broadcast_to([P, M, E0]),
                                   last[:, :].unsqueeze(1).broadcast_to([P, M, E0]), ALU.is_ge))
            step(dve.tensor_reduce(owner[:, :], past[:, :, :], AX.X, ALU.add))
            step(dve.tensor_scalar(tile_expert[:, :], owner[:, :], float(E0 - 1), None, ALU.min))
            step(dve.tensor_scalar(start[:, :], first[:, :], float(P), None, ALU.mult))
            step(dve.tensor_tensor(place[:, :, :], scan[:, 5, :, :], scan[:, 0, :, :], ALU.subtract))
            step(dve.tensor_tensor(tied[:, :, :], place[:, :, :], rank_ps[:, :].rearrange("p (t e) -> p t e", t=T), ALU.add))
            step(dve.tensor_tensor(place[:, :, :], tied[:, :, :], start[:, :].unsqueeze(1).broadcast_to([P, T, E0]), ALU.add))
            step(dve.tensor_tensor(score[:, :, :], place[:, :, :], chosen[:, :, :], ALU.mult))
            step(dve.tensor_reduce(best[:, :], score[:, :, :], AX.X, ALU.add))
            dve.tensor_copy(pos[:, :], best[:, :]).then_inc(s_pos, 1)
            dve.wait_ge(s_pos, 1)


def experts(nc, io, keep):
    ident, tile_expert = keep["ident"], keep["tile_expert"]
    with ExitStack() as ctx:
        m = Scope(nc, ctx, "p5_")
        W1 = m.sb("w1_all", [P, E0, F0])
        W2 = m.sb("w2_all", [P, E0, FC, D])
        small = m.sb("ln_b1", [P, E0, 2 + FC])
        b2 = m.sb("b2_rows", [P, E0, D])
        xs = m.sb("xs", [P, RING, D])
        w1 = m.sb("w1_tile", [P, RING, F0])
        xin = m.sb("xin", [P, RING, P])
        hT = m.sb("hT", [P, RING, FC, P])
        y = m.sb("y", [P, RING, D])
        x_ps = [m.ps(f"x_ps{r}", [P, P]) for r in range(2)]
        h_ps = [m.ps(f"h_ps{r}", [P, FC, P]) for r in range(2)]
        y_ps = [m.ps(f"y_ps{r}", [P, D]) for r in range(2)]

        s_w = m.sem("weights_loaded")
        s_ld = [m.sem(f"tile_loaded{r}") for r in range(RING)]
        s_w1 = m.sem("w1_copied")
        s_tr = m.sem("x_transposed")
        s_in = m.sem("x_scaled")
        s_h = m.sem("h_ready")
        s_r = m.sem("h_relu")
        s_y = m.sem("y_ready")
        s_yo = m.sem("y_kept")
        s_out = [m.sem(f"y_stored{r}") for r in range(RING)]
        apart = keep["apart"]
        block = ctx.enter_context(nc.Block())
        ROUNDS = MAXTILES // RING

        def rounds(eng, body):
            with eng.Fori(0, ROUNDS - 1) as k:
                body(k, False)
            body(ROUNDS - 1, True)

        def expert(eng, i):
            return eng.value_load(tile_expert[0:1, bass.ds(i, 1)], min_val=0, max_val=E0 - 1)

        @block.sync
        def _(sp):
            for r in range(RING):
                sp.sem_inc(s_out[r], 16)
                sp.dma_start(xs[:, r, :], io["sorted_in"][r * P:(r + 1) * P, :]).then_inc(s_ld[r], 16)
            for dst, src in ((W1[:, :, :], "w1"), (W2[:, :, :, :], "w2"), (small[:, :, :], "small")):
                sp.dma_start(dst, io[src]).then_inc(s_w, 16)
            sp.dma_start(b2[:, :, :], io["b2"].rearrange("(a e) d -> a e d", a=1).broadcast_to([P, E0, D])).then_inc(s_w, 16)

            def body(k, last):
                for r in range(RING):
                    i = k * RING + r
                    if not last:
                        sp.wait_ge(s_tr, i + 1)
                        sp.dma_start(xs[:, r, :], io["sorted_in"][bass.ds((i + RING) * P, P), :]).then_inc(s_ld[r], 16)
                    sp.wait_ge(s_yo, i + 3)
                    sp.dma_start(io["sorted_out"][bass.ds(i * P, P), :], y[:, r, :]).then_inc(s_out[r], 16)

            rounds(sp, body)
            for r in range(RING):
                sp.wait_ge(s_out[r], 16 * ROUNDS + 16)

        @block.gpsimd
        def _(pool):
            pool.wait_ge(s_w, 64)

            def body(k, last):
                for r in range(RING):
                    i = k * RING + r
                    e = expert(pool, i)
                    pool.wait_ge(s_h, i + 1)
                    pool.sem_inc(apart["pool"], 1)
                    pool.tensor_copy(w1[:, r, :], W1[:, bass.ds(e, 1), :].rearrange("p a f -> p (a f)")).then_inc(s_w1, 1)
                    pool.wait_ge(s_w1, i + 1)

            rounds(pool, body)

        @block.tensor
        def _(pe):
            def transpose(k, r):
                i = k * RING + r
                pe.wait_ge(s_ld[r % RING], 16 * (k + 1 + r // RING))
                pe.wait_ge(s_in, i + 1)
                pe.transpose(x_ps[r % 2][:, :], xs[:, r % RING, :], ident[:, :]).then_inc(s_tr, 1)

            def hidden(k, r):
                i = k * RING + r
                pe.wait_ge(s_in, i + 3)
                pe.wait_ge(s_w1, i + 1)
                pe.wait_ge(s_r, FC * i + FC)
                for c in range(FC):
                    mm = pe.matmul(h_ps[r % 2][:, c, :], w1[:, r % RING, c * P:(c + 1) * P], xin[:, r % RING, :],
                                   start=True, stop=True)
                mm.then_inc(s_h, 1)

            def output(k, r):
                i = k * RING + r
                e = expert(pe, i)
                pe.wait_ge(s_r, FC * i + 3 * FC)
                pe.wait_ge(s_yo, i + 1)
                for c in range(FC):
                    mm = pe.matmul(y_ps[r % 2][:, :], hT[:, r, c, :], W2[:, bass.ds(e, 1), c, :].rearrange("p a d -> p (a d)"),
                                   start=(c == 0), stop=(c == FC - 1))
                mm.then_inc(s_y, 1)

            pe.wait_ge(s_w, 64)
            transpose(0, 0)
            transpose(0, 1)
            hidden(0, 0)

            def body(k, last):
                for r in range(RING):
                    if not (last and r + 2 >= RING):
                        transpose(k, r + 2)
                    if not (last and r + 1 >= RING):
                        hidden(k, r + 1)
                    output(k, r)

            rounds(pe, body)

        @block.scalar
        def _(act):
            act.sem_inc(s_r, 2 * FC)
            act.wait_ge(s_w, 64)

            def body(k, last):
                for r in range(RING):
                    i = k * RING + r
                    e = expert(act, i)
                    act.wait_ge(s_y, i + 1)
                    act.wait_ge(s_h, i + 5)
                    act.sem_inc(apart["act"], 1)
                    for c in range(FC):
                        act.activation(hT[:, r, c, :], h_ps[r % 2][:, c, :], ACT.Relu,
                                       bias=small[:, bass.ds(e, 1), 2 + c]).then_inc(s_r, 1)

            rounds(act, body)

        @block.vector
        def _(dve):
            def scale(k, r):
                i = k * RING + r
                e = expert(dve, i)
                dve.wait_ge(s_tr, i + 1)
                dve.wait_ge(s_h, i + 1)
                dve.tensor_scalar(xin[:, r % RING, :], x_ps[r % 2][:, :], small[:, bass.ds(e, 1), 0],
                                  small[:, bass.ds(e, 1), 1], ALU.mult, ALU.add).then_inc(s_in, 1)

            dve.sem_inc(s_in, 2)
            dve.sem_inc(s_h, RING)
            dve.sem_inc(s_y, RING)
            dve.sem_inc(s_yo, 2)
            dve.wait_ge(s_w, 64)
            scale(0, 0)
            scale(0, 1)

            def body(k, last):
                for r in range(RING):
                    i = k * RING + r
                    if not (last and r + 2 >= RING):
                        scale(k, r + 2)
                    e = expert(dve, i)
                    dve.wait_ge(s_y, i + 1 + RING)
                    dve.wait_ge(s_out[r], 16 * k + 16)
                    dve.tensor_tensor(y[:, r, :], y_ps[r % 2][:, :], b2[:, bass.ds(e, 1), :].rearrange("p a d -> p (a d)"),
                                      ALU.add).then_inc(s_yo, 1)

            rounds(dve, body)


def normalise(dve, s_step, base, apart, rows, stats, mv, var, inv, s_in):
    for t in range(TB):
        dve.bn_stats(stats[:, t, :], rows(t)).then_inc(s_step, 1)
    dve.wait_ge(s_step, base + TB)
    dve.sem_inc(apart, 1)
    for t in range(TB):
        dve.bn_aggr(mv[:, t, :], stats[:, t, :]).then_inc(s_step, 1)
    dve.wait_ge(s_step, base + 2 * TB)
    dve.tensor_scalar(var, mv[:, :, 1], EPS, None, ALU.add).then_inc(s_step, 1)
    dve.wait_ge(s_step, base + 2 * TB + 1)
    dve.reciprocal(inv, var).then_inc(s_in, 1)


def row_tile(A, b, t):
    return A[:, bass.ds(b * TB + t, 1), :].rearrange("p a d -> p (a d)")


def combine_and_project(nc, io, keep):
    X, XN, ident, gate, pos = (keep[k] for k in ("X", "XN", "ident", "gate", "pos"))
    qT, kT, VP = keep["qT"], keep["kT"], keep["VP"]
    with ExitStack() as ctx:
        m = Scope(nc, ctx, "p6_")
        W = m.sb("w", [P, 4, D])
        bias = m.sb("bias", [P, 3])
        back = m.sb("back", [P, T, D])
        z, zn, xn = (m.sb(n, [P, TB, D]) for n in ("z", "zn", "xn"))
        stats, mv = m.sb("stats", [P, 2, TB, 6]), m.sb("mv", [P, 2, TB, 2])
        var, inv, rstd = (m.sb(n, [P, 2, TB]) for n in ("var", "inv", "rstd"))
        xnT, vT = m.sb("xnT", [P, S]), m.sb("vT", [P, S])
        t_ps = m.ps("t_ps", [P, S])
        p_ps = [m.ps(f"p_ps{j}", [P, S]) for j in range(3)]

        s_w, s_g = m.sem("w_loaded"), m.sem("rows_back")
        s_z, s_st, s_in, s_rt = m.sem("z_ready"), m.sem("ln_steps"), m.sem("inverse_variance_ready"), m.sem("rstd_ready")
        s_zn, s_x, s_xn = m.sem("z_normed"), m.sem("x_updated"), m.sem("xn_ready")
        s_tr, s_xnT = m.sem("xn_transposed"), m.sem("xnT_ready")
        s_p, s_pe, s_vp, s_vpe = m.sem("projected"), m.sem("projections_kept"), m.sem("vp_ready"), m.sem("vp_kept")
        apart = keep["apart"]
        block = ctx.enter_context(nc.Block())

        @block.sync
        def _(sp):
            sp.dma_start(W[:, :, :], io["l1_w"]).then_inc(s_w, 16)
            sp.dma_start(bias[:, :], io["b_qkv"]).then_inc(s_w, 16)

        @block.gpsimd
        def _(pool):
            for t in range(T):
                pool.indirect_dma_start(back[:, t, :], None, io["sorted_out"],
                                        bass.IndirectOffsetOnAxis(ap=pos[:, t:t + 1], axis=0)).then_inc(s_g, 16)

        @block.vector
        def _(dve):
            dve.wait_ge(s_g, 16 * T)
            with dve.Fori(0, B) as b:
                for t in range(TB):
                    dve.scalar_tensor_tensor(out=z[:, t, :], in0=row_tile(back, b, t),
                                             scalar=gate[:, bass.ds(b * TB + t, 1)], in1=row_tile(XN, b, t),
                                             op0=ALU.mult, op1=ALU.add).then_inc(s_z, 1)
                dve.wait_ge(s_z, TB * b + TB)
                dve.sem_inc(apart["dve"], 1)
                k = b * (4 * TB + 2)
                normalise(dve, s_st, k, apart["dve"], lambda t: z[:, t, :], stats[:, 0], mv[:, 0], var[:, 0, :], inv[:, 0, :], s_in)
                dve.wait_ge(s_rt, 2 * b + 1)
                for t in range(TB):
                    dve.tensor_scalar(zn[:, t, :], z[:, t, :], mv[:, 0, t, 0:1], rstd[:, 0, t:t + 1],
                                      ALU.subtract, ALU.mult).then_inc(s_zn, 1)
                dve.wait_ge(s_zn, TB * b + TB)
                rows = X[:, bass.ds(b * TB, TB), :]
                dve.tensor_tensor(rows, rows, zn[:, :, :], ALU.add).then_inc(s_x, 1)
                dve.wait_ge(s_x, b + 1)
                dve.sem_inc(apart["dve"], 1)
                normalise(dve, s_st, k + 2 * TB + 1, apart["dve"], lambda t: row_tile(X, b, t), stats[:, 1], mv[:, 1],
                          var[:, 1, :], inv[:, 1, :], s_in)
                dve.wait_ge(s_rt, 2 * b + 2)
                for t in range(TB):
                    dve.tensor_scalar(xn[:, t, :], row_tile(X, b, t), mv[:, 1, t, 0:1], rstd[:, 1, t:t + 1],
                                      ALU.subtract, ALU.mult).then_inc(s_xn, 1)
                dve.wait_ge(s_tr, b + 1)

        @block.scalar
        def _(act):
            act.wait_ge(s_w, 32)
            with act.Fori(0, B) as b:
                for k in range(2):
                    act.wait_ge(s_in, 2 * b + k + 1)
                    act.activation(rstd[:, k, :], inv[:, k, :], ACT.Sqrt).then_inc(s_rt, 1)
                act.wait_ge(s_tr, b + 1)
                act.activation(xnT[:, :], t_ps[:, :], ACT.Copy).then_inc(s_xnT, 1)
                for j, dst in ((2, vT[:, :]), (0, qT[:, bass.ds(b * S, S)]), (1, kT[:, bass.ds(b * S, S)])):
                    act.wait_ge(s_p, 3 * b + {2: 1, 0: 2, 1: 3}[j])
                    act.sem_inc(apart["act"], 1)
                    act.activation(dst, p_ps[j][:, :], ACT.Identity, bias=bias[:, j:j + 1]).then_inc(s_pe, 1)
                act.wait_ge(s_vp, b + 1)
                act.sem_inc(apart["act"], 1)
                act.activation(VP[:, bass.ds(b * TB, TB), :], t_ps[:, :].rearrange("p (t d) -> p t d", t=TB),
                               ACT.Copy).then_inc(s_vpe, 1)

        @block.tensor
        def _(pe):
            pe.wait_ge(s_w, 32)
            with pe.Fori(0, B) as b:
                pe.wait_ge(s_xn, TB * b + TB)
                for t in range(TB):
                    mm = pe.transpose(t_ps[:, t * P:(t + 1) * P], xn[:, t, :], ident[:, :])
                mm.then_inc(s_tr, 1)
                pe.wait_ge(s_xnT, b + 1)
                for j in (2, 0, 1):
                    for c in range(2):
                        mm = pe.matmul(p_ps[j][:, c * 512:(c + 1) * 512], W[:, j, :], xnT[:, c * 512:(c + 1) * 512],
                                       start=True, stop=True)
                    mm.then_inc(s_p, 1)
                pe.wait_ge(s_pe, 3 * b + 1)
                for t in range(TB):
                    mm = pe.matmul(t_ps[:, t * P:(t + 1) * P], vT[:, t * P:(t + 1) * P], W[:, 3, :], start=True, stop=True)
                mm.then_inc(s_vp, 1)
                pe.wait_ge(s_vpe, b + 1)
                pe.wait_ge(s_pe, 3 * b + 3)


BAND = {p: float(np.log(p / (1 - p))) for p in (0.95, 0.85, 0.25, 0.1)}
QK_LEAD, F_LEAD, EXP_LEAD, PV_LEAD = 4, 3, 2, 1
assert TB % 4 == 0


def banded_attention(nc, io, keep):
    ident, qT, kT, VP, Y = (keep[k] for k in ("ident", "qT", "kT", "VP", "Y"))
    with ExitStack() as ctx:
        m = Scope(nc, ctx, "p7_")
        bp = m.sb("b_proj", [P, D])
        q = m.sb("q", [P, 4, P])
        x = m.sb("x", [P, 4, S])
        low_d, low_c, low = (m.sb(n, [P, S]) for n in ("low_d", "low_c", "low_sum"))
        lows = m.sb("lows", [P, 2, S])
        up_a = m.sb("up_a", [P, S], BF16)
        up = m.sb("up", [P, S], BF16)
        factor = m.sb("factor", [P, S])
        f = m.sb("f", [P, 2, S])
        top, neg = m.sb("top", [P, 2]), m.sb("neg", [P, 2])
        probs = m.sb("probs", [P, 2, S])
        total = m.sb("total", [P, 4])
        inv = m.sb("inv", [P, 2])
        pT = m.sb("pT", [P, 2, TB, P])
        s_ps = [m.ps(f"s_ps{r}", [P, S]) for r in range(2)]
        t_ps = [m.ps(f"t_ps{r}", [P, 4, P]) for r in range(2)]
        y_ps = [m.ps(f"y_ps{r}", [P, D]) for r in range(2)]

        s_b = m.sem("b_loaded")
        s_q = [m.sem(f"q_loaded{r}") for r in range(4)]
        s_s = m.sem("scores_ready")
        s_x = m.sem("scores_scaled")
        s_low = m.sem("low_steps")
        s_f = m.sem("band_steps")
        s_e = m.sem("exps_ready")
        s_t = m.sem("p_transposed")
        s_pt = m.sem("pT_ready")
        s_y = m.sem("pv_ready")
        s_i = m.sem("sums_inverted")
        s_o = m.sem("rows_out")
        apart = keep["apart"]
        block = ctx.enter_context(nc.Block())

        def batches(eng, body):
            with eng.Fori(0, B - 1) as b:
                body(b, False)
            body(B - 1, True)

        def ahead(last, i):
            return not (last and i >= TB)

        @block.sync
        def _(sp):
            sp.dma_start(bp[:, :], io["b_proj"].rearrange("(a d) -> a d", a=1).broadcast_to([P, D])).then_inc(s_b, 16)

            def load(b, i):
                n = b * TB + i
                sp.wait_ge(s_s, n + 1)
                sp.dma_start(q[:, i % 4, :], qT[:, bass.ds(n * P, P)]).then_inc(s_q[i % 4], 16)

            for i in range(4):
                sp.dma_start(q[:, i, :], qT[:, i * P:(i + 1) * P]).then_inc(s_q[i], 16)

            def body(b, last):
                for i in range(TB):
                    if ahead(last, i + 4):
                        load(b, i + 4)

            batches(sp, body)

        @block.tensor
        def _(pe):
            def scores(b, i):
                n = b * TB + i
                pe.wait_ge(s_q[i % 4], 16 * (b * (TB // 4) + i // 4 + 1))
                pe.wait_ge(s_x, n + 1)
                for c in range(2):
                    mm = pe.matmul(s_ps[i % 2][:, c * 512:(c + 1) * 512], q[:, i % 4, :],
                                   kT[:, bass.ds((b + i // TB) * S + c * 512, 512)], start=True, stop=True)
                mm.then_inc(s_s, 1)

            def transpose(b, i):
                n = b * TB + i
                pe.wait_ge(s_e, n + 3)
                for c in range(2):
                    pe.wait_ge(s_pt, 2 * n + c + 1)
                    for k in range(4):
                        mm = pe.transpose(t_ps[c][:, k, :], probs[:, i % 2, (4 * c + k) * P:(4 * c + k + 1) * P], ident[:, :])
                    mm.then_inc(s_t, 1)

            def pv(b, i):
                n = b * TB + i
                pe.wait_ge(s_pt, 2 * n + 4)
                pe.wait_ge(s_o, n + 3)
                for k in range(TB):
                    mm = pe.matmul(y_ps[i % 2][:, :], pT[:, i % 2, k, :],
                                   VP[:, bass.ds((b + i // TB) * TB + k, 1), :].rearrange("p a d -> p (a d)"),
                                   start=(k == 0), stop=(k == TB - 1))
                mm.then_inc(s_y, 1)

            for i in range(QK_LEAD):
                scores(0, i)
            transpose(0, 0)
            pv(0, 0)

            def body(b, last):
                for i in range(TB):
                    if ahead(last, i + PV_LEAD):
                        transpose(b, i + PV_LEAD)
                    if ahead(last, i + QK_LEAD):
                        scores(b, i + QK_LEAD)
                    if ahead(last, i + PV_LEAD):
                        pv(b, i + PV_LEAD)

            batches(pe, body)

        @block.scalar
        def _(act):
            def scale(b, i):
                n = b * TB + i
                act.wait_ge(s_s, n + 5)
                act.wait_ge(s_f, 5 * n + 5)
                act.activation(x[:, i % 4, :], s_ps[i % 2][:, :], ACT.Copy, scale=SCALE).then_inc(s_x, 1)

            def exps(b, i):
                n = b * TB + i
                act.wait_ge(s_f, 5 * (n + 5))
                act.wait_ge(s_t, 2 * n + 2)
                act.wait_ge(s_o, n + 1)
                act.activation(probs[:, i % 2, :], f[:, i % 2, :], ACT.Exp, bias=neg[:, i % 2:i % 2 + 1],
                               accum_out=total[:, i % 4:i % 4 + 1]).then_inc(s_e, 1)

            def keep_t(b, i):
                n = b * TB + i
                act.wait_ge(s_t, 2 * n + 6)
                act.wait_ge(s_y, n + 1)
                act.wait_ge(s_pt, 2 * n + 3)
                act.activation(pT[:, i % 2, 4:8, :], t_ps[1][:, :, :], ACT.Copy).then_inc(s_pt, 1)

            act.sem_inc(s_x, 2)
            act.sem_inc(s_e, 2)
            for i in range(QK_LEAD):
                scale(0, i)
            for i in range(EXP_LEAD):
                exps(0, i)
            keep_t(0, 0)

            def body(b, last):
                for i in range(TB):
                    if ahead(last, i + QK_LEAD):
                        scale(b, i + QK_LEAD)
                    if ahead(last, i + EXP_LEAD):
                        exps(b, i + EXP_LEAD)
                    if ahead(last, i + PV_LEAD):
                        keep_t(b, i + PV_LEAD)

            batches(act, body)

        @block.gpsimd
        def _(pool):
            def lows_of(b, i):
                n = b * TB + i
                pool.wait_ge(s_x, n + 3)
                pool.sem_inc(apart["pool"], 1)
                pool.tensor_scalar(low_d[:, :], x[:, i % 4, :], BAND[0.1], -0.2, ALU.is_lt, ALU.mult).then_inc(s_low, 1)
                pool.wait_ge(s_low, 3 * n + 1)
                pool.sem_inc(apart["pool"], 1)
                pool.tensor_scalar(low_c[:, :], x[:, i % 4, :], BAND[0.25], -0.7, ALU.is_lt, ALU.mult).then_inc(s_low, 1)
                pool.wait_ge(s_low, 3 * n + 2)
                pool.wait_ge(s_f, 5 * (n + 3))
                pool.tensor_tensor(lows[:, i % 2, :], low_d[:, :], low_c[:, :], ALU.add).then_inc(s_low, 1)
                pool.wait_ge(s_low, 3 * n + 3)

            for i in range(QK_LEAD):
                lows_of(0, i)

            def body(b, last):
                for i in range(TB):
                    if ahead(last, i + QK_LEAD):
                        lows_of(b, i + QK_LEAD)

            batches(pool, body)

        @block.vector
        def _(dve):
            def band(b, i):
                n = b * TB + i
                dve.wait_ge(s_x, n + 3)
                k = 5 * n + 20
                dve.tensor_scalar(up_a[:, :], x[:, i % 4, :], BAND[0.85], 2.0, ALU.is_gt, ALU.add).then_inc(s_f, 1)
                dve.wait_ge(s_f, k + 1)
                dve.scalar_tensor_tensor(out=up[:, :], in0=x[:, i % 4, :], scalar=BAND[0.95], in1=up_a[:, :],
                                         op0=ALU.is_gt, op1=ALU.add).then_inc(s_f, 1)
                dve.wait_ge(s_f, k + 2)
                dve.wait_ge(s_low, 3 * n + 3)
                dve.scalar_tensor_tensor(out=factor[:, :], in0=up[:, :], scalar=0.5, in1=lows[:, i % 2, :],
                                         op0=ALU.mult, op1=ALU.add).then_inc(s_f, 1)
                dve.wait_ge(s_f, k + 3)
                dve.wait_ge(s_e, n + 1)
                dve.sem_inc(apart["dve"], 1)
                dve.tensor_tensor_reduce(out=f[:, i % 2, :], in0=factor[:, :], in1=x[:, i % 4, :], scale=1.0, scalar=LOW,
                                         op0=ALU.mult, op1=ALU.max, accum_out=top[:, i % 2:i % 2 + 1]).then_inc(s_f, 1)
                dve.wait_ge(s_f, k + 4)
                dve.tensor_scalar(neg[:, i % 2:i % 2 + 1], top[:, i % 2:i % 2 + 1], -1.0, None, ALU.mult).then_inc(s_f, 1)

            def keep_t(b, i):
                n = b * TB + i
                dve.wait_ge(s_t, 2 * n + 5)
                dve.wait_ge(s_y, n + 1)
                dve.wait_ge(s_pt, 2 * n + 2)
                dve.tensor_copy(pT[:, i % 2, 0:4, :], t_ps[0][:, :, :]).then_inc(s_pt, 1)

            def finish(b, i):
                n = b * TB + i
                dve.wait_ge(s_y, n + 3)
                dve.wait_ge(s_o, n + 3)
                dve.reciprocal(inv[:, i % 2:i % 2 + 1], total[:, i % 4:i % 4 + 1]).then_inc(s_i, 1)
                dve.wait_ge(s_i, n + 1)
                dve.scalar_tensor_tensor(out=row_tile(Y, b, i), in0=y_ps[i % 2][:, :], scalar=inv[:, i % 2:i % 2 + 1],
                                         in1=bp[:, :], op0=ALU.mult, op1=ALU.add).then_inc(s_o, 1)

            dve.sem_inc(s_s, 4)
            dve.sem_inc(s_f, 20)
            dve.sem_inc(s_t, 4)
            dve.sem_inc(s_pt, 2)
            dve.sem_inc(s_y, 2)
            dve.sem_inc(s_o, 4)
            dve.wait_ge(s_b, 16)
            for i in range(F_LEAD):
                band(0, i)
            keep_t(0, 0)

            def body(b, last):
                for i in range(TB):
                    if ahead(last, i + F_LEAD):
                        band(b, i + F_LEAD)
                    if ahead(last, i + PV_LEAD):
                        keep_t(b, i + PV_LEAD)
                    finish(b, i)

            batches(dve, body)


def ffn_inputs(nc, io, keep):
    X, Y, ident, XA = (keep[k] for k in ("X", "Y", "ident", "XA"))
    with ExitStack() as ctx:
        m = Scope(nc, ctx, "p8_")
        W = m.sb("attn_w", [P, D])
        vec = m.sb("vectors", [P, 3])
        zn, flat, xh = (m.sb(n, [P, TB, D]) for n in ("zn", "flat", "xh"))
        stats, mv = m.sb("stats", [P, 2, TB, 6]), m.sb("mv", [P, 2, TB, 2])
        var, inv, rstd = (m.sb(n, [P, 4, TB]) for n in ("var", "inv", "rstd"))
        hT, fT = m.sb("hT", [P, S]), m.sb("fT", [P, S])
        h_ps, f_ps, a_ps = (m.ps(n, [P, S]) for n in ("h_ps", "f_ps", "a_ps"))

        s_w = m.sem("w_loaded")
        s_st, s_in, s_rt, s_v2 = m.sem("ln_steps"), m.sem("inverse_variance_ready"), m.sem("rstd_ready"), m.sem("var2_steps")
        s_zn, s_x, s_f, s_h = m.sem("y_normed"), m.sem("x_updated"), m.sem("flat_ready"), m.sem("xh_ready")
        s_tr, s_T, s_a, s_xa = m.sem("transposed"), m.sem("transposes_kept"), m.sem("attn_ready"), m.sem("xa_ready")
        apart = keep["apart"]
        block = ctx.enter_context(nc.Block())

        @block.sync
        def _(sp):
            sp.dma_start(W[:, :], io["attn_w"]).then_inc(s_w, 16)
            sp.dma_start(vec[:, :], io["ffn_vectors"]).then_inc(s_w, 16)

        @block.vector
        def _(dve):
            with dve.Fori(0, B) as b:
                k = b * (4 * TB + 2)
                normalise(dve, s_st, k, apart["dve"], lambda t: row_tile(Y, b, t), stats[:, 0], mv[:, 0], var[:, 0, :], inv[:, 0, :], s_in)
                dve.wait_ge(s_rt, 3 * b + 1)
                for t in range(TB):
                    dve.tensor_scalar(zn[:, t, :], row_tile(Y, b, t), mv[:, 0, t, 0:1], rstd[:, 0, t:t + 1],
                                      ALU.subtract, ALU.mult).then_inc(s_zn, 1)
                dve.wait_ge(s_zn, TB * b + TB)
                rows = X[:, bass.ds(b * TB, TB), :]
                dve.tensor_tensor(rows, rows, zn[:, :, :], ALU.add).then_inc(s_x, 1)
                dve.wait_ge(s_x, b + 1)
                dve.sem_inc(apart["dve"], 1)
                normalise(dve, s_st, k + 2 * TB + 1, apart["dve"], lambda t: row_tile(X, b, t), stats[:, 1], mv[:, 1],
                          var[:, 1, :], inv[:, 1, :], s_in)
                dve.wait_ge(s_in, 3 * b + 2)
                dve.tensor_tensor(var[:, 2, :], mv[:, 1, :, 1], inv[:, 1, :], ALU.mult).then_inc(s_v2, 1)
                dve.wait_ge(s_v2, 2 * b + 1)
                dve.tensor_scalar(var[:, 3, :], var[:, 2, :], EPS, None, ALU.add).then_inc(s_v2, 1)
                dve.wait_ge(s_v2, 2 * b + 2)
                dve.reciprocal(inv[:, 2, :], var[:, 3, :]).then_inc(s_in, 1)
                dve.wait_ge(s_rt, 3 * b + 3)
                for t in range(TB):
                    dve.tensor_scalar(flat[:, t, :], row_tile(X, b, t), mv[:, 1, t, 0:1], rstd[:, 1, t:t + 1],
                                      ALU.subtract, ALU.mult).then_inc(s_f, 1)
                dve.wait_ge(s_f, TB * b + TB)
                for t in range(TB):
                    dve.tensor_scalar(xh[:, t, :], flat[:, t, :], rstd[:, 2, t:t + 1], None, ALU.mult).then_inc(s_h, 1)
                dve.wait_ge(s_a, b + 1)
                dve.wait_ge(s_T, 2 * b + 2)
                dve.tensor_tensor(XA[:, bass.ds(b * S, S)], a_ps[:, :], fT[:, :], ALU.add).then_inc(s_xa, 1)
                dve.wait_ge(s_xa, b + 1)

        @block.scalar
        def _(act):
            act.wait_ge(s_w, 32)
            with act.Fori(0, B) as b:
                for k in range(3):
                    act.wait_ge(s_in, 3 * b + k + 1)
                    act.activation(rstd[:, k, :], inv[:, k, :], ACT.Sqrt).then_inc(s_rt, 1)
                act.wait_ge(s_tr, 2 * b + 1)
                act.activation(fT[:, :], f_ps[:, :], ACT.Identity, bias=vec[:, 2:3]).then_inc(s_T, 1)
                act.wait_ge(s_tr, 2 * b + 2)
                act.activation(hT[:, :], h_ps[:, :], ACT.Identity, scale=vec[:, 0:1], bias=vec[:, 1:2]).then_inc(s_T, 1)
                act.wait_ge(s_xa, b + 1)

        @block.tensor
        def _(pe):
            pe.wait_ge(s_w, 32)
            with pe.Fori(0, B) as b:
                for ready, src, dst in ((s_f, flat, f_ps), (s_h, xh, h_ps)):
                    pe.wait_ge(ready, TB * b + TB)
                    for t in range(TB):
                        mm = pe.transpose(dst[:, t * P:(t + 1) * P], src[:, t, :], ident[:, :])
                    mm.then_inc(s_tr, 1)
                pe.wait_ge(s_T, 2 * b + 2)
                for c in range(2):
                    mm = pe.matmul(a_ps[:, c * 512:(c + 1) * 512], W[:, :], hT[:, c * 512:(c + 1) * 512], start=True, stop=True)
                mm.then_inc(s_a, 1)
                pe.wait_ge(s_xa, b + 1)


E1 = 8
CH = B * S // (2 * E1)
CT = CH // P


def static_experts(nc, io, keep):
    XA, Z = keep["XA"], keep["Z"]
    with ExitStack() as ctx:
        m = Scope(nc, ctx, "p9_")
        W1 = m.sb("w1", [P, E1, F0])
        W2 = m.sb("w2", [P, E1, FC, D])
        Wn = m.sb("next_w", [P, D])
        b12 = m.sb("b1_b2", [P, E1, FC + 1])
        bn = m.sb("next_b", [P, D])
        hT = m.sb("hT", [P, 2, FC, CH])
        eoT = m.sb("eoT", [P, 2, CH])
        pre = m.sb("pre", [P, 2, CT, D])
        h_ps = [m.ps(f"h_ps{r}", [P, FC, CH]) for r in range(2)]
        e_ps = [m.ps(f"e_ps{r}", [P, CH]) for r in range(2)]
        n_ps = [m.ps(f"n_ps{r}", [P, CT, D]) for r in range(2)]

        s_w = m.sem("w_loaded")
        s_h = m.sem("h_ready")
        s_g = m.sem("h_gelu")
        s_eo = m.sem("eo_ready")
        s_ek = m.sem("eo_kept")
        s_n = m.sem("next_ready")
        s_nb = m.sem("next_biased")
        s_z = m.sem("z_ready")
        apart = keep["apart"]
        block = ctx.enter_context(nc.Block())

        def micro_batches(eng, body):
            with eng.Fori(0, 1) as k:
                body(k, False)
            body(1, True)

        @block.sync
        def _(sp):
            for dst, src in ((W1[:, :, :], "f_w1"), (W2[:, :, :, :], "f_w2"), (Wn[:, :], "next_w"), (b12[:, :, :], "f_b12")):
                sp.dma_start(dst, io[src]).then_inc(s_w, 16)
            sp.dma_start(bn[:, :], io["next_b"].rearrange("(a d) -> a d", a=1).broadcast_to([P, D])).then_inc(s_w, 16)

        @block.tensor
        def _(pe):
            def first(k, i):
                n, e = k * E1 + i, i % E1
                pe.wait_ge(s_g, FC * n + FC)
                for c in range(FC):
                    mm = pe.matmul(h_ps[i % 2][:, c, :], W1[:, e, c * P:(c + 1) * P], XA[:, bass.ds(n * CH, CH)],
                                   start=True, stop=True)
                mm.then_inc(s_h, 1)

            def second(k, i):
                n, e = k * E1 + i, i % E1
                pe.wait_ge(s_g, FC * n + 3 * FC)
                pe.wait_ge(s_ek, n + 1)
                for c in range(FC):
                    mm = pe.matmul(e_ps[i % 2][:, :], W2[:, e, c, :], hT[:, i % 2, c, :], start=(c == 0), stop=(c == FC - 1))
                mm.then_inc(s_eo, 1)

            def third(k, i):
                n = k * E1 + i
                pe.wait_ge(s_ek, n + 3)
                pe.wait_ge(s_nb, n + 1)
                for t in range(CT):
                    mm = pe.matmul(n_ps[i % 2][:, t, :], eoT[:, i % 2, t * P:(t + 1) * P], Wn[:, :], start=True, stop=True)
                mm.then_inc(s_n, 1)

            pe.wait_ge(s_w, 80)
            first(0, 0)
            first(0, 1)
            second(0, 0)

            def body(k, last):
                for i in range(E1):
                    if not (last and i + 2 >= E1):
                        first(k, i + 2)
                    if not (last and i + 1 >= E1):
                        second(k, i + 1)
                    third(k, i)

            micro_batches(pe, body)

        @block.scalar
        def _(act):
            def gelu(k, i):
                n, e = k * E1 + i, i % E1
                act.wait_ge(s_eo, n + 1)
                act.wait_ge(s_h, n + 1)
                for c in range(FC):
                    act.activation(hT[:, i % 2, c, :], h_ps[i % 2][:, c, :], ACT.Gelu, bias=b12[:, e, c:c + 1]).then_inc(s_g, 1)

            act.sem_inc(s_g, 2 * FC)
            act.sem_inc(s_z, 2)
            act.wait_ge(s_w, 80)
            gelu(0, 0)
            gelu(0, 1)

            def body(k, last):
                for i in range(E1):
                    if not (last and i + 2 >= E1):
                        gelu(k, i + 2)
                    n = k * E1 + i
                    act.wait_ge(s_nb, n + 3)
                    act.sem_inc(apart["act"], 1)
                    act.activation(Z[:, bass.ds(n * CT, CT), :], pre[:, i % 2, :, :], ACT.Gelu).then_inc(s_z, 1)

            micro_batches(act, body)

        @block.vector
        def _(dve):
            def expert_bias(k, i):
                n, e = k * E1 + i, i % E1
                dve.wait_ge(s_n, n + 1)
                dve.wait_ge(s_eo, n + 3)
                dve.tensor_scalar(eoT[:, i % 2, :], e_ps[i % 2][:, :], b12[:, e, FC:FC + 1], None, ALU.add).then_inc(s_ek, 1)

            dve.sem_inc(s_eo, 2)
            dve.sem_inc(s_ek, 2)
            dve.sem_inc(s_n, 2)
            dve.sem_inc(s_nb, 2)
            dve.wait_ge(s_w, 80)
            expert_bias(0, 0)

            def body(k, last):
                for i in range(E1):
                    if not (last and i + 1 >= E1):
                        expert_bias(k, i + 1)
                    n = k * E1 + i
                    dve.wait_ge(s_z, n + 1)
                    dve.wait_ge(s_n, n + 3)
                    dve.tensor_tensor(pre[:, i % 2, :, :], n_ps[i % 2][:, :, :],
                                      bn[:, :].unsqueeze(1).broadcast_to([P, CT, D]), ALU.add).then_inc(s_nb, 1)

            micro_batches(dve, body)


def finish_rows(nc, io, keep):
    X, Z = keep["X"], keep["Z"]
    with ExitStack() as ctx:
        m = Scope(nc, ctx, "p10_")
        zn = m.sb("zn", [P, TB, D])
        stats, mv = m.sb("stats", [P, TB, 6]), m.sb("mv", [P, TB, 2])
        var, inv, rstd = (m.sb(n, [P, TB]) for n in ("var", "inv", "rstd"))
        s_st, s_in, s_rt = m.sem("ln_steps"), m.sem("inverse_variance_ready"), m.sem("rstd_ready")
        s_zn, s_x, s_out = m.sem("z_normed"), m.sem("x_updated"), m.sem("x_stored")
        apart = keep["apart"]["dve"]
        block = ctx.enter_context(nc.Block())

        @block.vector
        def _(dve):
            with dve.Fori(0, B) as b:
                normalise(dve, s_st, b * (2 * TB + 1), apart, lambda t: row_tile(Z, b, t), stats, mv, var[:, :], inv[:, :], s_in)
                dve.wait_ge(s_rt, b + 1)
                for t in range(TB):
                    dve.tensor_scalar(zn[:, t, :], row_tile(Z, b, t), mv[:, t, 0:1], rstd[:, t:t + 1],
                                      ALU.subtract, ALU.mult).then_inc(s_zn, 1)
                dve.wait_ge(s_zn, TB * b + TB)
                rows = X[:, bass.ds(b * TB, TB), :]
                dve.tensor_tensor(rows, rows, zn[:, :, :], ALU.add).then_inc(s_x, 1)
                dve.wait_ge(s_x, b + 1)

        @block.scalar
        def _(act):
            with act.Fori(0, B) as b:
                act.wait_ge(s_in, b + 1)
                act.activation(rstd[:, :], inv[:, :], ACT.Sqrt).then_inc(s_rt, 1)

        @block.sync
        def _(sp):
            with sp.Fori(0, B) as b:
                sp.wait_ge(s_x, b + 1)
                sp.dma_start(io["out"][bass.ds(b, 1), :, :].rearrange("b (t p) d -> p (b t) d", p=P),
                             X[:, bass.ds(b * TB, TB), :]).then_inc(s_out, 16)
            sp.wait_ge(s_out, 16 * B)


def build(nc, io):
    with ExitStack() as ctx:
        m = Scope(nc, ctx)
        apart = {e: m.sem(f"{e}_apart") for e in ("act", "dve", "pool")}
        keep = {"apart": apart, "X": m.sb("X", [P, T, D]), "ident": m.sb("ident", [P, P])}
        with ExitStack() as attn:
            a = Scope(nc, attn)
            keep["tri"] = a.sb("tri", [P, 4 * P])
            keep["Q4"] = a.sb("q_operands", [P, G, GH, S], BF16)
            keep["K4"] = a.sb("k_operands", [P, G, GH, S], BF16)
            keep["Vg"] = a.sb("v_groups", [P, B * G, TB, GH * HD])
            keep["Vone"] = a.sb("v_with_ones", [P, 2, TB, GH, 32])
            project_heads(nc, io, keep)
            causal_attention(nc, io, keep)
        for name in ("qT", "kT"):
            keep[name] = m.sb(name, [P, B * S])
        keep["VP"] = m.sb("VP", [P, T, D])
        with ExitStack() as moe:
            a = Scope(nc, moe)
            for name, shape, dt in (("XN", [P, T, D], F32), ("XH", [P, T, D], F32), ("aff", [P, T, E0], F32),
                                    ("gate", [P, T], F32), ("pos", [P, T], U32), ("tile_expert", [P, MAXTILES], I32)):
                keep[name] = a.sb(name, shape, dt)
            merge_heads(nc, io, keep)
            route(nc, io, keep)
            experts(nc, io, keep)
            combine_and_project(nc, io, keep)
        keep["Y"] = m.sb("Y", [P, T, D])
        banded_attention(nc, io, keep)
        keep["XA"] = m.sb("XA", [P, B * S])
        ffn_inputs(nc, io, keep)
        keep["Z"] = keep["Y"]
        static_experts(nc, io, keep)
        finish_rows(nc, io, keep)


def kernel(**inputs):
    import concourse.bacc as bacc
    from concourse.bass_utils import run_bass_kernel_spmd

    swap = np.arange(D) ^ 1
    turned = [np.asarray(inputs[f"L0_attn_W{k}"]).T for k in "qkvo"]
    Wq, Wk, Wv, Wo = turned
    arrays = {
        "x": np.asarray(inputs["L0_attn_x"]),
        "l0_w": np.stack([Wq, Wq[:, swap], Wk, Wk[:, swap], Wv, Wo], axis=1),
    }
    A = {k: np.asarray(v) for k, v in inputs.items()}
    per_row = lambda w: w.reshape(E0, -1, P).transpose(2, 0, 1)
    arrays["centroids"] = A["L0_ffn_centroids"].T
    arrays["w1"] = A["L0_ffn_w1"].transpose(2, 0, 1)
    arrays["w2"] = A["L0_ffn_w2"].transpose(2, 0, 1).reshape(FC, P, E0, D).transpose(1, 2, 0, 3)
    arrays["small"] = np.concatenate([per_row(A["L0_ffn_ln_g"]), per_row(A["L0_ffn_ln_b"]), per_row(A["L0_ffn_b1"])], -1)
    arrays["b2"] = A["L0_ffn_b2"]
    qkv = A["L1_attn_W_qkv"]
    arrays["l1_w"] = np.stack([qkv[:, 0:D], qkv[:, D:2 * D], qkv[:, 2 * D:], A["L1_attn_W_proj"]], 1)
    arrays["b_qkv"] = A["L1_attn_b_qkv"].reshape(3, D).T
    arrays["b_proj"] = A["L1_attn_b_proj"]
    arrays["attn_w"] = A["L1_ffn_attn_w"].T
    arrays["ffn_vectors"] = np.stack([A["L1_ffn_ln_scale"], A["L1_ffn_ln_bias"], A["L1_ffn_attn_b"]], 1)
    arrays["f_w1"] = A["L1_ffn_w1"].transpose(1, 0, 2)
    arrays["f_w2"] = A["L1_ffn_w2"].reshape(E1, FC, P, D).transpose(2, 0, 1, 3)
    arrays["f_b12"] = np.concatenate([per_row(A["L1_ffn_b1"]), per_row(A["L1_ffn_b2"])], -1)
    arrays["next_w"] = A["L1_ffn_next_w"].T
    arrays["next_b"] = A["L1_ffn_next_b"]
    freq = (1.0 / 10000.0 ** (np.arange(0, HD, 2, dtype=np.float32) / HD)).astype(np.float32)
    angle = np.outer(np.arange(S, dtype=np.float32), freq)
    angle = np.concatenate([angle, angle], -1).T
    sign = np.where(np.arange(HD) % 2 == 0, -1.0, 1.0).astype(np.float32)[:, None]
    arrays["rope"] = np.stack([np.tile(np.cos(angle), (H, 1)), np.tile(np.sin(angle) * sign, (H, 1))], 1).astype(np.float32)

    nc = bacc.Bacc("TRN2", target_bir_lowering=False, num_devices=1)
    io, feed = {}, {}
    for name, a in arrays.items():
        feed["in_" + name] = np.ascontiguousarray(a)
        io[name] = nc.dram_tensor("in_" + name, a.shape, mybir.dt.from_np(a.dtype), kind="ExternalInput").ap()
    io["q_parts"] = nc.dram_tensor("q_parts", (3, B, D, S), BF16, kind="Internal").ap()
    io["k_parts"] = nc.dram_tensor("k_parts", (3, B, D, S), BF16, kind="Internal").ap()
    io["heads_out"] = nc.dram_tensor("heads_out", (B * G, P, S), F32, kind="Internal").ap()
    io["sorted_in"] = nc.dram_tensor("sorted_in", (MAXTILES * P, D), F32, kind="Internal").ap()
    io["sorted_out"] = nc.dram_tensor("sorted_out", (MAXTILES * P, D), F32, kind="Internal").ap()
    io["out"] = nc.dram_tensor("out_0", (B, S, D), F32, kind="ExternalOutput").ap()
    build(nc, io)
    return run_bass_kernel_spmd(nc, [feed], core_ids=[0]).results[0]["out_0"]
```

```python
from contextlib import ExitStack

import concourse.bass as bass
import numpy as np
from concourse import mybir

P = 128
D = 128
B, S = 4, 1024
TB = S // P
T = B * TB
H, HD = 16, 8
GH = 4
G = H // GH
E0, F0 = 8, 512
FC = F0 // P
EPS = 1e-5
SCALE = HD ** -0.5
LOW = -3.0e38

F32 = mybir.dt.float32
BF16 = mybir.dt.bfloat16
I32 = mybir.dt.int32
U32 = mybir.dt.uint32
ALU = mybir.AluOpType
ACT = mybir.ActivationFunctionType
AX = mybir.AxisListType


class Scope:

    def __init__(self, nc, ctx, phase=""):
        self.nc, self.ctx, self.phase = nc, ctx, phase

    def sb(self, name, shape, dt=F32):
        return self.ctx.enter_context(self.nc.sbuf_tensor(self.phase + name, shape, dt))

    def ps(self, name, shape, dt=F32):
        return self.ctx.enter_context(self.nc.psum_tensor(self.phase + name, shape, dt))

    def sem(self, name):
        return self.ctx.enter_context(self.nc.semaphore(self.phase + name))


class Moments:

    def __init__(self, m, name):
        self.stats, self.mv = m.sb(name + "_stats", [P, TB, 6]), m.sb(name + "_mv", [P, TB, 2])
        self.var, self.inv, self.rstd = (m.sb(f"{name}_{k}", [P, TB]) for k in ("var", "inv", "rstd"))


class MomentSems:

    def __init__(self, m):
        self.stats, self.mv, self.var, self.inv = (
            m.sem(n) for n in ("tile_stats_done", "mean_var_done", "variance_done", "inverse_variance_ready"))


def moments(dve, s, apart, ln, n, rows):
    for t in range(TB):
        dve.bn_stats(ln.stats[:, t, :], rows(t)).then_inc(s.stats, 1)
    dve.wait_ge(s.stats, TB * n + TB)
    dve.sem_inc(apart, 1)
    for t in range(TB):
        dve.bn_aggr(ln.mv[:, t, :], ln.stats[:, t, :]).then_inc(s.mv, 1)
    dve.wait_ge(s.mv, TB * n + TB)
    dve.tensor_scalar(ln.var[:, :], ln.mv[:, :, 1], EPS, None, ALU.add).then_inc(s.var, 1)
    dve.wait_ge(s.var, n + 1)
    dve.reciprocal(ln.inv[:, :], ln.var[:, :]).then_inc(s.inv, 1)


def row_tile(A, b, t):
    return A[:, bass.ds(b * TB + t, 1), :].rearrange("p a d -> p (a d)")


def project_heads(nc, io, keep):
    X, ident, Q4, K4, Vg = keep["X"], keep["ident"], keep["Q4"], keep["K4"], keep["Vg"]
    tri = keep["tri"]
    with ExitStack() as ctx:
        m = Scope(nc, ctx, "p1_")
        W = m.sb("l0_w", [P, 5, D])
        rope = m.sb("rope", [P, 2, S])
        stats = m.sb("stats", [P, TB, 6])
        mv = m.sb("mv", [P, TB, 2])
        var, inv_var = m.sb("var", [P, TB]), m.sb("inv_var", [P, TB])
        rstd = m.sb("rstd", [P, TB])
        xn = m.sb("xn", [P, TB, D])
        xnT = m.sb("xnT", [P, S])
        part_c = m.sb("part_c", [P, 2, S])
        part_s = m.sb("part_s", [P, 2, S])
        rot = m.sb("rot", [P, 2, S])
        rest = m.sb("rest", [P, 2, 2, S])
        split = m.sb("split", [P, 2, 3, S], BF16)
        bank = [m.ps(f"proj{i}", [P, S]) for i in range(4)]

        s_x, s_w = m.sem("x_loaded"), m.sem("w_loaded")
        s_ident = m.sem("ident_done")
        s_var = m.sem("inv_var_steps")
        s_stat, s_agg, s_rstd, s_xn = m.sem("stats_done"), m.sem("mean_var_done"), m.sem("rstd_done"), m.sem("xn_ready")
        s_tr, s_xnT = m.sem("xn_transposed"), m.sem("xnT_ready")
        s_proj, s_v = m.sem("projected"), m.sem("v_projected")
        s_c, s_s, s_rot = m.sem("cos_part_done"), m.sem("sin_part_done"), m.sem("rotated")
        s_p1, s_r1, s_p2, s_r2, s_p3 = (m.sem(n) for n in ("part1", "rest1", "part2", "rest2", "part3"))
        s_vout = m.sem("v_kept")
        s_out = m.sem("splits_stored")
        s_z = m.sem("zeroed")
        apart = keep["apart"]
        block = ctx.enter_context(nc.Block())

        @block.sync
        def _(sp):
            sp.dma_start(X[:, :, :], io["x"].rearrange("b (t p) d -> p (b t) d", p=P)).then_inc(s_x, 16)
            sp.dma_start(W[:, :, :], io["l0_w"].rearrange("e j o -> e j o")[:, 0:5, :]).then_inc(s_w, 16)
            sp.dma_start(rope[:, :, :], io["rope"]).then_inc(s_w, 16)
            with sp.Fori(0, B) as b:
                sp.wait_ge(s_p3, 2 * b + 2)
                sp.wait_ge(s_p2, 2 * b + 2)
                sp.dma_start(io["q_parts"][:, bass.ds(b, 1), :, :].rearrange("i b r s -> r (b i) s"),
                             split[:, 0, :, :]).then_inc(s_out, 16)
                sp.dma_start(io["k_parts"][:, bass.ds(b, 1), :, :].rearrange("i b r s -> r (b i) s"),
                             split[:, 1, :, :]).then_inc(s_out, 16)
            sp.wait_ge(s_out, 32 * B)

        @block.gpsimd
        def _(pool):
            pool.memset(ident[:, :], 0.0).then_inc(s_ident, 1)
            pool.wait_ge(s_ident, 1)
            pool.affine_select(out=ident[:, :], in_=ident[:, :], compare_op=ALU.not_equal, fill=1.0, base=0,
                               pattern=[[-1, P]], channel_multiplier=1).then_inc(s_ident, 1)
            pool.memset(tri[:, :], 0.0).then_inc(s_z, 1)
            pool.wait_ge(s_z, 1)
            pool.affine_select(out=tri[:, 3 * P:4 * P], in_=tri[:, 3 * P:4 * P], compare_op=ALU.is_ge, fill=LOW,
                               base=0, pattern=[[-1, P]], channel_multiplier=1).then_inc(s_z, 1)
            pool.wait_ge(s_z, 2)
            pool.memset(Q4[64:P, :, :, :].bitcast(F32), 0.0).then_inc(s_z, 1)
            pool.memset(K4[64:P, :, :, :].bitcast(F32), 0.0).then_inc(s_z, 1)
            pool.wait_ge(s_z, 4)
            pool.memset(K4[96:99, :, :, :], 1.0).then_inc(s_z, 1)
            pool.wait_ge(s_z, 5)
            with pool.Fori(0, B) as b:
                for w in range(2):
                    pool.wait_ge(s_rot, 2 * b + w + 1)
                    pool.wait_ge(s_p1, 2 * b + w + 1)
                    pool.tensor_tensor(rest[:, w, 0, :], rot[:, w, :], split[:, w, 0, :], ALU.subtract).then_inc(s_r1, 1)
                    pool.wait_ge(s_p2, 2 * b + w + 1)
                    pool.tensor_tensor(rest[:, w, 1, :], rest[:, w, 0, :], split[:, w, 1, :], ALU.subtract).then_inc(s_r2, 1)
                    pool.wait_ge(s_r2, 2 * b + w + 1)
                    pool.sem_inc(apart["pool"], 1)
                    pool.tensor_copy(split[:, w, 2, :], rest[:, w, 1, :]).then_inc(s_p3, 1)
                    pool.wait_ge(s_p3, 2 * b + w + 1)

        @block.vector
        def _(dve):
            dve.memset(keep["Vone"][:, :, :, :, :], 0.0).then_inc(s_stat, 1)
            dve.wait_ge(s_stat, 1)
            dve.memset(keep["Vone"][:, :, :, :, HD:HD + 1], 1.0).then_inc(s_stat, 1)
            dve.wait_ge(s_x, 16)
            dve.wait_ge(s_w, 32)
            with dve.Fori(0, B) as b:
                for t in range(TB):
                    dve.bn_stats(stats[:, t, :], X[:, bass.ds(b * TB + t, 1), :].rearrange("p a d -> p (a d)")).then_inc(s_stat, 1)
                dve.wait_ge(s_stat, TB * b + TB + 2)
                dve.sem_inc(apart["dve"], 1)
                for t in range(TB):
                    dve.bn_aggr(mv[:, t, :], stats[:, t, :]).then_inc(s_agg, 1)
                dve.wait_ge(s_agg, TB * b + TB)
                dve.tensor_scalar(var[:, :], mv[:, :, 1], EPS, None, ALU.add).then_inc(s_var, 1)
                dve.wait_ge(s_var, 2 * b + 1)
                dve.reciprocal(inv_var[:, :], var[:, :]).then_inc(s_var, 1)
                dve.wait_ge(s_rstd, b + 1)
                for t in range(TB):
                    dve.tensor_scalar(xn[:, t, :], X[:, bass.ds(b * TB + t, 1), :].rearrange("p a d -> p (a d)"),
                                      mv[:, t, 0:1], rstd[:, t:t + 1], ALU.subtract, ALU.mult).then_inc(s_xn, 1)
                for w in range(2):
                    dve.wait_ge(s_proj, 4 * b + 2 * w + 1)
                    dve.tensor_tensor(part_c[:, w, :], bank[(1, 3)[w]][:, :], rope[:, 0, :], ALU.mult).then_inc(s_c, 1)
                    dve.wait_ge(s_proj, 4 * b + 2 * w + 2)
                    dve.tensor_tensor(part_s[:, w, :], bank[(2, 0)[w]][:, :], rope[:, 1, :], ALU.mult).then_inc(s_s, 1)
                    dve.wait_ge(s_s, 2 * b + w + 1)
                    dve.wait_ge(s_c, 2 * b + w + 1)
                    dve.tensor_tensor(rot[:, w, :], part_c[:, w, :], part_s[:, w, :], ALU.add).then_inc(s_rot, 1)
                dve.wait_ge(s_r1, 2 * b + 2)

        @block.scalar
        def _(act):
            with act.Fori(0, B) as b:
                act.wait_ge(s_var, 2 * b + 2)
                act.activation(rstd[:, :], inv_var[:, :], ACT.Sqrt).then_inc(s_rstd, 1)
                act.wait_ge(s_tr, b + 1)
                act.activation(xnT[:, :], bank[0][:, :], ACT.Copy).then_inc(s_xnT, 1)
                for w in range(2):
                    act.wait_ge(s_rot, 2 * b + w + 1)
                    act.activation(split[:, w, 0, :], rot[:, w, :], ACT.Copy).then_inc(s_p1, 1)
                    act.wait_ge(s_r1, 2 * b + w + 1)
                    act.activation(split[:, w, 1, :], rest[:, w, 0, :], ACT.Copy).then_inc(s_p2, 1)
                act.wait_ge(s_v, b + 1)
                for g in range(G):
                    act.activation(Vg[:, bass.ds(b * G + g, 1), :, :].rearrange("p a t r -> p (a t) r"),
                                   bank[1][:, :].rearrange("p (t g r) -> p t g r", t=TB, g=G)[:, :, g, :],
                                   ACT.Copy).then_inc(s_vout, 1)
                act.wait_ge(s_p3, 2 * b + 2)
                act.wait_ge(s_out, 32 * b + 32)

        @block.tensor
        def _(pe):
            pe.wait_ge(s_ident, 2)
            pe.wait_ge(s_w, 32)
            pe.wait_ge(s_stat, 2)
            with pe.Fori(0, B) as b:
                pe.wait_ge(s_xn, TB * b + TB)
                for t in range(TB):
                    tr = pe.transpose(bank[0][:, t * P:(t + 1) * P], xn[:, t, :], ident[:, :])
                tr.then_inc(s_tr, 1)
                pe.wait_ge(s_xnT, b + 1)
                for j, k in ((0, 1), (1, 2), (2, 3), (3, 0)):
                    for c in range(2):
                        mm = pe.matmul(bank[k][:, c * 512:(c + 1) * 512], W[:, j, :], xnT[:, c * 512:(c + 1) * 512],
                                       start=True, stop=True)
                    mm.then_inc(s_proj, 1)
                pe.wait_ge(s_c, 2 * b + 1)
                for t in range(TB):
                    mm = pe.matmul(bank[1][:, t * P:(t + 1) * P], xnT[:, t * P:(t + 1) * P], W[:, 4, :],
                                   start=True, stop=True)
                mm.then_inc(s_v, 1)
                pe.wait_ge(s_vout, G * b + G)
                pe.wait_ge(s_s, 2 * b + 2)


STEPS = [(0, kb) for kb in range(4)] + [(1, kb) for kb in range(8)]
NS = len(STEPS)
ST_LEAD, MAX_LEAD = 2, 23
MAX_STEPS = [
    [(6, 0, 512, "first"), (0, 0, 128, "only"), (7, 0, 512, "first"), (2, 0, 384, "only")],
    [(4, 0, 512, "first"), (5, 0, 512, "first"), (1, 0, 256, "only"), (5, 512, 256, "last")],
    [(3, 0, 512, "only"), (4, 512, 128, "last"), (7, 512, 512, "last"), (6, 512, 384, "last")],
]


def span(step):
    c, kb = STEPS[step]
    q0 = max(c * 512, kb * P)
    return q0, (c + 1) * 512 - q0


def causal_attention(nc, io, keep):
    ident, Q4, K4, Vg, Vone, tri = (keep[k] for k in ("ident", "Q4", "K4", "Vg", "Vone", "tri"))
    NB = G * NS
    with ExitStack() as ctx:
        m = Scope(nc, ctx, "p2_")
        PT = m.sb("probs", [P, 3, GH, 512])
        rowmax = m.sb("rowmax", [P, 2, GH, TB])
        half_max = m.sb("half_max", [P, 2, GH, 4])
        negmax = m.sb("negmax", [GH * TB, P])
        max_rest = m.sb("max_rest", [GH * TB, 2, P])
        max_parts = m.sb("max_parts", [GH * TB, 3, P], BF16)
        o_sb = m.sb("o_sb", [P, 2, 512])
        st = [m.ps(f"st{i}", [P, 2, 512]) for i in range(2)]
        sq = [m.ps(f"sq{i}", [P, 512]) for i in range(3)]
        o_ps = m.ps("o_ps", [P, 512])
        mt = st[1][0:GH * TB, 1, 0:P]

        s_ops = [m.sem(f"operands_loaded{g}") for g in range(G)]
        s_st, s_exp = m.sem("scores_ready"), m.sem("exps_done")
        s_diag = m.sem("diagonal_masked")
        s_pv = m.sem("pv_done")
        s_sq, s_max = m.sem("score_rows_ready"), m.sem("maxima_done")
        s_mt, s_neg = m.sem("maxima_transposed"), m.sem("maxima_negated")
        s_sp = m.sem("maxima_split_steps")
        s_row = m.sem("maxima_rows_stored")
        s_v = m.sem("v_group_ready")
        s_o = m.sem("o_evacuated")
        s_oout = [m.sem(f"o_stored{c}") for c in range(2)]
        apart = keep["apart"]
        block = ctx.enter_context(nc.Block())

        def batches(eng, body):
            with eng.Fori(0, B - 1) as b:
                body(b, False)
            body(B - 1, True)

        def load(sp, b, g):
            rows = slice(32 * g, 32 * g + 32)
            for i in range(3):
                for dst, src, parts in ((Q4, io["q_parts"], [i, i, i]), (K4, io["k_parts"], [0, 1, 2])):
                    src = src[parts[0]:parts[0] + 1] if parts[0] == parts[2] else src
                    src = src[:, bass.ds(b, 1), rows, :].rearrange("j b (d h) s -> (j b) d (h s)", h=GH).broadcast_to([3, HD, GH * S])
                    sp.dma_start(dst[24 * i:24 * i + 24, g, :, :].rearrange("p h s -> p (h s)"), src).then_inc(s_ops[g], 16)

        OPS = 6 * 16

        @block.sync
        def _(sp):
            for c in range(2):
                sp.sem_inc(s_oout[c], 16)
            for g in range(G):
                load(sp, 0, g)

            def max_rows(n, buf):
                sp.wait_ge(s_sp, 5 * n + 10)
                for i in range(3):
                    sp.dma_start(Q4[96 + i:97 + i, buf, :, :].rearrange("a h (t q) -> a (h t) q", q=P),
                                 max_parts[:, i, :]).then_inc(s_row, 16)

            def store_o(b, g, c):
                sp.wait_ge(s_o, 2 * (G * b + g) + c + 2)
                sp.dma_start(io["heads_out"][bass.ds(b * G + g, 1), :, c * 512:(c + 1) * 512].rearrange("a r s -> r (a s)"),
                             o_sb[:, c, :]).then_inc(s_oout[c], 16)

            max_rows(0, 0)

            def body(b, last):
                for g in range(G):
                    if not (last and g == G - 1):
                        max_rows(b * G + g + 1, (g + 1) % G)
                    store_o(b, g, 0)
                    if not last:
                        sp.wait_ge(s_st, 2 * NS * (b * G + g + 1))
                        load(sp, b + 1, g)
                    store_o(b, g, 1)

            batches(sp, body)
            for c in range(2):
                sp.wait_ge(s_oout[c], 16 * (B * G + 1))

        @block.tensor
        def _(pe):
            def scores(b, i, last=False):
                final = last and i // NS == G - 1
                g, s = i // NS % G, i % NS
                b = b + i // NB
                c, kb = STEPS[s]
                q0, w = span(s)
                if s == 0:
                    pe.wait_ge(s_row, 48 * (b * G + g + 1))
                def tile(hp):
                    u = 2 * ((b * G + g) * NS + s) + hp
                    pe.wait_ge(s_exp, u + 1)
                    if s == 4 and hp == 1 and not final:
                        pe.wait_ge(s_neg, b * G + g + 3)
                    for h in (0, 1):
                        mm = pe.matmul(st[hp][:, h, 0:w], K4[:, g, 2 * hp + h, kb * P:(kb + 1) * P],
                                       Q4[:, g, 2 * hp + h, q0:q0 + w], start=True, stop=True)
                    mm.then_inc(s_st, 1)
                return [lambda: tile(0), lambda: tile(1)]

            def maxima(b, i):
                g, ms = i // NS % G, i % NS
                b = b + i // NB
                h = ms // 3
                if ms == 0:
                    pe.wait_ge(s_ops[g], OPS * (b + 1))
                def tile(j):
                    qb, k0, w, _ = MAX_STEPS[ms % 3][j]
                    n = 4 * ((b * G + g) * NS + ms) + j
                    pe.wait_ge(s_max, n + 1)
                    pe.matmul(sq[(4 * ms + j) % 3][:, 0:w], Q4[0:96, g, h, qb * P:(qb + 1) * P], K4[0:96, g, h, k0:k0 + w],
                              start=True, stop=True).then_inc(s_sq, 1)
                return [lambda j=j: tile(j) for j in range(4)]

            def transpose_max(n, par):
                pe.wait_ge(s_max, 4 * NS * (n + 1) + 3)
                pe.wait_ge(s_neg, n + 1)
                pe.matmul(mt, rowmax[:, par, :, :].rearrange("p h t -> p (h t)"), ident[:, :],
                          is_transpose=True, start=True, stop=True).then_inc(s_mt, 1)

            def pv(b, i):
                g, s = i // NS, i % NS
                c, kb = STEPS[s]
                q0, w = span(s)
                n = b * G + g
                if s == 0:
                    pe.wait_ge(s_v, n + 1)
                if kb == 0:
                    pe.wait_ge(s_o, 2 * n + c + 1)
                if kb >= 4 * c:
                    pe.wait_ge(s_diag, TB * n + kb + 1)
                else:
                    pe.wait_ge(s_exp, 2 * (n * NS + s) + 4)
                for j in range(GH):
                    mm = pe.matmul(o_ps[32 * j:32 * j + 32, q0 - c * 512:512], Vone[:, g % 2, kb, j, :],
                                   PT[:, s % 3, j, 0:w], start=(kb == 0), stop=(kb == 4 * c + 3))
                mm.then_inc(s_pv, 1)

            for i in range(MAX_LEAD):
                for t in maxima(0, i):
                    t()
                if i == NS - 1:
                    transpose_max(0, 0)
            for i in range(ST_LEAD):
                for t in scores(0, i):
                    t()

            def body(b, last):
                for i in range(NB):
                    sc = scores(b, i + ST_LEAD, last) if not (last and i + ST_LEAD >= NB) else []
                    mx = maxima(b, i + MAX_LEAD) if not (last and i + MAX_LEAD >= NB) else []
                    if i % NS == 4 - ST_LEAD and not (last and i // NS == G - 1):
                        pe.wait_ge(s_exp, 2 * (b * NB + i + ST_LEAD) + 2)
                        transpose_max(b * G + i // NS + 1, (i // NS + 1) % 2)
                    for t in sc[0:1] + mx[0:1] + sc[1:2] + mx[1:3] + [lambda: pv(b, i)] + mx[3:4]:
                        t()

            batches(pe, body)

        @block.vector
        def _(dve):
            def maxima(b, i):
                g, ms = i // NS % G, i % NS
                b = b + i // NB
                h = ms // 3
                n0 = 4 * ((b * G + g) * NS + ms)
                if ms == 0:
                    dve.wait_ge(s_mt, b * G + g + 1)
                for j, (qb, k0, w, how) in enumerate(MAX_STEPS[ms % 3]):
                    dve.wait_ge(s_sq, n0 + j + 1)
                    bank = sq[(4 * ms + j) % 3]
                    out = rowmax[:, g % 2, h, qb:qb + 1]
                    part = half_max[:, g % 2, h, qb - 4:qb - 3] if qb >= 4 else None
                    if how == "first":
                        dve.tensor_reduce(part, bank[:, 0:w], AX.X, ALU.max).then_inc(s_max, 1)
                        continue
                    if how == "last":
                        dve.wait_ge(s_max, n0 + j + 3)
                    dve.sem_inc(apart["dve"], 1)
                    dve.tensor_tensor_reduce(out=bank[:, 0:w], in0=bank[:, 0:w], in1=tri[:, 512 - w:512], scale=1.0,
                                             scalar=(LOW if how == "only" else part), op0=ALU.add, op1=ALU.max,
                                             accum_out=out).then_inc(s_max, 1)

            dve.sem_inc(s_max, 3)
            dve.sem_inc(s_mt, 2)
            for i in range(MAX_LEAD):
                maxima(0, i)

            def body(b, last):
                for i in range(NB):
                    if not (last and i + MAX_LEAD >= NB):
                        maxima(b, i + MAX_LEAD)

            batches(dve, body)

        @block.scalar
        def _(act):
            def exps(b, i):
                s = i % NS
                _, w = span(s)
                n = (b * G) * NS + i
                act.wait_ge(s_pv, n + 1)
                for hp in range(2):
                    act.wait_ge(s_st, 2 * n + hp + 1)
                    act.activation(PT[:, s % 3, 2 * hp:2 * hp + 2, 0:w], st[hp][:, :, 0:w], ACT.Exp,
                                   scale=SCALE).then_inc(s_exp, 1)

            def negate(n):
                act.wait_ge(s_mt, n + 3)
                act.wait_ge(s_sp, 5 * n + 5)
                act.activation(negmax[:, :], mt, ACT.Copy, scale=-1.0).then_inc(s_neg, 1)

            act.sem_inc(s_exp, 2)
            act.sem_inc(s_o, 1)
            act.sem_inc(s_neg, 1)
            negate(0)
            for i in range(ST_LEAD):
                exps(0, i)

            def body(b, last):
                for i in range(NB):
                    g, s = i // NS, i % NS
                    if s == 4 - ST_LEAD and not (last and g == G - 1):
                        negate(b * G + g + 1)
                    if not (last and i + ST_LEAD >= NB):
                        exps(b, i + ST_LEAD)
                    if s in (3, NS - 1):
                        c = int(s > 3)
                        n = b * G + g
                        act.wait_ge(s_pv, b * NB + i + 4)
                        act.wait_ge(s_oout[c], 16 * n + 16)
                        act.activation(o_sb[:, c, :], o_ps[:, :], ACT.Copy).then_inc(s_o, 1)

            batches(act, body)

        @block.gpsimd
        def _(pool):
            def v_group(n, par):
                pool.wait_ge(s_pv, NS * n - NS + 3)
                pool.sem_inc(apart["pool"], 1)
                pool.tensor_copy(Vone[:, par, :, :, 0:HD],
                                 Vg[:, bass.ds(n, 1), :, :].rearrange("p a t (h d) -> p (a t) h d", h=GH)).then_inc(s_v, 1)
                pool.wait_ge(s_v, n + 1)

            def split_max(n, first=False):
                pool.wait_ge(s_neg, n + 2)
                if not first:
                    pool.wait_ge(s_row, 48 * n)
                src = negmax[:, :]
                for i in range(3):
                    pool.sem_inc(apart["pool"], 1)
                    pool.tensor_copy(max_parts[:, i, :], src).then_inc(s_sp, 1)
                    pool.wait_ge(s_sp, 5 * n + 2 * i + 6)
                    if i < 2:
                        pool.tensor_tensor(max_rest[:, i, :], src, max_parts[:, i, :], ALU.subtract).then_inc(s_sp, 1)
                        pool.wait_ge(s_sp, 5 * n + 2 * i + 7)
                        src = max_rest[:, i, :]

            def mask(b, i):
                s = i % NS
                c, kb = STEPS[s]
                if kb < 4 * c:
                    return
                pool.wait_ge(s_exp, 2 * (b * NB + i) + 4)
                pool.sem_inc(apart["pool"], 1)
                part = PT[:, s % 3, :, 0:P]
                pool.affine_select(out=part, in_=part, compare_op=ALU.is_ge, fill=0.0, base=0,
                                   pattern=[[0, GH], [1, P]], channel_multiplier=-1).then_inc(s_diag, 1)
                pool.wait_ge(s_diag, TB * G * b + TB * (i // NS) + kb + 1)

            pool.sem_inc(s_pv, 3)
            pool.sem_inc(s_sp, 5)
            pool.tensor_copy(Vone[:, 0, :, :, 0:HD], Vg[:, 0, :, :].rearrange("p t (h d) -> p t h d", h=GH)).then_inc(s_v, 1)
            pool.wait_ge(s_v, 1)
            split_max(0, first=True)
            for i in range(ST_LEAD):
                mask(0, i)

            def body(b, last):
                for i in range(NB):
                    g, s = i // NS, i % NS
                    if not (last and i + ST_LEAD >= NB):
                        mask(b, i + ST_LEAD)
                    if not (last and g == G - 1):
                        if s == 3:
                            v_group(b * G + g + 1, (g + 1) % 2)
                        if s == 5:
                            split_max(b * G + g + 1)

            batches(pool, body)


RING = 4
MAXTILES = -(-(T + E0 - 1) // RING) * RING


def merge_heads(nc, io, keep):
    X, ident, XN, XH = keep["X"], keep["ident"], keep["XN"], keep["XH"]
    with ExitStack() as ctx:
        m = Scope(nc, ctx, "p3_")
        Wo = m.sb("wo", [P, D])
        C = m.sb("centroids", [P, E0])
        att = m.sb("att", [P, B, S])
        sums = m.sb("sums", [P, B, S])
        recip = m.sb("recip", [P, S])
        attT = m.sb("attT", [P, S])
        stats = m.sb("stats", [P, 2, TB, 6])
        mv = m.sb("mv", [P, 2, TB, 2])
        var, inv, rstd = m.sb("var", [P, 3, TB]), m.sb("inv", [P, 3, TB]), m.sb("rstd", [P, 3, TB])
        yn = m.sb("yn", [P, TB, D])
        xn = m.sb("xn", [P, TB, D])
        xnT = m.sb("xnT", [P, S])
        y_ps = m.ps("y_ps", [P, TB, D])
        t_ps = m.ps("t_ps", [P, S])
        a_ps = m.ps("a_ps", [P, TB, E0])

        s_w = m.sem("w_loaded")
        s_att = [m.sem(f"att_loaded{b}") for b in range(B)]
        s_rc, s_attT, s_y = m.sem("sums_inverted"), m.sem("attT_ready"), m.sem("y_ready")
        s_st = m.sem("ln_steps")
        s_in, s_rt = m.sem("inverse_variance_ready"), m.sem("rstd_ready")
        s_yn, s_x = m.sem("y_normed"), m.sem("x_updated")
        s_xn, s_xh = m.sem("xn_ready"), m.sem("xh_ready")
        s_kept = m.sem("xn_kept")
        s_tr, s_xnT, s_a, s_af = m.sem("xn_transposed"), m.sem("xnT_ready"), m.sem("affinity_ready"), m.sem("affinity_kept")
        apart = keep["apart"]
        block = ctx.enter_context(nc.Block())

        @block.sync
        def _(sp):
            sp.dma_start(Wo[:, :], io["l0_w"][:, 5, :]).then_inc(s_w, 16)
            sp.dma_start(C[:, :], io["centroids"]).then_inc(s_w, 16)
            for b in range(B):
                rows = io["heads_out"][b * G:(b + 1) * G, :, :].rearrange("g (j r) s -> (g j) r s", j=GH)
                sp.dma_start(sums[:, b, :], rows[:, HD:HD + 1, :].broadcast_to([H, HD, S])).then_inc(s_att[b], 16)
                sp.dma_start(att[:, b, :], rows[:, 0:HD, :]).then_inc(s_att[b], 16)

        @block.vector
        def _(dve):
            for b in range(B):
                dve.wait_ge(s_att[b], 32)
            with dve.Fori(0, B) as b:
                dve.reciprocal(recip[:, :], sums[:, bass.ds(b, 1), :].rearrange("p a s -> p (a s)")).then_inc(s_rc, 1)
                dve.wait_ge(s_rc, b + 1)
                dve.tensor_tensor(attT[:, :], att[:, bass.ds(b, 1), :].rearrange("p a s -> p (a s)"), recip[:, :],
                                  ALU.mult).then_inc(s_attT, 1)
                dve.wait_ge(s_y, b + 1)
                for t in range(TB):
                    dve.bn_stats(stats[:, 0, t, :], y_ps[:, t, :]).then_inc(s_st, 1)
                k = b * (4 * TB + 4)
                dve.wait_ge(s_st, k + TB)
                dve.sem_inc(apart["dve"], 1)
                for t in range(TB):
                    dve.bn_aggr(mv[:, 0, t, :], stats[:, 0, t, :]).then_inc(s_st, 1)
                dve.wait_ge(s_st, k + 2 * TB)
                dve.tensor_scalar(var[:, 0, :], mv[:, 0, :, 1], EPS, None, ALU.add).then_inc(s_st, 1)
                dve.wait_ge(s_st, k + 2 * TB + 1)
                dve.reciprocal(inv[:, 0, :], var[:, 0, :]).then_inc(s_in, 1)
                dve.wait_ge(s_rt, 3 * b + 1)
                for t in range(TB):
                    dve.tensor_scalar(yn[:, t, :], y_ps[:, t, :], mv[:, 0, t, 0:1], rstd[:, 0, t:t + 1],
                                      ALU.subtract, ALU.mult).then_inc(s_yn, 1)
                dve.wait_ge(s_yn, TB * b + TB)
                rows = X[:, bass.ds(b * TB, TB), :]
                dve.tensor_tensor(rows, rows, yn[:, :, :], ALU.add).then_inc(s_x, 1)
                dve.wait_ge(s_x, b + 1)
                dve.sem_inc(apart["dve"], 1)
                for t in range(TB):
                    dve.bn_stats(stats[:, 1, t, :], X[:, bass.ds(b * TB + t, 1), :].rearrange("p a d -> p (a d)")).then_inc(s_st, 1)
                dve.wait_ge(s_st, k + 3 * TB + 1)
                dve.sem_inc(apart["dve"], 1)
                for t in range(TB):
                    dve.bn_aggr(mv[:, 1, t, :], stats[:, 1, t, :]).then_inc(s_st, 1)
                dve.wait_ge(s_st, k + 4 * TB + 1)
                dve.tensor_scalar(var[:, 1, :], mv[:, 1, :, 1], EPS, None, ALU.add).then_inc(s_st, 1)
                dve.wait_ge(s_st, k + 4 * TB + 2)
                dve.reciprocal(inv[:, 1, :], var[:, 1, :]).then_inc(s_in, 1)
                dve.wait_ge(s_in, 3 * b + 2)
                dve.tensor_tensor(var[:, 2, :], mv[:, 1, :, 1], inv[:, 1, :], ALU.mult).then_inc(s_st, 1)
                dve.wait_ge(s_st, k + 4 * TB + 3)
                dve.tensor_scalar(rstd[:, 2, :], var[:, 2, :], EPS, None, ALU.add).then_inc(s_st, 1)
                dve.wait_ge(s_st, k + 4 * TB + 4)
                dve.reciprocal(inv[:, 2, :], rstd[:, 2, :]).then_inc(s_in, 1)
                dve.wait_ge(s_rt, 3 * b + 3)
                for t in range(TB):
                    dve.tensor_scalar(xn[:, t, :], X[:, bass.ds(b * TB + t, 1), :].rearrange("p a d -> p (a d)"),
                                      mv[:, 1, t, 0:1], rstd[:, 1, t:t + 1], ALU.subtract, ALU.mult).then_inc(s_xn, 1)
                dve.wait_ge(s_xn, TB * b + TB)
                for t in range(TB):
                    dve.tensor_scalar(XH[:, bass.ds(b * TB + t, 1), :].rearrange("p a d -> p (a d)"), xn[:, t, :],
                                      rstd[:, 2, t:t + 1], None, ALU.mult).then_inc(s_xh, 1)
                dve.wait_ge(s_a, b + 1)
                dve.tensor_copy(keep["aff"][:, bass.ds(b * TB, TB), :], a_ps[:, :, :]).then_inc(s_af, 1)
                dve.wait_ge(s_af, b + 1)
                dve.wait_ge(s_xh, TB * b + TB)
                dve.wait_ge(s_kept, b + 1)

        @block.scalar
        def _(act):
            with act.Fori(0, B) as b:
                for k in range(3):
                    act.wait_ge(s_in, 3 * b + k + 1)
                    act.activation(rstd[:, k, :], inv[:, k, :], ACT.Sqrt).then_inc(s_rt, 1)
                act.wait_ge(s_tr, b + 1)
                act.activation(xnT[:, :], t_ps[:, :], ACT.Copy).then_inc(s_xnT, 1)

        @block.gpsimd
        def _(pool):
            with pool.Fori(0, B) as b:
                pool.wait_ge(s_xn, TB * b + TB)
                pool.sem_inc(apart["pool"], 1)
                pool.tensor_copy(XN[:, bass.ds(b * TB, TB), :], xn[:, :, :]).then_inc(s_kept, 1)
                pool.wait_ge(s_kept, b + 1)

        @block.tensor
        def _(pe):
            pe.wait_ge(s_w, 32)
            with pe.Fori(0, B) as b:
                pe.wait_ge(s_attT, b + 1)
                for t in range(TB):
                    mm = pe.matmul(y_ps[:, t, :], attT[:, t * P:(t + 1) * P], Wo[:, :], start=True, stop=True)
                mm.then_inc(s_y, 1)
                pe.wait_ge(s_xn, TB * b + TB)
                for t in range(TB):
                    mm = pe.transpose(t_ps[:, t * P:(t + 1) * P], xn[:, t, :], ident[:, :])
                mm.then_inc(s_tr, 1)
                pe.wait_ge(s_xnT, b + 1)
                for t in range(TB):
                    mm = pe.matmul(a_ps[:, t, :], xnT[:, t * P:(t + 1) * P], C[:, :], start=True, stop=True)
                mm.then_inc(s_a, 1)


def route(nc, io, keep):
    XH, aff, pos, gate, tile_expert = keep["XH"], keep["aff"], keep["pos"], keep["gate"], keep["tile_expert"]
    NE = T * E0
    with ExitStack() as ctx:
        m = Scope(nc, ctx, "p4_")
        top = m.sb("top", [P, T])
        tied = m.sb("tied", [P, T, E0])
        early = m.sb("early", [P, E0])
        score = m.sb("score", [P, T, E0])
        best = m.sb("best", [P, T])
        chosen = m.sb("chosen", [P, T, E0])
        chosen_bf = m.sb("chosen_bf", [P, T, E0], BF16)
        before = m.sb("before", [P, P], BF16)
        ones = m.sb("ones", [P, P], BF16)
        scan = m.sb("scan", [P, 6, T, E0])
        steps = m.sb("steps", [P, T])
        over = m.sb("over", [P, E0, T])
        tiles = m.sb("tiles", [P, E0])
        lower = m.sb("lower", [P, E0, E0])
        prod = m.sb("prod", [P, E0, E0])
        first = m.sb("first", [P, E0])
        last = m.sb("last", [P, E0])
        index = m.sb("index", [P, MAXTILES])
        past = m.sb("past", [P, MAXTILES, E0])
        owner = m.sb("owner", [P, MAXTILES])
        place = m.sb("place", [P, T, E0])
        start = m.sb("start", [P, E0])
        at = m.sb("at", [P, T])
        e_neg = m.sb("e_neg", [P, T])
        zeros = m.sb("zeros", [P, MAXTILES, D])
        rank_ps = m.ps("rank_ps", [P, NE])
        count_ps = m.ps("count_ps", [P, NE])

        s_c, s_z = m.sem("constants"), m.sem("zeros_stored")
        s_zm = m.sem("zeros_made")
        s_d, s_oh, s_cnt, s_e = m.sem("router_steps"), m.sem("chosen_ready"), m.sem("counts_ready"), m.sem("gate_exp")
        s_pos, s_sc = m.sem("places_ready"), m.sem("rows_placed")
        block = ctx.enter_context(nc.Block())

        @block.sync
        def _(sp):
            sp.wait_ge(s_zm, 1)
            sp.dma_start(io["sorted_in"].rearrange("(n p) d -> p n d", p=P), zeros[:, :, :]).then_inc(s_z, 16)

        @block.gpsimd
        def _(pool):
            n = 0
            def step(ins):
                nonlocal n
                n += 1
                ins.then_inc(s_c, 1)
                pool.wait_ge(s_c, n)
            step(pool.iota(early[:, :], [[-1, E0]], base=E0, channel_multiplier=0, allow_small_or_imprecise_dtypes=True))
            step(pool.iota(steps[:, :], [[P, T]], base=0, channel_multiplier=0, allow_small_or_imprecise_dtypes=True))
            step(pool.iota(index[:, :], [[1, MAXTILES]], base=0, channel_multiplier=0, allow_small_or_imprecise_dtypes=True))
            step(pool.memset(ones[:, :], 1.0))
            step(pool.memset(lower[:, :, :], 1.0))
            step(pool.affine_select(out=before[:, :], in_=ones[:, :], compare_op=ALU.is_gt, fill=0.0, base=0,
                                    pattern=[[1, P]], channel_multiplier=-1))
            step(pool.affine_select(out=lower[:, :, :], in_=lower[:, :, :], compare_op=ALU.is_gt, fill=0.0, base=0,
                                    pattern=[[1, E0], [-1, E0]], channel_multiplier=0))
            pool.wait_ge(s_pos, 1)
            pool.wait_ge(s_z, 16)
            for t in range(T):
                pool.indirect_dma_start(io["sorted_in"], bass.IndirectOffsetOnAxis(ap=pos[:, t:t + 1], axis=0),
                                        XH[:, t, :], None).then_inc(s_sc, 16)
            pool.wait_ge(s_sc, 16 * T)

        @block.tensor
        def _(pe):
            pe.wait_ge(s_c, 7)
            pe.wait_ge(s_oh, 1)
            oh = chosen_bf[:, :, :].rearrange("p t e -> p (t e)")
            pe.matmul(rank_ps[:, :], before[:, :], oh, start=True, stop=True).then_inc(s_cnt, 1)
            pe.matmul(count_ps[:, :], ones[:, :], oh, start=True, stop=True).then_inc(s_cnt, 1)

        @block.scalar
        def _(act):
            act.wait_ge(s_d, 1)
            act.activation(e_neg[:, :], top[:, :], ACT.Exp, scale=-1.0).then_inc(s_e, 1)

        @block.vector
        def _(dve):
            n = 0
            def step(ins):
                nonlocal n
                n += 1
                ins.then_inc(s_d, 1)
                dve.wait_ge(s_d, n)
            def over_e(x):
                return x.unsqueeze(2).broadcast_to([P, T, E0])
            step(dve.tensor_reduce(top[:, :], aff[:, :, :], AX.X, ALU.max))
            dve.memset(zeros[:, :, :], 0.0).then_inc(s_zm, 1)
            step(dve.tensor_tensor(tied[:, :, :], aff[:, :, :], over_e(top[:, :]), ALU.is_equal))
            dve.wait_ge(s_c, 7)
            step(dve.tensor_tensor(score[:, :, :], tied[:, :, :], early[:, :].unsqueeze(1).broadcast_to([P, T, E0]), ALU.mult))
            step(dve.tensor_reduce(best[:, :], score[:, :, :], AX.X, ALU.max))
            step(dve.tensor_tensor(chosen[:, :, :], score[:, :, :], over_e(best[:, :]), ALU.is_equal))
            dve.tensor_copy(chosen_bf[:, :, :], chosen[:, :, :]).then_inc(s_oh, 1)
            dve.wait_ge(s_e, 1)
            step(dve.tensor_scalar(at[:, :], e_neg[:, :], 1.0, None, ALU.add))
            step(dve.reciprocal(gate[:, :], at[:, :]))
            dve.wait_ge(s_cnt, 2)
            step(dve.tensor_copy(scan[:, 0, :, :], count_ps[:, :].rearrange("p (t e) -> p t e", t=T)))
            for k in range(5):
                r = 1 << k
                step(dve.tensor_copy(scan[:, k + 1, 0:r, :], scan[:, k, 0:r, :]))
                step(dve.tensor_tensor(scan[:, k + 1, r:T, :], scan[:, k, r:T, :], scan[:, k, 0:T - r, :], ALU.add))
            total = scan[:, 5, T - 1, :]
            step(dve.tensor_tensor(over[:, :, :], total.unsqueeze(2).broadcast_to([P, E0, T]),
                                   steps[:, :].unsqueeze(1).broadcast_to([P, E0, T]), ALU.is_gt))
            step(dve.tensor_reduce(tiles[:, :], over[:, :, :], AX.X, ALU.add))
            step(dve.tensor_tensor(prod[:, :, :], lower[:, :, :], tiles[:, :].unsqueeze(1).broadcast_to([P, E0, E0]), ALU.mult))
            step(dve.tensor_reduce(first[:, :], prod[:, :, :], AX.X, ALU.add))
            step(dve.tensor_tensor(last[:, :], first[:, :], tiles[:, :], ALU.add))
            M = MAXTILES
            step(dve.tensor_tensor(past[:, :, :], index[:, :].unsqueeze(2).broadcast_to([P, M, E0]),
                                   last[:, :].unsqueeze(1).broadcast_to([P, M, E0]), ALU.is_ge))
            step(dve.tensor_reduce(owner[:, :], past[:, :, :], AX.X, ALU.add))
            step(dve.tensor_scalar(tile_expert[:, :], owner[:, :], float(E0 - 1), None, ALU.min))
            step(dve.tensor_scalar(start[:, :], first[:, :], float(P), None, ALU.mult))
            step(dve.tensor_tensor(place[:, :, :], scan[:, 5, :, :], scan[:, 0, :, :], ALU.subtract))
            step(dve.tensor_tensor(tied[:, :, :], place[:, :, :], rank_ps[:, :].rearrange("p (t e) -> p t e", t=T), ALU.add))
            step(dve.tensor_tensor(place[:, :, :], tied[:, :, :], start[:, :].unsqueeze(1).broadcast_to([P, T, E0]), ALU.add))
            step(dve.tensor_tensor(score[:, :, :], place[:, :, :], chosen[:, :, :], ALU.mult))
            step(dve.tensor_reduce(best[:, :], score[:, :, :], AX.X, ALU.add))
            dve.tensor_copy(pos[:, :], best[:, :]).then_inc(s_pos, 1)
            dve.wait_ge(s_pos, 1)


def experts(nc, io, keep):
    ident, tile_expert = keep["ident"], keep["tile_expert"]
    with ExitStack() as ctx:
        m = Scope(nc, ctx, "p5_")
        W1 = m.sb("w1_all", [P, E0, F0])
        W2 = m.sb("w2_all", [P, E0, FC, D])
        small = m.sb("ln_b1", [P, E0, 2 + FC])
        b2 = m.sb("b2_rows", [P, E0, D])
        xs = m.sb("xs", [P, RING, D])
        w1 = m.sb("w1_tile", [P, RING, F0])
        xin = m.sb("xin", [P, RING, P])
        hT = m.sb("hT", [P, RING, FC, P])
        y = m.sb("y", [P, RING, D])
        x_ps = [m.ps(f"x_ps{r}", [P, P]) for r in range(2)]
        h_ps = [m.ps(f"h_ps{r}", [P, FC, P]) for r in range(2)]
        y_ps = [m.ps(f"y_ps{r}", [P, D]) for r in range(2)]

        s_w = m.sem("weights_loaded")
        s_ld = [m.sem(f"tile_loaded{r}") for r in range(RING)]
        s_w1 = m.sem("w1_copied")
        s_tr = m.sem("x_transposed")
        s_in = m.sem("x_scaled")
        s_h = m.sem("h_ready")
        s_r = m.sem("h_relu")
        s_y = m.sem("y_ready")
        s_yo = m.sem("y_kept")
        s_out = [m.sem(f"y_stored{r}") for r in range(RING)]
        apart = keep["apart"]
        block = ctx.enter_context(nc.Block())
        ROUNDS = MAXTILES // RING

        def rounds(eng, body):
            with eng.Fori(0, ROUNDS - 1) as k:
                body(k, False)
            body(ROUNDS - 1, True)

        def expert(eng, i):
            return eng.value_load(tile_expert[0:1, bass.ds(i, 1)], min_val=0, max_val=E0 - 1)

        @block.sync
        def _(sp):
            for r in range(RING):
                sp.sem_inc(s_out[r], 16)
                sp.dma_start(xs[:, r, :], io["sorted_in"][r * P:(r + 1) * P, :]).then_inc(s_ld[r], 16)
            for dst, src in ((W1[:, :, :], "w1"), (W2[:, :, :, :], "w2"), (small[:, :, :], "small")):
                sp.dma_start(dst, io[src]).then_inc(s_w, 16)
            sp.dma_start(b2[:, :, :], io["b2"].rearrange("(a e) d -> a e d", a=1).broadcast_to([P, E0, D])).then_inc(s_w, 16)

            def body(k, last):
                for r in range(RING):
                    i = k * RING + r
                    if not last:
                        sp.wait_ge(s_tr, i + 1)
                        sp.dma_start(xs[:, r, :], io["sorted_in"][bass.ds((i + RING) * P, P), :]).then_inc(s_ld[r], 16)
                    sp.wait_ge(s_yo, i + 3)
                    sp.dma_start(io["sorted_out"][bass.ds(i * P, P), :], y[:, r, :]).then_inc(s_out[r], 16)

            rounds(sp, body)
            for r in range(RING):
                sp.wait_ge(s_out[r], 16 * ROUNDS + 16)

        @block.gpsimd
        def _(pool):
            pool.wait_ge(s_w, 64)

            def body(k, last):
                for r in range(RING):
                    i = k * RING + r
                    e = expert(pool, i)
                    pool.wait_ge(s_h, i + 1)
                    pool.sem_inc(apart["pool"], 1)
                    pool.tensor_copy(w1[:, r, :], W1[:, bass.ds(e, 1), :].rearrange("p a f -> p (a f)")).then_inc(s_w1, 1)
                    pool.wait_ge(s_w1, i + 1)

            rounds(pool, body)

        @block.tensor
        def _(pe):
            def transpose(k, r):
                i = k * RING + r
                pe.wait_ge(s_ld[r % RING], 16 * (k + 1 + r // RING))
                pe.wait_ge(s_in, i + 1)
                pe.transpose(x_ps[r % 2][:, :], xs[:, r % RING, :], ident[:, :]).then_inc(s_tr, 1)

            def hidden(k, r):
                i = k * RING + r
                pe.wait_ge(s_in, i + 3)
                pe.wait_ge(s_w1, i + 1)
                pe.wait_ge(s_r, FC * i + FC)
                for c in range(FC):
                    mm = pe.matmul(h_ps[r % 2][:, c, :], w1[:, r % RING, c * P:(c + 1) * P], xin[:, r % RING, :],
                                   start=True, stop=True)
                mm.then_inc(s_h, 1)

            def output(k, r):
                i = k * RING + r
                e = expert(pe, i)
                pe.wait_ge(s_r, FC * i + 3 * FC)
                pe.wait_ge(s_yo, i + 1)
                for c in range(FC):
                    mm = pe.matmul(y_ps[r % 2][:, :], hT[:, r, c, :], W2[:, bass.ds(e, 1), c, :].rearrange("p a d -> p (a d)"),
                                   start=(c == 0), stop=(c == FC - 1))
                mm.then_inc(s_y, 1)

            pe.wait_ge(s_w, 64)
            transpose(0, 0)
            transpose(0, 1)
            hidden(0, 0)

            def body(k, last):
                for r in range(RING):
                    if not (last and r + 2 >= RING):
                        transpose(k, r + 2)
                    if not (last and r + 1 >= RING):
                        hidden(k, r + 1)
                    output(k, r)

            rounds(pe, body)

        @block.scalar
        def _(act):
            act.sem_inc(s_r, 2 * FC)
            act.wait_ge(s_w, 64)

            def body(k, last):
                for r in range(RING):
                    i = k * RING + r
                    e = expert(act, i)
                    act.wait_ge(s_y, i + 1)
                    act.wait_ge(s_h, i + 5)
                    act.sem_inc(apart["act"], 1)
                    for c in range(FC):
                        act.activation(hT[:, r, c, :], h_ps[r % 2][:, c, :], ACT.Relu,
                                       bias=small[:, bass.ds(e, 1), 2 + c]).then_inc(s_r, 1)

            rounds(act, body)

        @block.vector
        def _(dve):
            def scale(k, r):
                i = k * RING + r
                e = expert(dve, i)
                dve.wait_ge(s_tr, i + 1)
                dve.wait_ge(s_h, i + 1)
                dve.tensor_scalar(xin[:, r % RING, :], x_ps[r % 2][:, :], small[:, bass.ds(e, 1), 0],
                                  small[:, bass.ds(e, 1), 1], ALU.mult, ALU.add).then_inc(s_in, 1)

            dve.sem_inc(s_in, 2)
            dve.sem_inc(s_h, RING)
            dve.sem_inc(s_y, RING)
            dve.sem_inc(s_yo, 2)
            dve.wait_ge(s_w, 64)
            scale(0, 0)
            scale(0, 1)

            def body(k, last):
                for r in range(RING):
                    i = k * RING + r
                    if not (last and r + 2 >= RING):
                        scale(k, r + 2)
                    e = expert(dve, i)
                    dve.wait_ge(s_y, i + 1 + RING)
                    dve.wait_ge(s_out[r], 16 * k + 16)
                    dve.tensor_tensor(y[:, r, :], y_ps[r % 2][:, :], b2[:, bass.ds(e, 1), :].rearrange("p a d -> p (a d)"),
                                      ALU.add).then_inc(s_yo, 1)

            rounds(dve, body)


def normalise(dve, s_step, base, apart, rows, stats, mv, var, inv, s_in):
    for t in range(TB):
        dve.bn_stats(stats[:, t, :], rows(t)).then_inc(s_step, 1)
    dve.wait_ge(s_step, base + TB)
    dve.sem_inc(apart, 1)
    for t in range(TB):
        dve.bn_aggr(mv[:, t, :], stats[:, t, :]).then_inc(s_step, 1)
    dve.wait_ge(s_step, base + 2 * TB)
    dve.tensor_scalar(var, mv[:, :, 1], EPS, None, ALU.add).then_inc(s_step, 1)
    dve.wait_ge(s_step, base + 2 * TB + 1)
    dve.reciprocal(inv, var).then_inc(s_in, 1)


def combine_and_project(nc, io, keep):
    X, XN, ident, gate, pos = (keep[k] for k in ("X", "XN", "ident", "gate", "pos"))
    qT, kT, VP = keep["qT"], keep["kT"], keep["VP"]
    with ExitStack() as ctx:
        m = Scope(nc, ctx, "p6_")
        W = m.sb("w", [P, 4, D])
        bias = m.sb("bias", [P, 3])
        back = m.sb("back", [P, T, D])
        z, zn, xn = (m.sb(n, [P, TB, D]) for n in ("z", "zn", "xn"))
        stats, mv = m.sb("stats", [P, 2, TB, 6]), m.sb("mv", [P, 2, TB, 2])
        var, inv, rstd = (m.sb(n, [P, 2, TB]) for n in ("var", "inv", "rstd"))
        xnT, vT = m.sb("xnT", [P, S]), m.sb("vT", [P, S])
        t_ps = m.ps("t_ps", [P, S])
        p_ps = [m.ps(f"p_ps{j}", [P, S]) for j in range(3)]

        s_w, s_g = m.sem("w_loaded"), m.sem("rows_back")
        s_z, s_st, s_in, s_rt = m.sem("z_ready"), m.sem("ln_steps"), m.sem("inverse_variance_ready"), m.sem("rstd_ready")
        s_zn, s_x, s_xn = m.sem("z_normed"), m.sem("x_updated"), m.sem("xn_ready")
        s_tr, s_xnT = m.sem("xn_transposed"), m.sem("xnT_ready")
        s_p, s_pe, s_vp, s_vpe = m.sem("projected"), m.sem("projections_kept"), m.sem("vp_ready"), m.sem("vp_kept")
        apart = keep["apart"]
        block = ctx.enter_context(nc.Block())

        @block.sync
        def _(sp):
            sp.dma_start(W[:, :, :], io["l1_w"]).then_inc(s_w, 16)
            sp.dma_start(bias[:, :], io["b_qkv"]).then_inc(s_w, 16)

        @block.gpsimd
        def _(pool):
            for t in range(T):
                pool.indirect_dma_start(back[:, t, :], None, io["sorted_out"],
                                        bass.IndirectOffsetOnAxis(ap=pos[:, t:t + 1], axis=0)).then_inc(s_g, 16)

        @block.vector
        def _(dve):
            dve.wait_ge(s_g, 16 * T)
            with dve.Fori(0, B) as b:
                for t in range(TB):
                    dve.scalar_tensor_tensor(out=z[:, t, :], in0=row_tile(back, b, t),
                                             scalar=gate[:, bass.ds(b * TB + t, 1)], in1=row_tile(XN, b, t),
                                             op0=ALU.mult, op1=ALU.add).then_inc(s_z, 1)
                dve.wait_ge(s_z, TB * b + TB)
                dve.sem_inc(apart["dve"], 1)
                k = b * (4 * TB + 2)
                normalise(dve, s_st, k, apart["dve"], lambda t: z[:, t, :], stats[:, 0], mv[:, 0], var[:, 0, :], inv[:, 0, :], s_in)
                dve.wait_ge(s_rt, 2 * b + 1)
                for t in range(TB):
                    dve.tensor_scalar(zn[:, t, :], z[:, t, :], mv[:, 0, t, 0:1], rstd[:, 0, t:t + 1],
                                      ALU.subtract, ALU.mult).then_inc(s_zn, 1)
                dve.wait_ge(s_zn, TB * b + TB)
                rows = X[:, bass.ds(b * TB, TB), :]
                dve.tensor_tensor(rows, rows, zn[:, :, :], ALU.add).then_inc(s_x, 1)
                dve.wait_ge(s_x, b + 1)
                dve.sem_inc(apart["dve"], 1)
                normalise(dve, s_st, k + 2 * TB + 1, apart["dve"], lambda t: row_tile(X, b, t), stats[:, 1], mv[:, 1],
                          var[:, 1, :], inv[:, 1, :], s_in)
                dve.wait_ge(s_rt, 2 * b + 2)
                for t in range(TB):
                    dve.tensor_scalar(xn[:, t, :], row_tile(X, b, t), mv[:, 1, t, 0:1], rstd[:, 1, t:t + 1],
                                      ALU.subtract, ALU.mult).then_inc(s_xn, 1)
                dve.wait_ge(s_tr, b + 1)

        @block.scalar
        def _(act):
            act.wait_ge(s_w, 32)
            with act.Fori(0, B) as b:
                for k in range(2):
                    act.wait_ge(s_in, 2 * b + k + 1)
                    act.activation(rstd[:, k, :], inv[:, k, :], ACT.Sqrt).then_inc(s_rt, 1)
                act.wait_ge(s_tr, b + 1)
                act.activation(xnT[:, :], t_ps[:, :], ACT.Copy).then_inc(s_xnT, 1)
                for j, dst in ((2, vT[:, :]), (0, qT[:, bass.ds(b * S, S)]), (1, kT[:, bass.ds(b * S, S)])):
                    act.wait_ge(s_p, 3 * b + {2: 1, 0: 2, 1: 3}[j])
                    act.sem_inc(apart["act"], 1)
                    act.activation(dst, p_ps[j][:, :], ACT.Identity, bias=bias[:, j:j + 1]).then_inc(s_pe, 1)
                act.wait_ge(s_vp, b + 1)
                act.sem_inc(apart["act"], 1)
                act.activation(VP[:, bass.ds(b * TB, TB), :], t_ps[:, :].rearrange("p (t d) -> p t d", t=TB),
                               ACT.Copy).then_inc(s_vpe, 1)

        @block.tensor
        def _(pe):
            pe.wait_ge(s_w, 32)
            with pe.Fori(0, B) as b:
                pe.wait_ge(s_xn, TB * b + TB)
                for t in range(TB):
                    mm = pe.transpose(t_ps[:, t * P:(t + 1) * P], xn[:, t, :], ident[:, :])
                mm.then_inc(s_tr, 1)
                pe.wait_ge(s_xnT, b + 1)
                for j in (2, 0, 1):
                    for c in range(2):
                        mm = pe.matmul(p_ps[j][:, c * 512:(c + 1) * 512], W[:, j, :], xnT[:, c * 512:(c + 1) * 512],
                                       start=True, stop=True)
                    mm.then_inc(s_p, 1)
                pe.wait_ge(s_pe, 3 * b + 1)
                for t in range(TB):
                    mm = pe.matmul(t_ps[:, t * P:(t + 1) * P], vT[:, t * P:(t + 1) * P], W[:, 3, :], start=True, stop=True)
                mm.then_inc(s_vp, 1)
                pe.wait_ge(s_vpe, b + 1)
                pe.wait_ge(s_pe, 3 * b + 3)


UNIT = 0.2
BAND = {p: float(np.log(p / (1 - p))) for p in (0.95, 0.85, 0.25, 0.1)}
TERMS = ((0.1, ALU.is_ge, ALU.add, 0.5), (0.85, ALU.is_gt, ALU.mult, 2.5),
         (0.25, ALU.is_ge, ALU.mult, 3.5), (0.95, ALU.is_gt, ALU.mult, 2.5))
QK_LEAD, TERM_LEAD, F_LEAD, EXP_LEAD, PV_LEAD = 5, 4, 3, 2, 1
assert TB % 4 == 0


def banded_attention(nc, io, keep):
    ident, qT, kT, VP, Y = (keep[k] for k in ("ident", "qT", "kT", "VP", "Y"))
    with ExitStack() as ctx:
        m = Scope(nc, ctx, "p7_")
        bp = m.sb("b_proj", [P, D])
        q = m.sb("q", [P, 4, P])
        x = m.sb("x", [P, 4, S])
        terms = m.sb("band_terms", [P, 2, 4, S], BF16)
        pairs = m.sb("term_pairs", [P, 2, 2, S], BF16)
        factor = m.sb("factor", [P, S], BF16)
        f = m.sb("f", [P, 2, S])
        top, neg = m.sb("top", [P, 2]), m.sb("neg", [P, 2])
        probs = m.sb("probs", [P, 2, S])
        total = m.sb("total", [P, 4])
        inv = m.sb("inv", [P, 2])
        pT = m.sb("pT", [P, 2, TB, P])
        s_ps = [m.ps(f"s_ps{r}", [P, S]) for r in range(2)]
        t_ps = m.ps("t_ps", [P, TB, P])
        y_ps = [m.ps(f"y_ps{r}", [P, D]) for r in range(2)]

        s_b = m.sem("b_loaded")
        s_q = [m.sem(f"q_loaded{r}") for r in range(4)]
        s_s = m.sem("scores_ready")
        s_x = m.sem("scores_scaled")
        s_term = m.sem("band_terms_ready")
        s_pair = m.sem("term_pairs_ready")
        s_f = m.sem("band_steps")
        s_e = m.sem("exps_ready")
        s_t = m.sem("p_transposed")
        s_pt = m.sem("pT_ready")
        s_y = m.sem("pv_ready")
        s_i = m.sem("sums_inverted")
        s_o = m.sem("rows_out")
        apart = keep["apart"]
        block = ctx.enter_context(nc.Block())

        def batches(eng, body):
            with eng.Fori(0, B - 1) as b:
                body(b, False)
            body(B - 1, True)

        def ahead(last, i):
            return not (last and i >= TB)

        @block.sync
        def _(sp):
            sp.dma_start(bp[:, :], io["b_proj"].rearrange("(a d) -> a d", a=1).broadcast_to([P, D])).then_inc(s_b, 16)

            def load(b, i):
                n = b * TB + i
                sp.wait_ge(s_s, n + 1)
                sp.dma_start(q[:, i % 4, :], qT[:, bass.ds(n * P, P)]).then_inc(s_q[i % 4], 16)

            for i in range(4):
                sp.dma_start(q[:, i, :], qT[:, i * P:(i + 1) * P]).then_inc(s_q[i], 16)

            def body(b, last):
                for i in range(TB):
                    if ahead(last, i + 4):
                        load(b, i + 4)

            batches(sp, body)

        @block.tensor
        def _(pe):
            def scores(b, i):
                n = b * TB + i
                pe.wait_ge(s_q[i % 4], 16 * (b * (TB // 4) + i // 4 + 1))
                pe.wait_ge(s_x, n + 1)
                for c in range(2):
                    mm = pe.matmul(s_ps[i % 2][:, c * 512:(c + 1) * 512], q[:, i % 4, :],
                                   kT[:, bass.ds((b + i // TB) * S + c * 512, 512)], start=True, stop=True)
                mm.then_inc(s_s, 1)

            def transpose(b, i):
                n = b * TB + i
                pe.wait_ge(s_e, n + 3)
                pe.wait_ge(s_pt, n + 1)
                for k in range(TB):
                    mm = pe.transpose(t_ps[:, k, :], probs[:, i % 2, k * P:(k + 1) * P], ident[:, :])
                mm.then_inc(s_t, 1)

            def pv(b, i):
                n = b * TB + i
                pe.wait_ge(s_pt, n + 2)
                pe.wait_ge(s_o, n + 3)
                for k in range(TB):
                    mm = pe.matmul(y_ps[i % 2][:, :], pT[:, i % 2, k, :],
                                   VP[:, bass.ds((b + i // TB) * TB + k, 1), :].rearrange("p a d -> p (a d)"),
                                   start=(k == 0), stop=(k == TB - 1))
                mm.then_inc(s_y, 1)

            for i in range(QK_LEAD):
                scores(0, i)
            transpose(0, 0)
            pv(0, 0)

            def body(b, last):
                for i in range(TB):
                    if ahead(last, i + PV_LEAD):
                        transpose(b, i + PV_LEAD)
                    if ahead(last, i + QK_LEAD):
                        scores(b, i + QK_LEAD)
                    if ahead(last, i + PV_LEAD):
                        pv(b, i + PV_LEAD)

            batches(pe, body)

        @block.scalar
        def _(act):
            def scale(b, i):
                n = b * TB + i
                act.wait_ge(s_s, n + 5)
                act.wait_ge(s_f, 3 * n + 3)
                act.activation(x[:, i % 4, :], s_ps[i % 2][:, :], ACT.Copy, scale=SCALE).then_inc(s_x, 1)

            def exps(b, i):
                n = b * TB + i
                act.wait_ge(s_f, 3 * (n + 5))
                act.wait_ge(s_t, n + 1)
                act.wait_ge(s_o, n + 1)
                act.activation(probs[:, i % 2, :], f[:, i % 2, :], ACT.Exp, bias=neg[:, i % 2:i % 2 + 1], scale=UNIT,
                               accum_out=total[:, i % 4:i % 4 + 1]).then_inc(s_e, 1)

            def keep_t(b, i):
                n = b * TB + i
                act.wait_ge(s_t, n + 3)
                act.wait_ge(s_y, n + 1)
                act.activation(pT[:, i % 2, :, :], t_ps[:, :, :], ACT.Copy).then_inc(s_pt, 1)

            act.sem_inc(s_x, 2)
            act.sem_inc(s_e, 2)
            for i in range(QK_LEAD):
                scale(0, i)
            exps(0, 0)
            keep_t(0, 0)
            exps(0, 1)

            def body(b, last):
                for i in range(TB):
                    if ahead(last, i + PV_LEAD):
                        keep_t(b, i + PV_LEAD)
                    if ahead(last, i + EXP_LEAD):
                        exps(b, i + EXP_LEAD)
                    if ahead(last, i + QK_LEAD):
                        scale(b, i + QK_LEAD)

            batches(act, body)

        @block.gpsimd
        def _(pool):
            def pair_terms(b, i):
                n = b * TB + i
                pool.wait_ge(s_term, 4 * n + 4)
                pool.wait_ge(s_f, 3 * (n + 3))
                pool.tensor_tensor(pairs[:, i % 2, :, :], terms[:, i % 2, 0:2, :], terms[:, i % 2, 2:4, :],
                                   ALU.add).then_inc(s_pair, 1)
                pool.wait_ge(s_pair, n + 3)

            pool.sem_inc(s_pair, 2)
            for i in range(TERM_LEAD):
                pair_terms(0, i)

            def body(b, last):
                for i in range(TB):
                    if ahead(last, i + TERM_LEAD):
                        pair_terms(b, i + TERM_LEAD)

            batches(pool, body)

        @block.vector
        def _(dve):
            def band_terms(b, i):
                n = b * TB + i
                dve.wait_ge(s_x, n + 3)
                dve.wait_ge(s_pair, n + 1)
                for k, (p, compare, op, value) in enumerate(TERMS):
                    dve.tensor_scalar(terms[:, i % 2, k, :], x[:, i % 4, :], BAND[p], value, compare, op).then_inc(s_term, 1)

            def band(b, i):
                n = b * TB + i
                dve.wait_ge(s_pair, n + 3)
                k = 3 * n + 12
                dve.wait_ge(s_f, k)
                dve.tensor_tensor(factor[:, :], pairs[:, i % 2, 0, :], pairs[:, i % 2, 1, :], ALU.add).then_inc(s_f, 1)
                dve.wait_ge(s_f, k + 1)
                dve.wait_ge(s_e, n + 1)
                dve.sem_inc(apart["dve"], 1)
                dve.tensor_tensor_reduce(out=f[:, i % 2, :], in0=factor[:, :], in1=x[:, i % 4, :], scale=1.0, scalar=LOW,
                                         op0=ALU.mult, op1=ALU.max, accum_out=top[:, i % 2:i % 2 + 1]).then_inc(s_f, 1)
                dve.wait_ge(s_f, k + 2)
                dve.tensor_scalar(neg[:, i % 2:i % 2 + 1], top[:, i % 2:i % 2 + 1], -UNIT, None, ALU.mult).then_inc(s_f, 1)

            def finish(b, i):
                n = b * TB + i
                dve.wait_ge(s_y, n + 3)
                dve.wait_ge(s_o, n + 3)
                dve.reciprocal(inv[:, i % 2:i % 2 + 1], total[:, i % 4:i % 4 + 1]).then_inc(s_i, 1)
                dve.wait_ge(s_i, n + 1)
                dve.scalar_tensor_tensor(out=row_tile(Y, b, i), in0=y_ps[i % 2][:, :], scalar=inv[:, i % 2:i % 2 + 1],
                                         in1=bp[:, :], op0=ALU.mult, op1=ALU.add).then_inc(s_o, 1)

            dve.sem_inc(s_s, 4)
            dve.sem_inc(s_f, 12)
            dve.sem_inc(s_t, 2)
            dve.sem_inc(s_pt, 1)
            dve.sem_inc(s_y, 2)
            dve.sem_inc(s_o, 4)
            dve.wait_ge(s_b, 16)
            band_terms(0, 0)
            for i in range(F_LEAD):
                band_terms(0, i + 1)
                band(0, i)

            def body(b, last):
                for i in range(TB):
                    if ahead(last, i + TERM_LEAD):
                        band_terms(b, i + TERM_LEAD)
                    if ahead(last, i + F_LEAD):
                        band(b, i + F_LEAD)
                    finish(b, i)

            batches(dve, body)


def ffn_inputs(nc, io, keep):
    X, Y, ident, XA = (keep[k] for k in ("X", "Y", "ident", "XA"))
    with ExitStack() as ctx:
        m = Scope(nc, ctx, "p8_")
        W = m.sb("attn_w", [P, D])
        vec = m.sb("vectors", [P, 3])
        zn, flat, xh = (m.sb(n, [P, 2, TB, D]) for n in ("zn", "flat", "xh"))
        ln = [[Moments(m, f"{k}{h}") for k in ("y", "x")] for h in range(2)]
        var2, inv2, rstd2 = (m.sb(n, [P, 2, 2, TB]) for n in ("var2", "inv2", "rstd2"))
        hT, fT = m.sb("hT", [P, 2, S]), m.sb("fT", [P, 2, S])
        t_ps = [m.ps(f"t_ps{h}", [P, S]) for h in range(2)]
        a_ps = [m.ps(f"a_ps{h}", [P, S]) for h in range(2)]

        s_w = m.sem("w_loaded")
        s_ln = MomentSems(m)
        s_in, s_rt, s_v2 = s_ln.inv, m.sem("rstd_ready"), m.sem("var2_steps")
        s_zn, s_x, s_f, s_h = m.sem("y_normed"), m.sem("x_updated"), m.sem("flat_ready"), m.sem("xh_ready")
        s_tr, s_T, s_a = m.sem("transposed"), m.sem("transposes_kept"), m.sem("attn_ready")
        s_xa = m.sem("xa_ready")
        apart = keep["apart"]
        block = ctx.enter_context(nc.Block())

        @block.sync
        def _(sp):
            sp.dma_start(W[:, :], io["attn_w"]).then_inc(s_w, 16)
            sp.dma_start(vec[:, :], io["ffn_vectors"]).then_inc(s_w, 16)

        @block.vector
        def _(dve):
            dve.sem_inc(s_xa, 2)
            with dve.Fori(0, B // 2) as p:
                for h in range(2):
                    moments(dve, s_ln, apart["dve"], ln[h][0], 4 * p + h, lambda t: row_tile(Y, 2 * p + h, t))
                for h in range(2):
                    dve.wait_ge(s_rt, 6 * p + h + 1)
                    for t in range(TB):
                        dve.tensor_scalar(zn[:, h, t, :], row_tile(Y, 2 * p + h, t), ln[h][0].mv[:, t, 0:1],
                                          ln[h][0].rstd[:, t:t + 1], ALU.subtract, ALU.mult).then_inc(s_zn, 1)
                for h in range(2):
                    dve.wait_ge(s_x, 2 * p + h + 1)
                    dve.sem_inc(apart["dve"], 1)
                    moments(dve, s_ln, apart["dve"], ln[h][1], 4 * p + 2 + h, lambda t: row_tile(X, 2 * p + h, t))
                    dve.wait_ge(s_in, 6 * p + 3 + 2 * h)
                    dve.tensor_tensor(var2[:, h, 0, :], ln[h][1].mv[:, :, 1], ln[h][1].inv[:, :], ALU.mult).then_inc(s_v2, 1)
                    dve.wait_ge(s_v2, 4 * p + 2 * h + 1)
                    dve.tensor_scalar(var2[:, h, 1, :], var2[:, h, 0, :], EPS, None, ALU.add).then_inc(s_v2, 1)
                    dve.wait_ge(s_v2, 4 * p + 2 * h + 2)
                    dve.reciprocal(inv2[:, h, 0, :], var2[:, h, 1, :]).then_inc(s_in, 1)
                for h in range(2):
                    dve.wait_ge(s_rt, 6 * p + 3 + 2 * h)
                    for t in range(TB):
                        dve.tensor_scalar(flat[:, h, t, :], row_tile(X, 2 * p + h, t), ln[h][1].mv[:, t, 0:1],
                                          ln[h][1].rstd[:, t:t + 1], ALU.subtract, ALU.mult).then_inc(s_f, 1)
                for h in range(2):
                    dve.wait_ge(s_a, 2 * p + h + 1)
                    dve.tensor_tensor(XA[:, bass.ds((2 * p + h) * S, S)], a_ps[h][:, :], fT[:, h, :], ALU.add).then_inc(s_xa, 1)
                dve.wait_ge(s_xa, 2 * p + 4)

        @block.scalar
        def _(act):
            act.wait_ge(s_w, 32)
            with act.Fori(0, B // 2) as p:
                for h in range(2):
                    act.wait_ge(s_in, 6 * p + h + 1)
                    act.activation(ln[h][0].rstd[:, :], ln[h][0].inv[:, :], ACT.Sqrt).then_inc(s_rt, 1)
                for h in range(2):
                    act.wait_ge(s_in, 6 * p + 3 + 2 * h)
                    act.activation(ln[h][1].rstd[:, :], ln[h][1].inv[:, :], ACT.Sqrt).then_inc(s_rt, 1)
                    act.wait_ge(s_in, 6 * p + 4 + 2 * h)
                    act.activation(rstd2[:, h, 0, :], inv2[:, h, 0, :], ACT.Sqrt).then_inc(s_rt, 1)
                for h in range(2):
                    act.wait_ge(s_tr, 4 * p + 1 + h)
                    act.activation(fT[:, h, :], t_ps[h][:, :], ACT.Identity, bias=vec[:, 2:3]).then_inc(s_T, 1)
                for h in range(2):
                    act.wait_ge(s_tr, 4 * p + 3 + h)
                    act.activation(hT[:, h, :], t_ps[h][:, :], ACT.Identity, scale=vec[:, 0:1], bias=vec[:, 1:2]).then_inc(s_T, 1)

        @block.gpsimd
        def _(pool):
            with pool.Fori(0, B // 2) as p:
                for h in range(2):
                    pool.wait_ge(s_zn, TB * (2 * p + h + 1))
                    rows = X[:, bass.ds((2 * p + h) * TB, TB), :]
                    pool.tensor_tensor(rows, rows, zn[:, h, :, :], ALU.add).then_inc(s_x, 1)
                    pool.wait_ge(s_x, 2 * p + h + 1)
                for h in range(2):
                    pool.wait_ge(s_f, TB * (2 * p + h + 1))
                    pool.wait_ge(s_rt, 6 * p + 4 + 2 * h)
                    pool.tensor_tensor(xh[:, h, :, :], flat[:, h, :, :],
                                       rstd2[:, h, 0, :].unsqueeze(2).broadcast_to([P, TB, D]), ALU.mult).then_inc(s_h, 1)
                    pool.wait_ge(s_h, 2 * p + h + 1)

        @block.tensor
        def _(pe):
            pe.wait_ge(s_w, 32)
            with pe.Fori(0, B // 2) as p:
                for h in range(2):
                    pe.wait_ge(s_f, TB * (2 * p + h + 1))
                    for t in range(TB):
                        mm = pe.transpose(t_ps[h][:, t * P:(t + 1) * P], flat[:, h, t, :], ident[:, :])
                    mm.then_inc(s_tr, 1)
                for h in range(2):
                    pe.wait_ge(s_h, 2 * p + h + 1)
                    pe.wait_ge(s_T, 4 * p + 1 + h)
                    for t in range(TB):
                        mm = pe.transpose(t_ps[h][:, t * P:(t + 1) * P], xh[:, h, t, :], ident[:, :])
                    mm.then_inc(s_tr, 1)
                for h in range(2):
                    pe.wait_ge(s_T, 4 * p + 3 + h)
                    pe.wait_ge(s_xa, 2 * p + h + 1)
                    for c in range(2):
                        mm = pe.matmul(a_ps[h][:, c * 512:(c + 1) * 512], W[:, :], hT[:, h, c * 512:(c + 1) * 512],
                                       start=True, stop=True)
                    mm.then_inc(s_a, 1)


E1 = 8
CH = B * S // (2 * E1)
CT = CH // P


def static_experts(nc, io, keep):
    XA, Z = keep["XA"], keep["Z"]
    with ExitStack() as ctx:
        m = Scope(nc, ctx, "p9_")
        W1 = m.sb("w1", [P, E1, F0])
        W2 = m.sb("w2", [P, E1, FC, D])
        Wn = m.sb("next_w", [P, D])
        b12 = m.sb("b1_b2", [P, E1, FC + 1])
        bn = m.sb("next_b", [P, D])
        hT = m.sb("hT", [P, 2, FC, CH])
        eoT = m.sb("eoT", [P, 2, CH])
        pre = m.sb("pre", [P, 2, CT, D])
        h_ps = [m.ps(f"h_ps{r}", [P, FC, CH]) for r in range(2)]
        e_ps = [m.ps(f"e_ps{r}", [P, CH]) for r in range(2)]
        n_ps = [m.ps(f"n_ps{r}", [P, CT, D]) for r in range(2)]

        s_w = m.sem("w_loaded")
        s_h = m.sem("h_ready")
        s_g = m.sem("h_gelu")
        s_eo = m.sem("eo_ready")
        s_ek = m.sem("eo_kept")
        s_n = m.sem("next_ready")
        s_nb = m.sem("next_biased")
        s_z = m.sem("z_ready")
        apart = keep["apart"]
        block = ctx.enter_context(nc.Block())

        def micro_batches(eng, body):
            with eng.Fori(0, 1) as k:
                body(k, False)
            body(1, True)

        @block.sync
        def _(sp):
            for dst, src in ((W1[:, :, :], "f_w1"), (W2[:, :, :, :], "f_w2"), (Wn[:, :], "next_w"), (b12[:, :, :], "f_b12")):
                sp.dma_start(dst, io[src]).then_inc(s_w, 16)
            sp.dma_start(bn[:, :], io["next_b"].rearrange("(a d) -> a d", a=1).broadcast_to([P, D])).then_inc(s_w, 16)

        @block.tensor
        def _(pe):
            def first(k, i):
                n, e = k * E1 + i, i % E1
                pe.wait_ge(s_g, FC * n + FC)
                for c in range(FC):
                    mm = pe.matmul(h_ps[i % 2][:, c, :], W1[:, e, c * P:(c + 1) * P], XA[:, bass.ds(n * CH, CH)],
                                   start=True, stop=True)
                mm.then_inc(s_h, 1)

            def second(k, i):
                n, e = k * E1 + i, i % E1
                pe.wait_ge(s_g, FC * n + 3 * FC)
                pe.wait_ge(s_ek, n + 1)
                for c in range(FC):
                    mm = pe.matmul(e_ps[i % 2][:, :], W2[:, e, c, :], hT[:, i % 2, c, :], start=(c == 0), stop=(c == FC - 1))
                mm.then_inc(s_eo, 1)

            def third(k, i):
                n = k * E1 + i
                pe.wait_ge(s_ek, n + 3)
                pe.wait_ge(s_nb, n + 1)
                for t in range(CT):
                    mm = pe.matmul(n_ps[i % 2][:, t, :], eoT[:, i % 2, t * P:(t + 1) * P], Wn[:, :], start=True, stop=True)
                mm.then_inc(s_n, 1)

            pe.wait_ge(s_w, 80)
            first(0, 0)
            first(0, 1)
            second(0, 0)

            def body(k, last):
                for i in range(E1):
                    if not (last and i + 2 >= E1):
                        first(k, i + 2)
                    if not (last and i + 1 >= E1):
                        second(k, i + 1)
                    third(k, i)

            micro_batches(pe, body)

        @block.scalar
        def _(act):
            def gelu(k, i):
                n, e = k * E1 + i, i % E1
                act.wait_ge(s_eo, n + 1)
                act.wait_ge(s_h, n + 1)
                for c in range(FC):
                    act.activation(hT[:, i % 2, c, :], h_ps[i % 2][:, c, :], ACT.Gelu, bias=b12[:, e, c:c + 1]).then_inc(s_g, 1)

            act.sem_inc(s_g, 2 * FC)
            act.sem_inc(s_z, 2)
            act.wait_ge(s_w, 80)
            gelu(0, 0)
            gelu(0, 1)

            def body(k, last):
                for i in range(E1):
                    if not (last and i + 2 >= E1):
                        gelu(k, i + 2)
                    n = k * E1 + i
                    act.wait_ge(s_nb, n + 3)
                    act.sem_inc(apart["act"], 1)
                    act.activation(Z[:, bass.ds(n * CT, CT), :], pre[:, i % 2, :, :], ACT.Gelu).then_inc(s_z, 1)

            micro_batches(act, body)

        @block.vector
        def _(dve):
            def expert_bias(k, i):
                n, e = k * E1 + i, i % E1
                dve.wait_ge(s_n, n + 1)
                dve.wait_ge(s_eo, n + 3)
                dve.tensor_scalar(eoT[:, i % 2, :], e_ps[i % 2][:, :], b12[:, e, FC:FC + 1], None, ALU.add).then_inc(s_ek, 1)

            dve.sem_inc(s_eo, 2)
            dve.sem_inc(s_ek, 2)
            dve.sem_inc(s_n, 2)
            dve.sem_inc(s_nb, 2)
            dve.wait_ge(s_w, 80)
            expert_bias(0, 0)

            def body(k, last):
                for i in range(E1):
                    if not (last and i + 1 >= E1):
                        expert_bias(k, i + 1)
                    n = k * E1 + i
                    dve.wait_ge(s_z, n + 1)
                    dve.wait_ge(s_n, n + 3)
                    dve.tensor_tensor(pre[:, i % 2, :, :], n_ps[i % 2][:, :, :],
                                      bn[:, :].unsqueeze(1).broadcast_to([P, CT, D]), ALU.add).then_inc(s_nb, 1)

            micro_batches(dve, body)


def finish_rows(nc, io, keep):
    X, Z = keep["X"], keep["Z"]
    with ExitStack() as ctx:
        m = Scope(nc, ctx, "p10_")
        zn = m.sb("zn", [P, 2, TB, D])
        ln = [Moments(m, f"z{h}") for h in range(2)]
        s_ln = MomentSems(m)
        s_rt, s_zn = m.sem("rstd_ready"), m.sem("z_normed")
        s_x, s_out = m.sem("x_updated"), m.sem("x_stored")
        apart = keep["apart"]["dve"]
        block = ctx.enter_context(nc.Block())

        @block.vector
        def _(dve):
            with dve.Fori(0, B // 2) as p:
                for h in range(2):
                    moments(dve, s_ln, apart, ln[h], 2 * p + h, lambda t: row_tile(Z, 2 * p + h, t))
                for h in range(2):
                    dve.wait_ge(s_rt, 2 * p + h + 1)
                    for t in range(TB):
                        dve.tensor_scalar(zn[:, h, t, :], row_tile(Z, 2 * p + h, t), ln[h].mv[:, t, 0:1],
                                          ln[h].rstd[:, t:t + 1], ALU.subtract, ALU.mult).then_inc(s_zn, 1)
                dve.wait_ge(s_x, 2 * p + 2)

        @block.scalar
        def _(act):
            with act.Fori(0, B // 2) as p:
                for h in range(2):
                    act.wait_ge(s_ln.inv, 2 * p + h + 1)
                    act.activation(ln[h].rstd[:, :], ln[h].inv[:, :], ACT.Sqrt).then_inc(s_rt, 1)

        @block.gpsimd
        def _(pool):
            with pool.Fori(0, B // 2) as p:
                for h in range(2):
                    pool.wait_ge(s_zn, TB * (2 * p + h + 1))
                    rows = X[:, bass.ds((2 * p + h) * TB, TB), :]
                    pool.tensor_tensor(rows, rows, zn[:, h, :, :], ALU.add).then_inc(s_x, 1)
                    pool.wait_ge(s_x, 2 * p + h + 1)

        @block.sync
        def _(sp):
            with sp.Fori(0, B) as b:
                sp.wait_ge(s_x, b + 1)
                sp.dma_start(io["out"][bass.ds(b, 1), :, :].rearrange("b (t p) d -> p (b t) d", p=P),
                             X[:, bass.ds(b * TB, TB), :]).then_inc(s_out, 16)
            sp.wait_ge(s_out, 16 * B)


def build(nc, io):
    with ExitStack() as ctx:
        m = Scope(nc, ctx)
        apart = {e: m.sem(f"{e}_apart") for e in ("act", "dve", "pool")}
        keep = {"apart": apart, "X": m.sb("X", [P, T, D]), "ident": m.sb("ident", [P, P])}
        with ExitStack() as attn:
            a = Scope(nc, attn)
            keep["tri"] = a.sb("tri", [P, 4 * P])
            keep["Q4"] = a.sb("q_operands", [P, G, GH, S], BF16)
            keep["K4"] = a.sb("k_operands", [P, G, GH, S], BF16)
            keep["Vg"] = a.sb("v_groups", [P, B * G, TB, GH * HD])
            keep["Vone"] = a.sb("v_with_ones", [P, 2, TB, GH, 32])
            project_heads(nc, io, keep)
            causal_attention(nc, io, keep)
        for name in ("qT", "kT"):
            keep[name] = m.sb(name, [P, B * S])
        keep["VP"] = m.sb("VP", [P, T, D])
        with ExitStack() as moe:
            a = Scope(nc, moe)
            for name, shape, dt in (("XN", [P, T, D], F32), ("XH", [P, T, D], F32), ("aff", [P, T, E0], F32),
                                    ("gate", [P, T], F32), ("pos", [P, T], U32), ("tile_expert", [P, MAXTILES], I32)):
                keep[name] = a.sb(name, shape, dt)
            merge_heads(nc, io, keep)
            route(nc, io, keep)
            experts(nc, io, keep)
            combine_and_project(nc, io, keep)
        keep["Y"] = m.sb("Y", [P, T, D])
        banded_attention(nc, io, keep)
        keep["XA"] = m.sb("XA", [P, B * S])
        ffn_inputs(nc, io, keep)
        keep["Z"] = keep["Y"]
        static_experts(nc, io, keep)
        finish_rows(nc, io, keep)


def kernel(**inputs):
    import concourse.bacc as bacc
    from concourse.bass_utils import run_bass_kernel_spmd

    order = np.arange(D).reshape(G, GH, HD).transpose(0, 2, 1).reshape(-1)
    swap = order ^ 1
    turned = [np.asarray(inputs[f"L0_attn_W{k}"]).T for k in "qkvo"]
    Wq, Wk, Wv, Wo = turned
    arrays = {
        "x": np.asarray(inputs["L0_attn_x"]),
        "l0_w": np.stack([Wq[:, order], Wq[:, swap], Wk[:, order], Wk[:, swap], Wv, Wo], axis=1),
    }
    A = {k: np.asarray(v) for k, v in inputs.items()}
    per_row = lambda w: w.reshape(E0, -1, P).transpose(2, 0, 1)
    arrays["centroids"] = A["L0_ffn_centroids"].T
    arrays["w1"] = A["L0_ffn_w1"].transpose(2, 0, 1)
    arrays["w2"] = A["L0_ffn_w2"].transpose(2, 0, 1).reshape(FC, P, E0, D).transpose(1, 2, 0, 3)
    arrays["small"] = np.concatenate([per_row(A["L0_ffn_ln_g"]), per_row(A["L0_ffn_ln_b"]), per_row(A["L0_ffn_b1"])], -1)
    arrays["b2"] = A["L0_ffn_b2"]
    qkv = A["L1_attn_W_qkv"]
    arrays["l1_w"] = np.stack([qkv[:, 0:D], qkv[:, D:2 * D], qkv[:, 2 * D:], A["L1_attn_W_proj"]], 1)
    arrays["b_qkv"] = A["L1_attn_b_qkv"].reshape(3, D).T
    arrays["b_proj"] = A["L1_attn_b_proj"]
    arrays["attn_w"] = A["L1_ffn_attn_w"].T
    arrays["ffn_vectors"] = np.stack([A["L1_ffn_ln_scale"], A["L1_ffn_ln_bias"], A["L1_ffn_attn_b"]], 1)
    arrays["f_w1"] = A["L1_ffn_w1"].transpose(1, 0, 2)
    arrays["f_w2"] = A["L1_ffn_w2"].reshape(E1, FC, P, D).transpose(2, 0, 1, 3)
    arrays["f_b12"] = np.concatenate([per_row(A["L1_ffn_b1"]), per_row(A["L1_ffn_b2"])], -1)
    arrays["next_w"] = A["L1_ffn_next_w"].T
    arrays["next_b"] = A["L1_ffn_next_b"]
    freq = (1.0 / 10000.0 ** (np.arange(0, HD, 2, dtype=np.float32) / HD)).astype(np.float32)
    angle = np.outer(np.arange(S, dtype=np.float32), freq)
    angle = np.concatenate([angle, angle], -1).T
    sign = np.where(np.arange(HD) % 2 == 0, -1.0, 1.0).astype(np.float32)[:, None]
    arrays["rope"] = np.stack([np.tile(np.cos(angle), (H, 1))[order], np.tile(np.sin(angle) * sign, (H, 1))[order]], 1).astype(np.float32)

    nc = bacc.Bacc("TRN2", target_bir_lowering=False, num_devices=1)
    io, feed = {}, {}
    for name, a in arrays.items():
        feed["in_" + name] = np.ascontiguousarray(a)
        io[name] = nc.dram_tensor("in_" + name, a.shape, mybir.dt.from_np(a.dtype), kind="ExternalInput").ap()
    io["q_parts"] = nc.dram_tensor("q_parts", (3, B, D, S), BF16, kind="Internal").ap()
    io["k_parts"] = nc.dram_tensor("k_parts", (3, B, D, S), BF16, kind="Internal").ap()
    io["heads_out"] = nc.dram_tensor("heads_out", (B * G, P, S), F32, kind="Internal").ap()
    io["sorted_in"] = nc.dram_tensor("sorted_in", (MAXTILES * P, D), F32, kind="Internal").ap()
    io["sorted_out"] = nc.dram_tensor("sorted_out", (MAXTILES * P, D), F32, kind="Internal").ap()
    io["out"] = nc.dram_tensor("out_0", (B, S, D), F32, kind="ExternalOutput").ap()
    build(nc, io)
    return run_bass_kernel_spmd(nc, [feed], core_ids=[0]).results[0]["out_0"]
```

```python
from contextlib import ExitStack

import concourse.bass as bass
import numpy as np
from concourse import mybir

P = 128
D = 128
B, S = 4, 1024
TB = S // P
T = B * TB
H, HD = 16, 8
GH = 4
G = H // GH
E0, F0 = 8, 512
FC = F0 // P
EPS = 1e-5
SCALE = HD ** -0.5
LOW = -3.0e38

F32 = mybir.dt.float32
BF16 = mybir.dt.bfloat16
I32 = mybir.dt.int32
U32 = mybir.dt.uint32
ALU = mybir.AluOpType
ACT = mybir.ActivationFunctionType
AX = mybir.AxisListType


class Scope:

    def __init__(self, nc, ctx, phase=""):
        self.nc, self.ctx, self.phase = nc, ctx, phase

    def sb(self, name, shape, dt=F32):
        return self.ctx.enter_context(self.nc.sbuf_tensor(self.phase + name, shape, dt))

    def ps(self, name, shape, dt=F32):
        return self.ctx.enter_context(self.nc.psum_tensor(self.phase + name, shape, dt))

    def sem(self, name):
        return self.ctx.enter_context(self.nc.semaphore(self.phase + name))


class Moments:

    def __init__(self, m, name):
        self.stats, self.mv = m.sb(name + "_stats", [P, TB, 6]), m.sb(name + "_mv", [P, TB, 2])
        self.var, self.inv, self.rstd = (m.sb(f"{name}_{k}", [P, TB]) for k in ("var", "inv", "rstd"))


class MomentSems:

    def __init__(self, m):
        self.steps, self.inv = m.sem("moment_steps"), m.sem("inverse_variance_ready")


def moments(dve, s, apart, ln, n, rows):
    base = n * (2 * TB + 1)
    for t in range(TB):
        dve.bn_stats(ln.stats[:, t, :], rows(t)).then_inc(s.steps, 1)
    dve.wait_ge(s.steps, base + TB)
    dve.sem_inc(apart, 1)
    for t in range(TB):
        dve.bn_aggr(ln.mv[:, t, :], ln.stats[:, t, :]).then_inc(s.steps, 1)
    dve.wait_ge(s.steps, base + 2 * TB)
    dve.tensor_scalar(ln.var[:, :], ln.mv[:, :, 1], EPS, None, ALU.add).then_inc(s.steps, 1)
    dve.wait_ge(s.steps, base + 2 * TB + 1)
    dve.reciprocal(ln.inv[:, :], ln.var[:, :]).then_inc(s.inv, 1)


def row_tile(A, b, t):
    return A[:, bass.ds(b * TB + t, 1), :].rearrange("p a d -> p (a d)")


def pairs(eng, body):
    with eng.Fori(0, B // 2 - 1) as p:
        body(p, False)
    body(B // 2 - 1, True)


def load_operands(sp, io, keep, b, g):
    rows = slice(32 * g, 32 * g + 32)
    for i in range(3):
        for dst, src, parts in ((keep["Q4"], io["q_parts"], [i, i, i]), (keep["K4"], io["k_parts"], [0, 1, 2])):
            src = src[parts[0]:parts[0] + 1] if parts[0] == parts[2] else src
            src = src[:, bass.ds(b, 1), rows, :].rearrange("j b (d h) s -> (j b) d (h s)", h=GH).broadcast_to([3, HD, GH * S])
            sp.dma_start(dst[24 * i:24 * i + 24, g, :, :].rearrange("p h s -> p (h s)"), src
                         ).then_inc(keep["operands_loaded"][g], 16)


OPS = 6 * 16


def project_heads(nc, io, keep):
    X, ident, Q4, K4, Vg = keep["X"], keep["ident"], keep["Q4"], keep["K4"], keep["Vg"]
    tri, Vone = keep["tri"], keep["Vone"]
    with ExitStack() as ctx:
        m = Scope(nc, ctx, "p1_")
        W = m.sb("l0_w", [P, 5, D])
        rope = m.sb("rope", [P, 2, S])
        pads = m.sb("pads", [P, 2, S], BF16)
        ln = [Moments(m, f"x{h}") for h in range(2)]
        xn = m.sb("xn", [P, 2, TB, D])
        xnT = m.sb("xnT", [P, 2, S])
        part_c = m.sb("part_c", [P, 2, S])
        part_s = m.sb("part_s", [P, 2, S])
        rot = m.sb("rot", [P, 2, S])
        rest = m.sb("rest", [P, 2, S])
        split = m.sb("split", [P, 2, 2, 3, S], BF16)
        bank = [m.ps(f"proj{i}", [P, S]) for i in range(4)]

        s_x, s_w = [m.sem(f"x_loaded{b}") for b in range(B)], m.sem("w_loaded")
        s_c = m.sem("constants_made")
        s_pad = m.sem("pads_stored")
        s_ln = MomentSems(m)
        s_rt, s_xn = m.sem("rstd_ready"), m.sem("xn_ready")
        s_tr = m.sem("xn_transposed")
        s_xnT = m.sem("xnT_ready")
        s_p = m.sem("projected")
        s_r = m.sem("rotary_products")
        s_v = m.sem("v_projected")
        s_vk = m.sem("v_kept")
        s_rot = m.sem("rotated")
        s_p1, s_p2, s_p3 = m.sem("part1_done"), m.sem("part2_done"), m.sem("part3_done")
        s_r1 = m.sem("rest_done")
        s_out = [m.sem(f"parts_stored{h}") for h in range(2)]
        apart = keep["apart"]
        block = ctx.enter_context(nc.Block())
        assert B == 4

        @block.sync
        def _(sp):
            rows = io["x"].rearrange("b (t p) d -> b p t d", p=P)
            for b in range(B):
                sp.dma_start(X[:, b * TB:(b + 1) * TB, :], rows[b]).then_inc(s_x[b], 16)
                if b == 1:
                    sp.dma_start(W[:, :, :], io["l0_w"][:, 0:5, :]).then_inc(s_w, 16)
                    sp.dma_start(rope[:, :, :], io["rope"]).then_inc(s_w, 16)
            sp.wait_ge(s_c, 6)
            for w, dst in enumerate((Q4, K4)):
                sp.dma_start(dst[9 * HD:P, :, :, :].rearrange("p g h s -> p (g h) s"),
                             pads[9 * HD:P, w, :].unsqueeze(1).broadcast_to([P - 9 * HD, H, S])).then_inc(s_pad, 16)
            for h in range(2):
                sp.sem_inc(s_out[h], 32)

            def body(p, last):
                if last:
                    sp.wait_ge(s_out[0], 64)
                    for g in range(G):
                        load_operands(sp, io, keep, 0, g)
                for h in range(2):
                    b = 2 * p + h
                    for w, dst in enumerate(("q_parts", "k_parts")):
                        sp.wait_ge(s_p3, 2 * b + w + 1)
                        sp.dma_start(io[dst][:, bass.ds(b, 1), :, :].rearrange("i b r s -> r (b i) s"),
                                     split[:, h, w, :, :]).then_inc(s_out[h], 16)

            pairs(sp, body)
            sp.wait_ge(s_pad, 32)
            for h in range(2):
                sp.wait_ge(s_out[h], 32 * (B // 2) + 32)

        @block.gpsimd
        def _(pool):
            def done(instruction, k):
                instruction.then_inc(s_c, 1)
                pool.wait_ge(s_c, k)

            done(pool.memset(ident[:, :], 0.0), 1)
            done(pool.affine_select(out=ident[:, :], in_=ident[:, :], compare_op=ALU.not_equal, fill=1.0, base=0,
                                    pattern=[[-1, P]], channel_multiplier=1), 2)
            done(pool.memset(tri[:, :], 0.0), 3)
            done(pool.affine_select(out=tri[:, 3 * P:4 * P], in_=tri[:, 3 * P:4 * P], compare_op=ALU.is_ge, fill=LOW,
                                    base=0, pattern=[[-1, P]], channel_multiplier=1), 4)
            done(pool.memset(pads[:, :, :].bitcast(F32), 0.0), 5)
            done(pool.memset(pads[96:99, 1, :], 1.0), 6)
            done(pool.memset(Vone[:, 0, :, :, :], 0.0), 7)
            done(pool.memset(Vone[:, 1, :, :, :], 0.0), 8)
            done(pool.memset(Vone[:, :, :, :, HD:HD + 1], 1.0), 9)
            with pool.Fori(0, B // 2) as p:
                for h in range(2):
                    for w in range(2):
                        n = 4 * p + 2 * h + w
                        pool.wait_ge(s_rot, n + 1)
                        pool.wait_ge(s_p1, n + 1)
                        pool.tensor_tensor(rest[:, w, :], rot[:, w, :], split[:, h, w, 0, :], ALU.subtract).then_inc(s_r1, 1)
                        pool.wait_ge(s_r1, n + 3)
                        pool.wait_ge(s_p2, n + 1)
                        pool.tensor_tensor(split[:, h, w, 2, :], rest[:, w, :], split[:, h, w, 1, :], ALU.subtract).then_inc(s_p3, 1)
                        pool.wait_ge(s_p3, n + 1)

        @block.vector
        def _(dve):
            dve.sem_inc(s_r, 4)
            def pair(p, x_loaded):
                for h in range(2):
                    dve.wait_ge(x_loaded[h], 16)
                    moments(dve, s_ln, apart["dve"], ln[h], 2 * p + h, lambda t: row_tile(X, 2 * p + h, t))
                for h in range(2):
                    dve.wait_ge(s_rt, 2 * p + h + 1)
                    dve.wait_ge(s_tr, 2 * p + h + 1)
                    for t in range(TB):
                        dve.tensor_scalar(xn[:, h, t, :], row_tile(X, 2 * p + h, t), ln[h].mv[:, t, 0:1],
                                          ln[h].rstd[:, t:t + 1], ALU.subtract, ALU.mult).then_inc(s_xn, 1)
                dve.wait_ge(s_w, 32)
                for h in range(2):
                    for w in range(2):
                        n = 4 * p + 2 * h + w
                        q, swapped = bank[JOBS.index("qk"[w] + str(h)) % 4], bank[JOBS.index("QK"[w] + str(h)) % 4]
                        dve.wait_ge(s_p, 2 * n + 1)
                        dve.wait_ge(s_r1, n + 1)
                        dve.tensor_tensor(part_c[:, w, :], q[:, :], rope[:, 0, :], ALU.mult).then_inc(s_r, 1)
                        dve.wait_ge(s_p, 2 * n + 2)
                        dve.tensor_tensor(part_s[:, w, :], swapped[:, :], rope[:, 1, :], ALU.mult).then_inc(s_r, 1)
                        dve.wait_ge(s_r, 2 * n + 6)
                        dve.tensor_tensor(rot[:, w, :], part_c[:, w, :], part_s[:, w, :], ALU.add).then_inc(s_rot, 1)

            with dve.Fori(0, B // 2 - 1) as p:
                pair(p, s_x[0:2])
            pair(B // 2 - 1, s_x[2:4])

        @block.scalar
        def _(act):
            act.sem_inc(s_vk, 1)
            act.sem_inc(s_r1, 2)
            with act.Fori(0, B // 2) as p:
                def keep_xnT(h):
                    act.wait_ge(s_tr, 2 * p + h + 3)
                    act.activation(xnT[:, h, :], bank[JOBS.index(f"t{h}") % 4][:, :], ACT.Copy).then_inc(s_xnT, 1)

                def first_part(h, w):
                    n = 4 * p + 2 * h + w
                    act.wait_ge(s_rot, n + 1)
                    act.wait_ge(s_out[h], 32 * p + 32)
                    act.activation(split[:, h, w, 0, :], rot[:, w, :], ACT.Copy).then_inc(s_p1, 1)

                def second_part(h, w):
                    n = 4 * p + 2 * h + w
                    act.wait_ge(s_r1, n + 3)
                    act.activation(split[:, h, w, 1, :], rest[:, w, :], ACT.Copy).then_inc(s_p2, 1)

                def keep_v(h):
                    act.wait_ge(s_v, 2 * p + h + 1)
                    act.sem_inc(apart["act"], 1)
                    act.activation(Vg[:, bass.ds((2 * p + h) * G, G), :, :],
                                   bank[JOBS.index(f"v{h}") % 4][:, :].rearrange("p (t g r) -> p g t r", t=TB, g=G),
                                   ACT.Copy).then_inc(s_vk, 1)

                for h in range(2):
                    act.wait_ge(s_ln.inv, 2 * p + h + 1)
                    act.activation(ln[h].rstd[:, :], ln[h].inv[:, :], ACT.Sqrt).then_inc(s_rt, 1)
                keep_xnT(0)
                first_part(0, 0)
                keep_xnT(1)
                second_part(0, 0)
                keep_v(0)
                first_part(0, 1)
                second_part(0, 1)
                first_part(1, 0)
                second_part(1, 0)
                keep_v(1)
                first_part(1, 1)
                second_part(1, 1)

        @block.tensor
        def _(pe):
            pe.sem_inc(s_tr, 2)
            pe.wait_ge(s_c, 2)
            pe.wait_ge(s_w, 32)
            with pe.Fori(0, B // 2) as p:
                def turned(h):
                    out = bank[JOBS.index(f"t{h}") % 4]
                    pe.wait_ge(s_xn, TB * (2 * p + h + 1))
                    for t in range(TB):
                        mm = pe.transpose(out[:, t * P:(t + 1) * P], xn[:, h, t, :], ident[:, :])
                    mm.then_inc(s_tr, 1)

                def product(what, h):
                    out, j = bank[JOBS.index(f"{what}{h}") % 4], "qQkK".index(what)
                    for c in range(2):
                        mm = pe.matmul(out[:, c * 512:(c + 1) * 512], W[:, j, :], xnT[:, h, c * 512:(c + 1) * 512],
                                       start=True, stop=True)
                    mm.then_inc(s_p, 1)

                def values(h):
                    out = bank[JOBS.index(f"v{h}") % 4]
                    for t in range(TB):
                        mm = pe.matmul(out[:, t * P:(t + 1) * P], xnT[:, h, t * P:(t + 1) * P], W[:, 4, :],
                                       start=True, stop=True)
                    mm.then_inc(s_v, 1)

                pe.wait_ge(s_r, 8 * p + 2)
                turned(0)
                pe.wait_ge(s_xnT, 2 * p + 1)
                pe.wait_ge(s_r, 8 * p + 3)
                product("q", 0)
                pe.wait_ge(s_r, 8 * p + 4)
                product("Q", 0)
                pe.wait_ge(s_vk, 2 * p + 1)
                product("k", 0)
                product("K", 0)
                pe.wait_ge(s_r, 8 * p + 5)
                turned(1)
                pe.wait_ge(s_r, 8 * p + 6)
                values(0)
                pe.wait_ge(s_xnT, 2 * p + 2)
                pe.wait_ge(s_r, 8 * p + 7)
                product("q", 1)
                pe.wait_ge(s_r, 8 * p + 8)
                product("Q", 1)
                product("k", 1)
                pe.wait_ge(s_vk, 2 * p + 2)
                product("K", 1)
                pe.wait_ge(s_r, 8 * p + 9)
                values(1)


JOBS = ["t0", "q0", "Q0", "k0", "K0", "t1", "v0", "q1", "Q1", "k1", "K1", "v1"]


STEPS = [(0, kb) for kb in range(4)] + [(1, kb) for kb in range(8)]
NS = len(STEPS)
ST_LEAD, MAX_LEAD = 2, 19
TURN = 8
MAX_STEPS = [
    [(6, 0, 512, "first"), (0, 0, 128, "only"), (7, 0, 512, "first"), (2, 0, 384, "only")],
    [(4, 0, 512, "first"), (5, 0, 512, "first"), (1, 0, 256, "only"), (5, 512, 256, "last")],
    [(3, 0, 512, "only"), (4, 512, 128, "last"), (7, 512, 512, "last"), (6, 512, 384, "last")],
]


def span(step):
    c, kb = STEPS[step]
    q0 = max(c * 512, kb * P)
    return q0, (c + 1) * 512 - q0


def softmax_sums(io, p):
    rows = io["heads_out"].rearrange("n (j r) s -> (n j) r s", j=GH)
    return rows[2 * H * p:2 * H * (p + 1), HD, :].rearrange("h (c s) -> h c s", c=2)


def inverted_sums(io, p):
    return io["inv_sums"][2 * H * p:2 * H * (p + 1), :].rearrange("h (c s) -> (h c) s", c=2)


def causal_attention(nc, io, keep):
    ident, Q4, K4, Vg, Vone, tri = (keep[k] for k in ("ident", "Q4", "K4", "Vg", "Vone", "tri"))
    NB = G * NS
    with ExitStack() as ctx:
        m = Scope(nc, ctx, "p2_")
        PT = m.sb("probs", [P, 3, GH, 512])
        rowmax = m.sb("rowmax", [P, 2, GH, TB])
        half_max = m.sb("half_max", [P, 2, GH, 4])
        negmax = m.sb("negmax", [GH * TB, P])
        max_rest = m.sb("max_rest", [GH * TB, 2, P])
        max_parts = m.sb("max_parts", [GH * TB, 3, P], BF16)
        o_sb = m.sb("o_sb", [P, 2, 512])
        sums, inv_sums = (m.sb(n, [2 * H * 2, S // 2]) for n in ("sums", "inv_sums"))
        st = [m.ps(f"st{i}", [P, 2, 512]) for i in range(2)]
        sq = [m.ps(f"sq{i}", [P, 512]) for i in range(3)]
        o_ps = m.ps("o_ps", [P, 512])
        mt = st[1][0:GH * TB, 1, 0:P]

        s_ops = keep["operands_loaded"]
        s_st, s_exp = m.sem("scores_ready"), m.sem("exps_done")
        s_diag = m.sem("diagonal_masked")
        s_pv = m.sem("pv_done")
        s_sq, s_max = m.sem("score_rows_ready"), m.sem("maxima_done")
        s_mt, s_neg = m.sem("maxima_transposed"), m.sem("maxima_negated")
        s_sp = m.sem("maxima_split_steps")
        s_row = m.sem("maxima_rows_stored")
        s_v = m.sem("v_group_ready")
        s_o = m.sem("o_evacuated")
        s_oout = [m.sem(f"o_stored{c}") for c in range(2)]
        s_sums, s_is, s_iout = m.sem("sums_loaded"), m.sem("sums_inverted"), m.sem("inverted_sums_stored")
        apart = keep["apart"]
        block = ctx.enter_context(nc.Block())

        def batches(eng, body):
            with eng.Fori(0, B - 1) as b:
                body(b, False)
            body(B - 1, True)

        @block.sync
        def _(sp):
            for c in range(2):
                sp.sem_inc(s_oout[c], 16)
            def max_rows(n, buf):
                sp.wait_ge(s_sp, 5 * n + 10)
                for i in range(3):
                    sp.dma_start(Q4[96 + i:97 + i, buf, :, :].rearrange("a h (t q) -> a (h t) q", q=P),
                                 max_parts[:, i, :]).then_inc(s_row, 16)

            def store_o(b, g, c):
                sp.wait_ge(s_o, 2 * (G * b + g) + c + 2)
                sp.dma_start(io["heads_out"][bass.ds(b * G + g, 1), :, c * 512:(c + 1) * 512].rearrange("a r s -> r (a s)"),
                             o_sb[:, c, :]).then_inc(s_oout[c], 16)

            max_rows(0, 0)

            def body(b, last):
                for g in range(G):
                    if not (last and g == G - 1):
                        max_rows(b * G + g + 1, (g + 1) % G)
                    store_o(b, g, 0)
                    if not last:
                        sp.wait_ge(s_st, 2 * NS * (b * G + g + 1))
                        load_operands(sp, io, keep, b + 1, g)
                    store_o(b, g, 1)
                    if last and g == 0:
                        for c in range(2):
                            sp.wait_ge(s_oout[c], 16 * (2 * G + 1))
                        sp.dma_start(sums[:, :], softmax_sums(io, 0)).then_inc(s_sums, 16)

            batches(sp, body)
            sp.wait_ge(s_is, 1)
            sp.dma_start(inverted_sums(io, 0), inv_sums[:, :]).then_inc(s_iout, 16)
            sp.wait_ge(s_iout, 16)
            for c in range(2):
                sp.wait_ge(s_oout[c], 16 * (B * G + 1))

        @block.tensor
        def _(pe):
            def scores(b, i, hp, last=False):
                if last and i >= NB:
                    return
                final = last and i // NS == G - 1
                g, s = i // NS % G, i % NS
                b = b + i // NB
                c, kb = STEPS[s]
                q0, w = span(s)
                if s == 0 and hp == 0:
                    pe.wait_ge(s_row, 48 * (b * G + g + 1))
                u = 2 * ((b * G + g) * NS + s) + hp
                pe.wait_ge(s_exp, u + 1)
                if s == TURN and hp == 1 and not final:
                    pe.wait_ge(s_neg, b * G + g + 3)
                for h in (0, 1):
                    mm = pe.matmul(st[hp][:, h, 0:w], K4[:, g, 2 * hp + h, kb * P:(kb + 1) * P],
                                   Q4[:, g, 2 * hp + h, q0:q0 + w], start=True, stop=True)
                mm.then_inc(s_st, 1)

            def maxima(b, i, j, last=False):
                if last and i >= NB:
                    return
                g, ms = i // NS % G, i % NS
                b = b + i // NB
                if ms == 0 and j == 0:
                    pe.wait_ge(s_ops[g], OPS * (b + 1))
                qb, k0, w, _ = MAX_STEPS[ms % 3][j]
                n = 4 * ((b * G + g) * NS + ms) + j
                pe.wait_ge(s_max, n + 1)
                pe.matmul(sq[(4 * ms + j) % 3][:, 0:w], Q4[0:96, g, ms // 3, qb * P:(qb + 1) * P],
                          K4[0:96, g, ms // 3, k0:k0 + w], start=True, stop=True).then_inc(s_sq, 1)

            def transpose_max(n, par):
                pe.wait_ge(s_max, 4 * NS * (n + 1) + 3)
                pe.wait_ge(s_neg, n + 1)
                pe.matmul(mt, rowmax[:, par, :, :].rearrange("p h t -> p (h t)"), ident[:, :],
                          is_transpose=True, start=True, stop=True).then_inc(s_mt, 1)

            def pv(b, i):
                g, s = i // NS, i % NS
                c, kb = STEPS[s]
                q0, w = span(s)
                n = b * G + g
                if s == 0:
                    pe.wait_ge(s_v, n + 1)
                if kb == 0:
                    pe.wait_ge(s_o, 2 * n + c + 1)
                if kb >= 4 * c:
                    pe.wait_ge(s_diag, TB * n + kb + 1)
                else:
                    pe.wait_ge(s_exp, 2 * (n * NS + s) + 4)
                for j in range(GH):
                    mm = pe.matmul(o_ps[32 * j:32 * j + 32, q0 - c * 512:512], Vone[:, g % 2, kb, j, :],
                                   PT[:, s % 3, j, 0:w], start=(kb == 0), stop=(kb == 4 * c + 3))
                mm.then_inc(s_pv, 1)

            for i in range(MAX_LEAD):
                for j in range(4):
                    maxima(0, i, j)
                if i == NS - 1:
                    transpose_max(0, 0)
            for i in range(ST_LEAD):
                scores(0, i, 0)
                scores(0, i, 1)

            def body(b, last):
                for i in range(NB):
                    scores(b, i + ST_LEAD, 0, last)
                    maxima(b, i + MAX_LEAD, 0, last)
                    if i % NS == TURN - ST_LEAD and not (last and i // NS == G - 1):
                        pe.wait_ge(s_exp, 2 * (b * NB + i + ST_LEAD) + 2)
                        transpose_max(b * G + i // NS + 1, (i // NS + 1) % 2)
                    maxima(b, i + MAX_LEAD, 1, last)
                    scores(b, i + ST_LEAD, 1, last)
                    maxima(b, i + MAX_LEAD, 2, last)
                    pv(b, i)
                    maxima(b, i + MAX_LEAD, 3, last)

            batches(pe, body)

        @block.vector
        def _(dve):
            def maxima(b, i):
                g, ms = i // NS % G, i % NS
                b = b + i // NB
                h = ms // 3
                n0 = 4 * ((b * G + g) * NS + ms)
                if ms == 0:
                    dve.wait_ge(s_mt, b * G + g + 1)
                for j, (qb, k0, w, how) in enumerate(MAX_STEPS[ms % 3]):
                    dve.wait_ge(s_sq, n0 + j + 1)
                    bank = sq[(4 * ms + j) % 3]
                    out = rowmax[:, g % 2, h, qb:qb + 1]
                    part = half_max[:, g % 2, h, qb - 4:qb - 3] if qb >= 4 else None
                    if how == "first":
                        dve.tensor_reduce(part, bank[:, 0:w], AX.X, ALU.max).then_inc(s_max, 1)
                        continue
                    if how == "last":
                        dve.wait_ge(s_max, n0 + j + 3)
                    dve.sem_inc(apart["dve"], 1)
                    dve.tensor_tensor_reduce(out=bank[:, 0:w], in0=bank[:, 0:w], in1=tri[:, 512 - w:512], scale=1.0,
                                             scalar=(LOW if how == "only" else part), op0=ALU.add, op1=ALU.max,
                                             accum_out=out).then_inc(s_max, 1)

            dve.sem_inc(s_max, 3)
            dve.sem_inc(s_mt, 2)
            for i in range(MAX_LEAD):
                maxima(0, i)

            def body(b, last):
                for i in range(NB):
                    if not (last and i + MAX_LEAD >= NB):
                        maxima(b, i + MAX_LEAD)

            batches(dve, body)
            dve.wait_ge(s_sums, 16)
            dve.reciprocal(inv_sums[:, :], sums[:, :]).then_inc(s_is, 1)

        @block.scalar
        def _(act):
            def exps(b, i, hp, last=False):
                if last and i >= NB:
                    return
                s = i % NS
                _, w = span(s)
                n = (b * G) * NS + i
                act.wait_ge(s_pv, n + 1)
                act.wait_ge(s_st, 2 * n + hp + 1)
                act.activation(PT[:, s % 3, 2 * hp:2 * hp + 2, 0:w], st[hp][:, :, 0:w], ACT.Exp,
                               scale=SCALE).then_inc(s_exp, 1)

            def negate(n):
                act.wait_ge(s_mt, n + 3)
                act.wait_ge(s_sp, 5 * n + 5)
                act.activation(negmax[:, :], mt, ACT.Copy, scale=-1.0).then_inc(s_neg, 1)

            act.sem_inc(s_exp, 2)
            act.sem_inc(s_o, 1)
            act.sem_inc(s_neg, 1)
            negate(0)
            for i in range(ST_LEAD):
                exps(0, i, 0)
                exps(0, i, 1)

            def body(b, last):
                for i in range(NB):
                    g, s = i // NS, i % NS
                    exps(b, i + ST_LEAD, 0, last)
                    if s == TURN - ST_LEAD and not (last and g == G - 1):
                        negate(b * G + g + 1)
                    exps(b, i + ST_LEAD, 1, last)
                    if s in (3, NS - 1):
                        c = int(s > 3)
                        n = b * G + g
                        act.wait_ge(s_pv, b * NB + i + 4)
                        act.wait_ge(s_oout[c], 16 * n + 16)
                        act.activation(o_sb[:, c, :], o_ps[:, :], ACT.Copy).then_inc(s_o, 1)

            batches(act, body)

        @block.gpsimd
        def _(pool):
            def v_group(n, par):
                pool.wait_ge(s_pv, NS * n - NS + 3)
                pool.sem_inc(apart["pool"], 1)
                pool.tensor_copy(Vone[:, par, :, :, 0:HD],
                                 Vg[:, bass.ds(n, 1), :, :].rearrange("p a t (h d) -> p (a t) h d", h=GH)).then_inc(s_v, 1)
                pool.wait_ge(s_v, n + 1)

            def split_max(n, first=False):
                pool.wait_ge(s_neg, n + 2)
                if not first:
                    pool.wait_ge(s_row, 48 * n)
                src = negmax[:, :]
                for i in range(3):
                    pool.sem_inc(apart["pool"], 1)
                    pool.tensor_copy(max_parts[:, i, :], src).then_inc(s_sp, 1)
                    pool.wait_ge(s_sp, 5 * n + 2 * i + 6)
                    if i < 2:
                        pool.tensor_tensor(max_rest[:, i, :], src, max_parts[:, i, :], ALU.subtract).then_inc(s_sp, 1)
                        pool.wait_ge(s_sp, 5 * n + 2 * i + 7)
                        src = max_rest[:, i, :]

            def mask(b, i):
                s = i % NS
                c, kb = STEPS[s]
                if kb < 4 * c:
                    return
                pool.wait_ge(s_exp, 2 * (b * NB + i) + 4)
                pool.sem_inc(apart["pool"], 1)
                part = PT[:, s % 3, :, 0:P]
                pool.affine_select(out=part, in_=part, compare_op=ALU.is_ge, fill=0.0, base=0,
                                   pattern=[[0, GH], [1, P]], channel_multiplier=-1).then_inc(s_diag, 1)
                pool.wait_ge(s_diag, TB * G * b + TB * (i // NS) + kb + 1)

            pool.sem_inc(s_pv, 3)
            pool.sem_inc(s_sp, 5)
            pool.tensor_copy(Vone[:, 0, :, :, 0:HD], Vg[:, 0, :, :].rearrange("p t (h d) -> p t h d", h=GH)).then_inc(s_v, 1)
            pool.wait_ge(s_v, 1)
            split_max(0, first=True)
            for i in range(ST_LEAD):
                mask(0, i)

            def body(b, last):
                for i in range(NB):
                    g, s = i // NS, i % NS
                    if not (last and i + ST_LEAD >= NB):
                        mask(b, i + ST_LEAD)
                    if not (last and g == G - 1):
                        if s == 3:
                            v_group(b * G + g + 1, (g + 1) % 2)
                        if s == 5:
                            split_max(b * G + g + 1)

            batches(pool, body)


RING = 4
MAXTILES = -(-(T + E0 - 1) // RING) * RING


def merge_heads(nc, io, keep):
    X, ident, XN, XH = keep["X"], keep["ident"], keep["XN"], keep["XH"]
    with ExitStack() as ctx:
        m = Scope(nc, ctx, "p3_")
        Wo = m.sb("wo", [P, D])
        C = m.sb("centroids", [P, E0])
        sums, inv_sums = (m.sb(n, [2 * H * 2, S // 2]) for n in ("sums", "inv_sums"))
        att = m.sb("att", [P, B, S])
        inv = m.sb("inv", [P, B, S])
        attT = m.sb("attT", [P, 2, S])
        yn, xn = (m.sb(n, [P, 2, TB, D]) for n in ("yn", "xn"))
        ln = [[Moments(m, f"{k}{h}") for k in ("y", "x")] for h in range(2)]
        var2, inv2, rstd2 = (m.sb(n, [P, 2, 2, TB]) for n in ("var2", "inv2", "rstd2"))
        xnT = m.sb("xnT", [P, 2, S])
        y_ps = [m.ps(f"y_ps{h}", [P, TB, D]) for h in range(2)]
        t_ps = m.ps("t_ps", [P, S])
        a_ps = [m.ps(f"a_ps{h}", [P, TB, E0]) for h in range(2)]

        s_w, s_ew = m.sem("w_loaded"), m.sem("expert_weights_loaded")
        s_sums, s_is, s_iout = m.sem("sums_loaded"), m.sem("sums_inverted"), m.sem("inverted_sums_stored")
        s_att = [m.sem(f"heads_loaded{p}") for p in range(B // 2)]
        s_attT, s_y = m.sem("attT_ready"), m.sem("y_ready")
        s_ln = MomentSems(m)
        s_in, s_rt, s_v2 = s_ln.inv, m.sem("rstd_ready"), m.sem("var2_steps")
        s_yn, s_x, s_xn, s_xh = m.sem("y_normed"), m.sem("x_updated"), m.sem("xn_ready"), m.sem("xn_kept_steps")
        s_tr = m.sem("xn_transposed")
        s_xnT = m.sem("xnT_ready")
        s_a, s_af = m.sem("affinity_ready"), m.sem("affinity_kept")
        apart = keep["apart"]
        block = ctx.enter_context(nc.Block())

        @block.sync
        def _(sp):
            rows = io["heads_out"].rearrange("n (j r) s -> (n j) r s", j=GH)
            sp.dma_start(sums[:, :], softmax_sums(io, 1)).then_inc(s_sums, 16)
            sp.dma_start(Wo[:, :], io["l0_w"][:, 5, :]).then_inc(s_w, 16)
            sp.dma_start(C[:, :], io["centroids"]).then_inc(s_w, 16)

            def load_heads(b):
                sp.dma_start(att[:, b, :], rows[b * H:(b + 1) * H, 0:HD, :]).then_inc(s_att[b // 2], 16)

            def load_inverted(b):
                sp.dma_start(inv[:, b, :], io["inv_sums"][b * H:(b + 1) * H, :].unsqueeze(1).broadcast_to([H, HD, S])
                             ).then_inc(s_att[b // 2], 16)

            for b in range(2):
                load_heads(b)
                load_inverted(b)
            sp.wait_ge(s_is, 1)
            sp.dma_start(inverted_sums(io, 1), inv_sums[:, :]).then_inc(s_iout, 16)
            sp.wait_ge(s_iout, 16)
            for b in range(2, B):
                load_heads(b)
                load_inverted(b)
            for name, src in (("w1_all", "w1"), ("w2_all", "w2"), ("ln_b1", "small")):
                sp.dma_start(keep[name][:], io[src]).then_inc(s_ew, 16)
            sp.dma_start(keep["b2_rows"][:], io["b2"].rearrange("(a e) d -> a e d", a=1).broadcast_to([P, E0, D])).then_inc(s_ew, 16)
            sp.wait_ge(s_ew, 64)

        @block.vector
        def _(dve):
            dve.wait_ge(s_sums, 16)
            dve.reciprocal(inv_sums[:, :], sums[:, :]).then_inc(s_is, 1)
            def attention_rows(p, loaded):
                dve.wait_ge(loaded, 64)
                for h in range(2):
                    b = 2 * p + h
                    dve.tensor_tensor(attT[:, h, :], att[:, bass.ds(b, 1), :].rearrange("p a s -> p (a s)"),
                                      inv[:, bass.ds(b, 1), :].rearrange("p a s -> p (a s)"), ALU.mult).then_inc(s_attT, 1)
                for h in range(2):
                    dve.wait_ge(s_y, 2 * p + h + 1)
                    dve.sem_inc(apart["dve"], 1)
                    moments(dve, s_ln, apart["dve"], ln[h][0], 4 * p + h, lambda t: y_ps[h][:, t, :])

            attention_rows(0, s_att[0])

            def body(p, last):
                for h in range(2):
                    dve.wait_ge(s_rt, 6 * p + h + 1)
                    for t in range(TB):
                        dve.tensor_scalar(yn[:, h, t, :], y_ps[h][:, t, :], ln[h][0].mv[:, t, 0:1],
                                          ln[h][0].rstd[:, t:t + 1], ALU.subtract, ALU.mult).then_inc(s_yn, 1)
                for h in range(2):
                    dve.wait_ge(s_x, 2 * p + h + 1)
                    dve.sem_inc(apart["dve"], 1)
                    moments(dve, s_ln, apart["dve"], ln[h][1], 4 * p + 2 + h, lambda t: row_tile(X, 2 * p + h, t))
                    dve.wait_ge(s_in, 6 * p + 3 + 2 * h)
                    dve.tensor_tensor(var2[:, h, 0, :], ln[h][1].mv[:, :, 1], ln[h][1].inv[:, :], ALU.mult).then_inc(s_v2, 1)
                    dve.wait_ge(s_v2, 4 * p + 2 * h + 1)
                    dve.tensor_scalar(var2[:, h, 1, :], var2[:, h, 0, :], EPS, None, ALU.add).then_inc(s_v2, 1)
                    dve.wait_ge(s_v2, 4 * p + 2 * h + 2)
                    dve.reciprocal(inv2[:, h, 0, :], var2[:, h, 1, :]).then_inc(s_in, 1)
                for h in range(2):
                    dve.wait_ge(s_rt, 6 * p + 3 + 2 * h)
                    for t in range(TB):
                        dve.tensor_scalar(xn[:, h, t, :], row_tile(X, 2 * p + h, t), ln[h][1].mv[:, t, 0:1],
                                          ln[h][1].rstd[:, t:t + 1], ALU.subtract, ALU.mult).then_inc(s_xn, 1)
                if not last:
                    attention_rows(p + 1, s_att[1])
                for h in range(2):
                    dve.wait_ge(s_a, 2 * p + h + 1)
                    dve.tensor_copy(keep["aff"][:, bass.ds((2 * p + h) * TB, TB), :], a_ps[h][:, :, :]).then_inc(s_af, 1)
                dve.wait_ge(s_xh, 4 * p + 4)

            pairs(dve, body)

        @block.scalar
        def _(act):
            act.sem_inc(s_xnT, 1)
            def y_roots(p):
                for h in range(2):
                    act.wait_ge(s_in, 6 * p + h + 1)
                    act.activation(ln[h][0].rstd[:, :], ln[h][0].inv[:, :], ACT.Sqrt).then_inc(s_rt, 1)

            y_roots(0)

            def body(p, last):
                for h in range(2):
                    act.wait_ge(s_in, 6 * p + 3 + 2 * h)
                    act.activation(ln[h][1].rstd[:, :], ln[h][1].inv[:, :], ACT.Sqrt).then_inc(s_rt, 1)
                    act.wait_ge(s_in, 6 * p + 4 + 2 * h)
                    act.activation(rstd2[:, h, 0, :], inv2[:, h, 0, :], ACT.Sqrt).then_inc(s_rt, 1)
                for h in range(2):
                    act.wait_ge(s_tr, 2 * p + h + 1)
                    act.activation(xnT[:, h, :], t_ps[:, :], ACT.Copy).then_inc(s_xnT, 1)
                if not last:
                    y_roots(p + 1)

            pairs(act, body)

        @block.gpsimd
        def _(pool):
            with pool.Fori(0, B // 2) as p:
                for h in range(2):
                    pool.wait_ge(s_yn, TB * (2 * p + h + 1))
                    rows = X[:, bass.ds((2 * p + h) * TB, TB), :]
                    pool.tensor_tensor(rows, rows, yn[:, h, :, :], ALU.add).then_inc(s_x, 1)
                    pool.wait_ge(s_x, 2 * p + h + 1)
                for h in range(2):
                    b = 2 * p + h
                    pool.wait_ge(s_xn, TB * (b + 1))
                    pool.wait_ge(s_rt, 6 * p + 4 + 2 * h)
                    pool.tensor_tensor(XH[:, bass.ds(b * TB, TB), :], xn[:, h, :, :],
                                       rstd2[:, h, 0, :].unsqueeze(2).broadcast_to([P, TB, D]), ALU.mult).then_inc(s_xh, 1)
                    pool.wait_ge(s_xh, 2 * b + 1)
                    pool.sem_inc(apart["pool"], 1)
                    pool.tensor_copy(XN[:, bass.ds(b * TB, TB), :], xn[:, h, :, :]).then_inc(s_xh, 1)
                    pool.wait_ge(s_xh, 2 * b + 2)

        @block.tensor
        def _(pe):
            pe.wait_ge(s_w, 32)
            def project(p):
                for h in range(2):
                    pe.wait_ge(s_attT, 2 * p + h + 1)
                    for t in range(TB):
                        mm = pe.matmul(y_ps[h][:, t, :], attT[:, h, t * P:(t + 1) * P], Wo[:, :], start=True, stop=True)
                    mm.then_inc(s_y, 1)

            project(0)

            def body(p, last):
                for h in range(2):
                    pe.wait_ge(s_xn, TB * (2 * p + h + 1))
                    pe.wait_ge(s_xnT, 2 * p + h + 1)
                    for t in range(TB):
                        mm = pe.transpose(t_ps[:, t * P:(t + 1) * P], xn[:, h, t, :], ident[:, :])
                    mm.then_inc(s_tr, 1)
                if not last:
                    project(p + 1)
                for h in range(2):
                    pe.wait_ge(s_xnT, 2 * p + h + 2)
                    for t in range(TB):
                        mm = pe.matmul(a_ps[h][:, t, :], xnT[:, h, t * P:(t + 1) * P], C[:, :], start=True, stop=True)
                    mm.then_inc(s_a, 1)

            pairs(pe, body)


def route(nc, io, keep):
    XH, aff, pos, gate, tile_expert = keep["XH"], keep["aff"], keep["pos"], keep["gate"], keep["tile_expert"]
    NE = T * E0
    with ExitStack() as ctx:
        m = Scope(nc, ctx, "p4_")
        top = m.sb("top", [P, T])
        tied = m.sb("tied", [P, T, E0])
        early = m.sb("early", [P, E0])
        score = m.sb("score", [P, T, E0])
        best = m.sb("best", [P, T])
        chosen = m.sb("chosen", [P, T, E0])
        chosen_bf = m.sb("chosen_bf", [P, T, E0], BF16)
        before = m.sb("before", [P, P], BF16)
        ones = m.sb("ones", [P, P], BF16)
        scan = m.sb("scan", [P, 6, T, E0])
        steps = m.sb("steps", [P, T])
        over = m.sb("over", [P, E0, T])
        tiles = m.sb("tiles", [P, E0])
        lower = m.sb("lower", [P, E0, E0])
        prod = m.sb("prod", [P, E0, E0])
        first = m.sb("first", [P, E0])
        last = m.sb("last", [P, E0])
        index = m.sb("index", [P, MAXTILES])
        past = m.sb("past", [P, MAXTILES, E0])
        owner = m.sb("owner", [P, MAXTILES])
        place = m.sb("place", [P, T, E0])
        start = m.sb("start", [P, E0])
        at = m.sb("at", [P, T])
        e_neg = m.sb("e_neg", [P, T])
        zeros = m.sb("zeros", [P, MAXTILES, D])
        rank_ps = m.ps("rank_ps", [P, NE])
        count_ps = m.ps("count_ps", [P, NE])

        s_c, s_z = m.sem("constants"), m.sem("zeros_stored")
        s_zm = m.sem("zeros_made")
        s_d, s_oh, s_cnt, s_e = m.sem("router_steps"), m.sem("chosen_ready"), m.sem("counts_ready"), m.sem("gate_exp")
        s_pos, s_sc = m.sem("places_ready"), m.sem("rows_placed")
        block = ctx.enter_context(nc.Block())

        @block.sync
        def _(sp):
            sp.wait_ge(s_zm, 1)
            sp.dma_start(io["sorted_in"].rearrange("(n p) d -> p n d", p=P), zeros[:, :, :]).then_inc(s_z, 16)

        @block.gpsimd
        def _(pool):
            n = 0
            def step(ins):
                nonlocal n
                n += 1
                ins.then_inc(s_c, 1)
                pool.wait_ge(s_c, n)
            step(pool.iota(early[:, :], [[-1, E0]], base=E0, channel_multiplier=0, allow_small_or_imprecise_dtypes=True))
            step(pool.iota(steps[:, :], [[P, T]], base=0, channel_multiplier=0, allow_small_or_imprecise_dtypes=True))
            step(pool.iota(index[:, :], [[1, MAXTILES]], base=0, channel_multiplier=0, allow_small_or_imprecise_dtypes=True))
            step(pool.memset(ones[:, :], 1.0))
            step(pool.memset(lower[:, :, :], 1.0))
            step(pool.affine_select(out=before[:, :], in_=ones[:, :], compare_op=ALU.is_gt, fill=0.0, base=0,
                                    pattern=[[1, P]], channel_multiplier=-1))
            step(pool.affine_select(out=lower[:, :, :], in_=lower[:, :, :], compare_op=ALU.is_gt, fill=0.0, base=0,
                                    pattern=[[1, E0], [-1, E0]], channel_multiplier=0))
            pool.wait_ge(s_pos, 1)
            pool.wait_ge(s_z, 16)
            for t in range(T):
                pool.indirect_dma_start(io["sorted_in"], bass.IndirectOffsetOnAxis(ap=pos[:, t:t + 1], axis=0),
                                        XH[:, t, :], None).then_inc(s_sc, 16)
            pool.wait_ge(s_sc, 16 * T)

        @block.tensor
        def _(pe):
            pe.wait_ge(s_c, 7)
            pe.wait_ge(s_oh, 1)
            oh = chosen_bf[:, :, :].rearrange("p t e -> p (t e)")
            pe.matmul(rank_ps[:, :], before[:, :], oh, start=True, stop=True).then_inc(s_cnt, 1)
            pe.matmul(count_ps[:, :], ones[:, :], oh, start=True, stop=True).then_inc(s_cnt, 1)

        @block.scalar
        def _(act):
            act.wait_ge(s_d, 1)
            act.activation(e_neg[:, :], top[:, :], ACT.Exp, scale=-1.0).then_inc(s_e, 1)

        @block.vector
        def _(dve):
            n = 0
            def step(ins):
                nonlocal n
                n += 1
                ins.then_inc(s_d, 1)
                dve.wait_ge(s_d, n)
            def over_e(x):
                return x.unsqueeze(2).broadcast_to([P, T, E0])
            step(dve.tensor_reduce(top[:, :], aff[:, :, :], AX.X, ALU.max))
            dve.memset(zeros[:, :, :], 0.0).then_inc(s_zm, 1)
            step(dve.tensor_tensor(tied[:, :, :], aff[:, :, :], over_e(top[:, :]), ALU.is_equal))
            dve.wait_ge(s_c, 7)
            step(dve.tensor_tensor(score[:, :, :], tied[:, :, :], early[:, :].unsqueeze(1).broadcast_to([P, T, E0]), ALU.mult))
            step(dve.tensor_reduce(best[:, :], score[:, :, :], AX.X, ALU.max))
            step(dve.tensor_tensor(chosen[:, :, :], score[:, :, :], over_e(best[:, :]), ALU.is_equal))
            dve.tensor_copy(chosen_bf[:, :, :], chosen[:, :, :]).then_inc(s_oh, 1)
            dve.wait_ge(s_e, 1)
            step(dve.tensor_scalar(at[:, :], e_neg[:, :], 1.0, None, ALU.add))
            step(dve.reciprocal(gate[:, :], at[:, :]))
            dve.wait_ge(s_cnt, 2)
            step(dve.tensor_copy(scan[:, 0, :, :], count_ps[:, :].rearrange("p (t e) -> p t e", t=T)))
            for k in range(5):
                r = 1 << k
                step(dve.tensor_copy(scan[:, k + 1, 0:r, :], scan[:, k, 0:r, :]))
                step(dve.tensor_tensor(scan[:, k + 1, r:T, :], scan[:, k, r:T, :], scan[:, k, 0:T - r, :], ALU.add))
            total = scan[:, 5, T - 1, :]
            step(dve.tensor_tensor(over[:, :, :], total.unsqueeze(2).broadcast_to([P, E0, T]),
                                   steps[:, :].unsqueeze(1).broadcast_to([P, E0, T]), ALU.is_gt))
            step(dve.tensor_reduce(tiles[:, :], over[:, :, :], AX.X, ALU.add))
            step(dve.tensor_tensor(prod[:, :, :], lower[:, :, :], tiles[:, :].unsqueeze(1).broadcast_to([P, E0, E0]), ALU.mult))
            step(dve.tensor_reduce(first[:, :], prod[:, :, :], AX.X, ALU.add))
            step(dve.tensor_tensor(last[:, :], first[:, :], tiles[:, :], ALU.add))
            M = MAXTILES
            step(dve.tensor_tensor(past[:, :, :], index[:, :].unsqueeze(2).broadcast_to([P, M, E0]),
                                   last[:, :].unsqueeze(1).broadcast_to([P, M, E0]), ALU.is_ge))
            step(dve.tensor_reduce(owner[:, :], past[:, :, :], AX.X, ALU.add))
            step(dve.tensor_scalar(tile_expert[:, :], owner[:, :], float(E0 - 1), None, ALU.min))
            step(dve.tensor_scalar(start[:, :], first[:, :], float(P), None, ALU.mult))
            step(dve.tensor_tensor(place[:, :, :], scan[:, 5, :, :], scan[:, 0, :, :], ALU.subtract))
            step(dve.tensor_tensor(tied[:, :, :], place[:, :, :], rank_ps[:, :].rearrange("p (t e) -> p t e", t=T), ALU.add))
            step(dve.tensor_tensor(place[:, :, :], tied[:, :, :], start[:, :].unsqueeze(1).broadcast_to([P, T, E0]), ALU.add))
            step(dve.tensor_tensor(score[:, :, :], place[:, :, :], chosen[:, :, :], ALU.mult))
            step(dve.tensor_reduce(best[:, :], score[:, :, :], AX.X, ALU.add))
            dve.tensor_copy(pos[:, :], best[:, :]).then_inc(s_pos, 1)
            dve.wait_ge(s_pos, 1)


def experts(nc, io, keep):
    ident, tile_expert = keep["ident"], keep["tile_expert"]
    with ExitStack() as ctx:
        m = Scope(nc, ctx, "p5_")
        W1, W2, small, b2 = (keep[k] for k in ("w1_all", "w2_all", "ln_b1", "b2_rows"))
        xs = m.sb("xs", [P, RING, D])
        w1 = m.sb("w1_tile", [P, RING, F0])
        xin = m.sb("xin", [P, RING, P])
        hT = m.sb("hT", [P, RING, FC, P])
        y = m.sb("y", [P, RING, D])
        x_ps = [m.ps(f"x_ps{r}", [P, P]) for r in range(2)]
        h_ps = [m.ps(f"h_ps{r}", [P, FC, P]) for r in range(2)]
        y_ps = [m.ps(f"y_ps{r}", [P, D]) for r in range(2)]

        s_ld = [m.sem(f"tile_loaded{r}") for r in range(RING)]
        s_w1 = m.sem("w1_copied")
        s_tr = m.sem("x_transposed")
        s_in = m.sem("x_scaled")
        s_h = m.sem("h_ready")
        s_r = m.sem("h_relu")
        s_y = m.sem("y_ready")
        s_yo = m.sem("y_kept")
        s_out = [m.sem(f"y_stored{r}") for r in range(RING)]
        apart = keep["apart"]
        block = ctx.enter_context(nc.Block())
        ROUNDS = MAXTILES // RING

        def rounds(eng, body):
            with eng.Fori(0, ROUNDS - 1) as k:
                body(k, False)
            body(ROUNDS - 1, True)

        def expert(eng, i):
            return eng.value_load(tile_expert[0:1, bass.ds(i, 1)], min_val=0, max_val=E0 - 1)

        @block.sync
        def _(sp):
            for r in range(RING):
                sp.sem_inc(s_out[r], 16)
                sp.dma_start(xs[:, r, :], io["sorted_in"][r * P:(r + 1) * P, :]).then_inc(s_ld[r], 16)

            def body(k, last):
                for r in range(RING):
                    i = k * RING + r
                    if not last:
                        sp.wait_ge(s_tr, i + 1)
                        sp.dma_start(xs[:, r, :], io["sorted_in"][bass.ds((i + RING) * P, P), :]).then_inc(s_ld[r], 16)
                    sp.wait_ge(s_yo, i + 3)
                    sp.dma_start(io["sorted_out"][bass.ds(i * P, P), :], y[:, r, :]).then_inc(s_out[r], 16)

            rounds(sp, body)
            for r in range(RING):
                sp.wait_ge(s_out[r], 16 * ROUNDS + 16)

        @block.tensor
        def _(pe):
            def transpose(k, r):
                i = k * RING + r
                pe.wait_ge(s_ld[r % RING], 16 * (k + 1 + r // RING))
                pe.wait_ge(s_in, i + 1)
                pe.transpose(x_ps[r % 2][:, :], xs[:, r % RING, :], ident[:, :]).then_inc(s_tr, 1)

            def hidden(k, r):
                i = k * RING + r
                pe.wait_ge(s_in, i + 3)
                pe.wait_ge(s_w1, i + 1)
                pe.wait_ge(s_r, FC * i + FC)
                for c in range(FC):
                    mm = pe.matmul(h_ps[r % 2][:, c, :], w1[:, r % RING, c * P:(c + 1) * P], xin[:, r % RING, :],
                                   start=True, stop=True)
                mm.then_inc(s_h, 1)

            def output(k, r):
                i = k * RING + r
                e = expert(pe, i)
                pe.wait_ge(s_r, FC * i + 3 * FC)
                pe.wait_ge(s_yo, i + 1)
                for c in range(FC):
                    mm = pe.matmul(y_ps[r % 2][:, :], hT[:, r, c, :], W2[:, bass.ds(e, 1), c, :].rearrange("p a d -> p (a d)"),
                                   start=(c == 0), stop=(c == FC - 1))
                mm.then_inc(s_y, 1)

            transpose(0, 0)
            transpose(0, 1)
            hidden(0, 0)

            def body(k, last):
                for r in range(RING):
                    if not (last and r + 2 >= RING):
                        transpose(k, r + 2)
                    if not (last and r + 1 >= RING):
                        hidden(k, r + 1)
                    output(k, r)

            rounds(pe, body)

        @block.scalar
        def _(act):
            act.sem_inc(s_r, 2 * FC)

            def body(k, last):
                for r in range(RING):
                    i = k * RING + r
                    e = expert(act, i)
                    act.wait_ge(s_y, i + 1)
                    act.wait_ge(s_h, i + 5)
                    act.sem_inc(apart["act"], 1)
                    for c in range(FC):
                        act.activation(hT[:, r, c, :], h_ps[r % 2][:, c, :], ACT.Relu,
                                       bias=small[:, bass.ds(e, 1), 2 + c]).then_inc(s_r, 1)

            rounds(act, body)

        @block.vector
        def _(dve):
            def scale(k, r):
                i = k * RING + r
                e = expert(dve, i)
                dve.wait_ge(s_h, i + 1)
                dve.tensor_copy(w1[:, r % RING, :], W1[:, bass.ds(e, 1), :].rearrange("p a f -> p (a f)")).then_inc(s_w1, 1)
                dve.wait_ge(s_tr, i + 1)
                dve.tensor_scalar(xin[:, r % RING, :], x_ps[r % 2][:, :], small[:, bass.ds(e, 1), 0],
                                  small[:, bass.ds(e, 1), 1], ALU.mult, ALU.add).then_inc(s_in, 1)

            dve.sem_inc(s_in, 2)
            dve.sem_inc(s_h, RING)
            dve.sem_inc(s_y, RING)
            dve.sem_inc(s_yo, 2)
            scale(0, 0)
            scale(0, 1)

            def body(k, last):
                for r in range(RING):
                    i = k * RING + r
                    if not (last and r + 2 >= RING):
                        scale(k, r + 2)
                    e = expert(dve, i)
                    dve.wait_ge(s_y, i + 1 + RING)
                    dve.wait_ge(s_out[r], 16 * k + 16)
                    dve.tensor_tensor(y[:, r, :], y_ps[r % 2][:, :], b2[:, bass.ds(e, 1), :].rearrange("p a d -> p (a d)"),
                                      ALU.add).then_inc(s_yo, 1)

            rounds(dve, body)


def combine_and_project(nc, io, keep):
    X, XN, ident, gate, pos = (keep[k] for k in ("X", "XN", "ident", "gate", "pos"))
    qT, kT, VP = keep["qT"], keep["kT"], keep["VP"]
    with ExitStack() as ctx:
        m = Scope(nc, ctx, "p6_")
        W = m.sb("w", [P, 4, D])
        bias = m.sb("bias", [P, 3])
        back = m.sb("back", [P, T, D])
        z, zn, xn = (m.sb(n, [P, 2, TB, D]) for n in ("z", "zn", "xn"))
        ln = [[Moments(m, f"{k}{h}") for k in ("z", "x")] for h in range(2)]
        xnT, vT = m.sb("xnT", [P, 2, S]), m.sb("vT", [P, 2, S])
        t_ps = [m.ps(f"t_ps{h}", [P, S]) for h in range(2)]
        p_ps = [m.ps(f"p_ps{j}", [P, S]) for j in range(2)]

        s_w = m.sem("w_loaded")
        s_g = [m.sem(f"rows_back{b}") for b in range(B)]
        s_ln = MomentSems(m)
        s_in, s_rt = s_ln.inv, m.sem("rstd_ready")
        s_z, s_zn, s_x, s_xn = m.sem("z_ready"), m.sem("z_normed"), m.sem("x_updated"), m.sem("xn_ready")
        s_tr = m.sem("xn_transposed")
        s_xnT = m.sem("xnT_ready")
        s_p = m.sem("projected")
        s_pe = m.sem("projections_kept")
        s_vp = m.sem("vp_ready")
        s_vpe = m.sem("vp_kept")
        apart = keep["apart"]
        block = ctx.enter_context(nc.Block())

        @block.sync
        def _(sp):
            sp.dma_start(W[:, :, :], io["l1_w"]).then_inc(s_w, 16)
            sp.dma_start(bias[:, :], io["b_qkv"]).then_inc(s_w, 16)

        @block.gpsimd
        def _(pool):
            for t in range(T):
                pool.indirect_dma_start(back[:, t, :], None, io["sorted_out"], bass.IndirectOffsetOnAxis(ap=pos[:, t:t + 1], axis=0)
                                        ).then_inc(s_g[t // TB], 16)

        @block.vector
        def _(dve):
            dve.sem_inc(s_vpe, 2)
            def pair(p, rows_back):
                for h in range(2):
                    dve.wait_ge(rows_back[h], 16 * TB)
                    for t in range(TB):
                        dve.scalar_tensor_tensor(out=z[:, h, t, :], in0=row_tile(back, 2 * p + h, t),
                                                 scalar=gate[:, bass.ds((2 * p + h) * TB + t, 1)], in1=row_tile(XN, 2 * p + h, t),
                                                 op0=ALU.mult, op1=ALU.add).then_inc(s_z, 1)
                    dve.wait_ge(s_z, TB * (2 * p + h + 1))
                    dve.sem_inc(apart["dve"], 1)
                    moments(dve, s_ln, apart["dve"], ln[h][0], 4 * p + h, lambda t: z[:, h, t, :])
                for h in range(2):
                    dve.wait_ge(s_rt, 4 * p + h + 1)
                    for t in range(TB):
                        dve.tensor_scalar(zn[:, h, t, :], z[:, h, t, :], ln[h][0].mv[:, t, 0:1], ln[h][0].rstd[:, t:t + 1],
                                          ALU.subtract, ALU.mult).then_inc(s_zn, 1)
                    dve.wait_ge(s_zn, TB * (2 * p + h + 1))
                    rows = X[:, bass.ds((2 * p + h) * TB, TB), :]
                    dve.tensor_tensor(rows, rows, zn[:, h, :, :], ALU.add).then_inc(s_x, 1)
                for h in range(2):
                    dve.wait_ge(s_x, 2 * p + h + 1)
                    dve.sem_inc(apart["dve"], 1)
                    moments(dve, s_ln, apart["dve"], ln[h][1], 4 * p + 2 + h, lambda t: row_tile(X, 2 * p + h, t))
                for h in range(2):
                    dve.wait_ge(s_rt, 4 * p + h + 3)
                    dve.wait_ge(s_tr, 2 * p + h + 1)
                    for t in range(TB):
                        dve.tensor_scalar(xn[:, h, t, :], row_tile(X, 2 * p + h, t), ln[h][1].mv[:, t, 0:1],
                                          ln[h][1].rstd[:, t:t + 1], ALU.subtract, ALU.mult).then_inc(s_xn, 1)

            assert B == 4
            pairs(dve, lambda p, last: pair(p, s_g[2:4] if last else s_g[0:2]))

        @block.scalar
        def _(act):
            act.sem_inc(s_pe, 2)
            act.wait_ge(s_w, 32)
            def root(p, k):
                act.wait_ge(s_in, 4 * p + k + 1)
                act.activation(ln[k % 2][k // 2].rstd[:, :], ln[k % 2][k // 2].inv[:, :], ACT.Sqrt).then_inc(s_rt, 1)

            def evacuate(b, h):
                act.wait_ge(s_tr, b + 3)
                act.activation(xnT[:, h, :], t_ps[h][:, :], ACT.Copy).then_inc(s_xnT, 1)
                for k, (j, dst) in enumerate(((2, vT[:, h, :]), (0, qT[:, bass.ds(b * S, S)]), (1, kT[:, bass.ds(b * S, S)]))):
                    act.wait_ge(s_p, 3 * b + k + 1)
                    act.sem_inc(apart["act"], 1)
                    act.activation(dst, p_ps[(3 * h + k) % 2][:, :], ACT.Identity, bias=bias[:, j:j + 1]).then_inc(s_pe, 1)
                act.wait_ge(s_vp, b + 1)
                act.sem_inc(apart["act"], 1)
                act.activation(VP[:, bass.ds(b * TB, TB), :], t_ps[h][:, :].rearrange("p (t d) -> p t d", t=TB),
                               ACT.Copy).then_inc(s_vpe, 1)

            root(0, 0)
            root(0, 1)

            def body(p, last):
                root(p, 2)
                root(p, 3)
                for h in range(2):
                    evacuate(2 * p + h, h)
                    if not last:
                        root(p + 1, h)

            pairs(act, body)

        @block.tensor
        def _(pe):
            pe.sem_inc(s_tr, 2)
            pe.wait_ge(s_w, 32)
            with pe.Fori(0, B // 2) as p:
                for h in range(2):
                    b = 2 * p + h
                    pe.wait_ge(s_xn, TB * (b + 1))
                    pe.wait_ge(s_vpe, b + 1)
                    for t in range(TB):
                        mm = pe.transpose(t_ps[h][:, t * P:(t + 1) * P], xn[:, h, t, :], ident[:, :])
                    mm.then_inc(s_tr, 1)
                    pe.wait_ge(s_xnT, b + 1)
                    for k, j in enumerate((2, 0, 1)):
                        pe.wait_ge(s_pe, 3 * b + k + 1)
                        for c in range(2):
                            mm = pe.matmul(p_ps[(3 * h + k) % 2][:, c * 512:(c + 1) * 512], W[:, j, :],
                                           xnT[:, h, c * 512:(c + 1) * 512], start=True, stop=True)
                        mm.then_inc(s_p, 1)
                    pe.wait_ge(s_pe, 3 * b + 3)
                    for t in range(TB):
                        mm = pe.matmul(t_ps[h][:, t * P:(t + 1) * P], vT[:, h, t * P:(t + 1) * P], W[:, 3, :], start=True, stop=True)
                    mm.then_inc(s_vp, 1)


UNIT = 0.2
BAND = {p: float(np.log(p / (1 - p))) for p in (0.95, 0.85, 0.25, 0.1)}
TERMS = ((0.1, ALU.is_ge, ALU.add, 0.5), (0.85, ALU.is_gt, ALU.mult, 2.5),
         (0.25, ALU.is_ge, ALU.mult, 3.5), (0.95, ALU.is_gt, ALU.mult, 2.5))
QK_LEAD, TERM_LEAD, F_LEAD, EXP_LEAD, PV_LEAD = 5, 4, 3, 2, 1
assert TB % 4 == 0


def banded_attention(nc, io, keep):
    ident, qT, kT, VP, Y = (keep[k] for k in ("ident", "qT", "kT", "VP", "Y"))
    with ExitStack() as ctx:
        m = Scope(nc, ctx, "p7_")
        bp = m.sb("b_proj", [P, D])
        q = m.sb("q", [P, 4, P])
        x = m.sb("x", [P, 4, S])
        terms = m.sb("band_terms", [P, 2, 4, S], BF16)
        pairs = m.sb("term_pairs", [P, 2, 2, S], BF16)
        factor = m.sb("factor", [P, S], BF16)
        f = m.sb("f", [P, 2, S])
        top, neg = m.sb("top", [P, 2]), m.sb("neg", [P, 2])
        probs = m.sb("probs", [P, 2, S])
        total = m.sb("total", [P, 4])
        inv = m.sb("inv", [P, 2])
        pT = m.sb("pT", [P, 2, TB, P])
        s_ps = [m.ps(f"s_ps{r}", [P, S]) for r in range(2)]
        t_ps = m.ps("t_ps", [P, TB, P])
        y_ps = [m.ps(f"y_ps{r}", [P, D]) for r in range(2)]

        s_b, s_fw = m.sem("b_loaded"), m.sem("ffn_weights_loaded")
        s_q = [m.sem(f"q_loaded{r}") for r in range(4)]
        s_s = m.sem("scores_ready")
        s_x = m.sem("scores_scaled")
        s_term = m.sem("band_terms_ready")
        s_pair = m.sem("term_pairs_ready")
        s_f = m.sem("band_steps")
        s_e = m.sem("exps_ready")
        s_t = m.sem("p_transposed")
        s_pt = m.sem("pT_ready")
        s_y = m.sem("pv_ready")
        s_i = m.sem("sums_inverted")
        s_o = m.sem("rows_out")
        apart = keep["apart"]
        block = ctx.enter_context(nc.Block())

        def batches(eng, body):
            with eng.Fori(0, B - 1) as b:
                body(b, False)
            body(B - 1, True)

        def ahead(last, i):
            return not (last and i >= TB)

        @block.sync
        def _(sp):
            sp.dma_start(bp[:, :], io["b_proj"].rearrange("(a d) -> a d", a=1).broadcast_to([P, D])).then_inc(s_b, 16)

            def load(b, i):
                n = b * TB + i
                sp.wait_ge(s_s, n + 1)
                sp.dma_start(q[:, i % 4, :], qT[:, bass.ds(n * P, P)]).then_inc(s_q[i % 4], 16)

            for i in range(4):
                sp.dma_start(q[:, i, :], qT[:, i * P:(i + 1) * P]).then_inc(s_q[i], 16)

            def body(b, last):
                for i in range(TB):
                    if ahead(last, i + 4):
                        load(b, i + 4)

            for name in ("f_w1", "f_w2", "next_w", "f_b12"):
                sp.dma_start(keep[name][:], io[name]).then_inc(s_fw, 16)
            sp.dma_start(keep["next_b_rows"][:], io["next_b"].rearrange("(a d) -> a d", a=1).broadcast_to([P, D])).then_inc(s_fw, 16)
            batches(sp, body)
            sp.wait_ge(s_fw, 80)

        @block.tensor
        def _(pe):
            def scores(b, i):
                n = b * TB + i
                pe.wait_ge(s_q[i % 4], 16 * (b * (TB // 4) + i // 4 + 1))
                pe.wait_ge(s_x, n + 1)
                for c in range(2):
                    mm = pe.matmul(s_ps[i % 2][:, c * 512:(c + 1) * 512], q[:, i % 4, :],
                                   kT[:, bass.ds((b + i // TB) * S + c * 512, 512)], start=True, stop=True)
                mm.then_inc(s_s, 1)

            def transpose(b, i):
                n = b * TB + i
                pe.wait_ge(s_e, n + 3)
                pe.wait_ge(s_pt, n + 1)
                for k in range(TB):
                    mm = pe.transpose(t_ps[:, k, :], probs[:, i % 2, k * P:(k + 1) * P], ident[:, :])
                mm.then_inc(s_t, 1)

            def pv(b, i):
                n = b * TB + i
                pe.wait_ge(s_pt, n + 2)
                pe.wait_ge(s_o, n + 3)
                for k in range(TB):
                    mm = pe.matmul(y_ps[i % 2][:, :], pT[:, i % 2, k, :],
                                   VP[:, bass.ds((b + i // TB) * TB + k, 1), :].rearrange("p a d -> p (a d)"),
                                   start=(k == 0), stop=(k == TB - 1))
                mm.then_inc(s_y, 1)

            for i in range(QK_LEAD):
                scores(0, i)
            transpose(0, 0)
            pv(0, 0)

            def body(b, last):
                for i in range(TB):
                    if ahead(last, i + PV_LEAD):
                        transpose(b, i + PV_LEAD)
                    if ahead(last, i + QK_LEAD):
                        scores(b, i + QK_LEAD)
                    if ahead(last, i + PV_LEAD):
                        pv(b, i + PV_LEAD)

            batches(pe, body)

        @block.scalar
        def _(act):
            def scale(b, i):
                n = b * TB + i
                act.wait_ge(s_s, n + 5)
                act.wait_ge(s_f, 3 * n + 3)
                act.activation(x[:, i % 4, :], s_ps[i % 2][:, :], ACT.Copy, scale=SCALE).then_inc(s_x, 1)

            def exps(b, i):
                n = b * TB + i
                act.wait_ge(s_f, 3 * (n + 5))
                act.wait_ge(s_t, n + 1)
                act.wait_ge(s_o, n + 1)
                act.activation(probs[:, i % 2, :], f[:, i % 2, :], ACT.Exp, bias=neg[:, i % 2:i % 2 + 1], scale=UNIT,
                               accum_out=total[:, i % 4:i % 4 + 1]).then_inc(s_e, 1)

            def keep_t(b, i):
                n = b * TB + i
                act.wait_ge(s_t, n + 3)
                act.wait_ge(s_y, n + 1)
                act.activation(pT[:, i % 2, :, :], t_ps[:, :, :], ACT.Copy).then_inc(s_pt, 1)

            act.sem_inc(s_x, 2)
            act.sem_inc(s_e, 2)
            for i in range(QK_LEAD):
                scale(0, i)
            exps(0, 0)
            keep_t(0, 0)
            exps(0, 1)

            def body(b, last):
                for i in range(TB):
                    if ahead(last, i + PV_LEAD):
                        keep_t(b, i + PV_LEAD)
                    if ahead(last, i + EXP_LEAD):
                        exps(b, i + EXP_LEAD)
                    if ahead(last, i + QK_LEAD):
                        scale(b, i + QK_LEAD)

            batches(act, body)

        @block.gpsimd
        def _(pool):
            def pair_terms(b, i):
                n = b * TB + i
                pool.wait_ge(s_term, 4 * n + 4)
                pool.wait_ge(s_f, 3 * (n + 3))
                pool.tensor_tensor(pairs[:, i % 2, :, :], terms[:, i % 2, 0:2, :], terms[:, i % 2, 2:4, :],
                                   ALU.add).then_inc(s_pair, 1)
                pool.wait_ge(s_pair, n + 3)

            pool.sem_inc(s_pair, 2)
            for i in range(TERM_LEAD):
                pair_terms(0, i)

            def body(b, last):
                for i in range(TB):
                    if ahead(last, i + TERM_LEAD):
                        pair_terms(b, i + TERM_LEAD)

            batches(pool, body)

        @block.vector
        def _(dve):
            def band_terms(b, i):
                n = b * TB + i
                dve.wait_ge(s_x, n + 3)
                dve.wait_ge(s_pair, n + 1)
                for k, (p, compare, op, value) in enumerate(TERMS):
                    dve.tensor_scalar(terms[:, i % 2, k, :], x[:, i % 4, :], BAND[p], value, compare, op).then_inc(s_term, 1)

            def factor_of(b, i):
                n = b * TB + i
                dve.wait_ge(s_pair, n + 3)
                dve.wait_ge(s_f, 3 * n + 12)
                dve.tensor_tensor(factor[:, :], pairs[:, i % 2, 0, :], pairs[:, i % 2, 1, :], ALU.add).then_inc(s_f, 1)

            def product_of(b, i):
                n = b * TB + i
                dve.wait_ge(s_f, 3 * n + 13)
                dve.wait_ge(s_e, n + 1)
                dve.sem_inc(apart["dve"], 1)
                dve.tensor_tensor_reduce(out=f[:, i % 2, :], in0=factor[:, :], in1=x[:, i % 4, :], scale=1.0, scalar=LOW,
                                         op0=ALU.mult, op1=ALU.max, accum_out=top[:, i % 2:i % 2 + 1]).then_inc(s_f, 1)

            def negate(b, i):
                dve.wait_ge(s_f, 3 * (b * TB + i) + 14)
                dve.tensor_scalar(neg[:, i % 2:i % 2 + 1], top[:, i % 2:i % 2 + 1], -UNIT, None, ALU.mult).then_inc(s_f, 1)

            def invert_sum(b, i):
                n = b * TB + i
                dve.wait_ge(s_y, n + 3)
                dve.wait_ge(s_o, n + 3)
                dve.reciprocal(inv[:, i % 2:i % 2 + 1], total[:, i % 4:i % 4 + 1]).then_inc(s_i, 1)

            def finish(b, i):
                dve.wait_ge(s_i, b * TB + i + 1)
                dve.scalar_tensor_tensor(out=row_tile(Y, b, i), in0=y_ps[i % 2][:, :], scalar=inv[:, i % 2:i % 2 + 1],
                                         in1=bp[:, :], op0=ALU.mult, op1=ALU.add).then_inc(s_o, 1)

            dve.sem_inc(s_s, 4)
            dve.sem_inc(s_f, 12)
            dve.sem_inc(s_t, 2)
            dve.sem_inc(s_pt, 1)
            dve.sem_inc(s_y, 2)
            dve.sem_inc(s_o, 4)
            dve.wait_ge(s_b, 16)
            band_terms(0, 0)
            for i in range(F_LEAD):
                band_terms(0, i + 1)
                factor_of(0, i)
                product_of(0, i)
                negate(0, i)

            def body(b, last):
                for i in range(TB):
                    if ahead(last, i + TERM_LEAD):
                        band_terms(b, i + TERM_LEAD)
                    if ahead(last, i + F_LEAD):
                        factor_of(b, i + F_LEAD)
                    invert_sum(b, i)
                    if ahead(last, i + F_LEAD):
                        product_of(b, i + F_LEAD)
                    finish(b, i)
                    if ahead(last, i + F_LEAD):
                        negate(b, i + F_LEAD)

            batches(dve, body)


def ffn_inputs(nc, io, keep):
    X, Y, ident, XA = (keep[k] for k in ("X", "Y", "ident", "XA"))
    with ExitStack() as ctx:
        m = Scope(nc, ctx, "p8_")
        W = m.sb("attn_w", [P, D])
        vec = m.sb("vectors", [P, 3])
        zn, flat, xh = (m.sb(n, [P, 2, TB, D]) for n in ("zn", "flat", "xh"))
        ln = [[Moments(m, f"{k}{h}") for k in ("y", "x")] for h in range(2)]
        var2, inv2, rstd2 = (m.sb(n, [P, 2, 2, TB]) for n in ("var2", "inv2", "rstd2"))
        hT, fT = m.sb("hT", [P, 2, S]), m.sb("fT", [P, 2, S])
        t_ps = [m.ps(f"t_ps{h}", [P, S]) for h in range(2)]
        a_ps = [m.ps(f"a_ps{h}", [P, S]) for h in range(2)]

        s_w = m.sem("w_loaded")
        s_ln = MomentSems(m)
        s_in, s_rt, s_v2 = s_ln.inv, m.sem("rstd_ready"), m.sem("var2_steps")
        s_zn, s_x, s_f, s_h = m.sem("y_normed"), m.sem("x_updated"), m.sem("flat_ready"), m.sem("xh_ready")
        s_tr, s_T, s_a = m.sem("transposed"), m.sem("transposes_kept"), m.sem("attn_ready")
        s_xa = m.sem("xa_ready")
        apart = keep["apart"]
        block = ctx.enter_context(nc.Block())

        @block.sync
        def _(sp):
            sp.dma_start(W[:, :], io["attn_w"]).then_inc(s_w, 16)
            sp.dma_start(vec[:, :], io["ffn_vectors"]).then_inc(s_w, 16)

        @block.vector
        def _(dve):
            dve.sem_inc(s_xa, 2)
            def y_moments(p):
                for h in range(2):
                    moments(dve, s_ln, apart["dve"], ln[h][0], 4 * p + h, lambda t: row_tile(Y, 2 * p + h, t))

            y_moments(0)

            def body(p, last):
                for h in range(2):
                    dve.wait_ge(s_rt, 6 * p + h + 1)
                    for t in range(TB):
                        dve.tensor_scalar(zn[:, h, t, :], row_tile(Y, 2 * p + h, t), ln[h][0].mv[:, t, 0:1],
                                          ln[h][0].rstd[:, t:t + 1], ALU.subtract, ALU.mult).then_inc(s_zn, 1)
                for h in range(2):
                    dve.wait_ge(s_x, 2 * p + h + 1)
                    dve.sem_inc(apart["dve"], 1)
                    moments(dve, s_ln, apart["dve"], ln[h][1], 4 * p + 2 + h, lambda t: row_tile(X, 2 * p + h, t))
                    dve.wait_ge(s_in, 6 * p + 3 + 2 * h)
                    dve.tensor_tensor(var2[:, h, 0, :], ln[h][1].mv[:, :, 1], ln[h][1].inv[:, :], ALU.mult).then_inc(s_v2, 1)
                    dve.wait_ge(s_v2, 4 * p + 2 * h + 1)
                    dve.tensor_scalar(var2[:, h, 1, :], var2[:, h, 0, :], EPS, None, ALU.add).then_inc(s_v2, 1)
                    dve.wait_ge(s_v2, 4 * p + 2 * h + 2)
                    dve.reciprocal(inv2[:, h, 0, :], var2[:, h, 1, :]).then_inc(s_in, 1)
                for h in range(2):
                    dve.wait_ge(s_rt, 6 * p + 3 + 2 * h)
                    for t in range(TB):
                        dve.tensor_scalar(flat[:, h, t, :], row_tile(X, 2 * p + h, t), ln[h][1].mv[:, t, 0:1],
                                          ln[h][1].rstd[:, t:t + 1], ALU.subtract, ALU.mult).then_inc(s_f, 1)
                if not last:
                    y_moments(p + 1)
                for h in range(2):
                    dve.wait_ge(s_a, 2 * p + h + 1)
                    dve.tensor_tensor(XA[:, bass.ds((2 * p + h) * S, S)], a_ps[h][:, :], fT[:, h, :], ALU.add).then_inc(s_xa, 1)
                dve.wait_ge(s_xa, 2 * p + 4)

            pairs(dve, body)

        @block.scalar
        def _(act):
            act.wait_ge(s_w, 32)
            def y_roots(p):
                for h in range(2):
                    act.wait_ge(s_in, 6 * p + h + 1)
                    act.activation(ln[h][0].rstd[:, :], ln[h][0].inv[:, :], ACT.Sqrt).then_inc(s_rt, 1)

            y_roots(0)

            def body(p, last):
                for h in range(2):
                    act.wait_ge(s_in, 6 * p + 3 + 2 * h)
                    act.activation(ln[h][1].rstd[:, :], ln[h][1].inv[:, :], ACT.Sqrt).then_inc(s_rt, 1)
                    act.wait_ge(s_in, 6 * p + 4 + 2 * h)
                    act.activation(rstd2[:, h, 0, :], inv2[:, h, 0, :], ACT.Sqrt).then_inc(s_rt, 1)
                for h in range(2):
                    act.wait_ge(s_tr, 4 * p + 1 + h)
                    act.activation(fT[:, h, :], t_ps[h][:, :], ACT.Identity, bias=vec[:, 2:3]).then_inc(s_T, 1)
                for h in range(2):
                    act.wait_ge(s_tr, 4 * p + 3 + h)
                    act.activation(hT[:, h, :], t_ps[h][:, :], ACT.Identity, scale=vec[:, 0:1], bias=vec[:, 1:2]).then_inc(s_T, 1)
                if not last:
                    y_roots(p + 1)

            pairs(act, body)

        @block.gpsimd
        def _(pool):
            with pool.Fori(0, B // 2) as p:
                for h in range(2):
                    pool.wait_ge(s_zn, TB * (2 * p + h + 1))
                    rows = X[:, bass.ds((2 * p + h) * TB, TB), :]
                    pool.tensor_tensor(rows, rows, zn[:, h, :, :], ALU.add).then_inc(s_x, 1)
                    pool.wait_ge(s_x, 2 * p + h + 1)
                for h in range(2):
                    pool.wait_ge(s_f, TB * (2 * p + h + 1))
                    pool.wait_ge(s_rt, 6 * p + 4 + 2 * h)
                    pool.tensor_tensor(xh[:, h, :, :], flat[:, h, :, :],
                                       rstd2[:, h, 0, :].unsqueeze(2).broadcast_to([P, TB, D]), ALU.mult).then_inc(s_h, 1)
                    pool.wait_ge(s_h, 2 * p + h + 1)

        @block.tensor
        def _(pe):
            pe.wait_ge(s_w, 32)
            with pe.Fori(0, B // 2) as p:
                for h in range(2):
                    pe.wait_ge(s_f, TB * (2 * p + h + 1))
                    for t in range(TB):
                        mm = pe.transpose(t_ps[h][:, t * P:(t + 1) * P], flat[:, h, t, :], ident[:, :])
                    mm.then_inc(s_tr, 1)
                for h in range(2):
                    pe.wait_ge(s_h, 2 * p + h + 1)
                    pe.wait_ge(s_T, 4 * p + 1 + h)
                    for t in range(TB):
                        mm = pe.transpose(t_ps[h][:, t * P:(t + 1) * P], xh[:, h, t, :], ident[:, :])
                    mm.then_inc(s_tr, 1)
                for h in range(2):
                    pe.wait_ge(s_T, 4 * p + 3 + h)
                    pe.wait_ge(s_xa, 2 * p + h + 1)
                    for c in range(2):
                        mm = pe.matmul(a_ps[h][:, c * 512:(c + 1) * 512], W[:, :], hT[:, h, c * 512:(c + 1) * 512],
                                       start=True, stop=True)
                    mm.then_inc(s_a, 1)


E1 = 8
CH = B * S // (2 * E1)
CT = CH // P


def static_experts(nc, io, keep):
    XA, Z = keep["XA"], keep["Z"]
    with ExitStack() as ctx:
        m = Scope(nc, ctx, "p9_")
        W1, W2, Wn, b12, bn = (keep[k] for k in ("f_w1", "f_w2", "next_w", "f_b12", "next_b_rows"))
        hT = m.sb("hT", [P, 2, FC, CH])
        eoT = m.sb("eoT", [P, 2, CH])
        pre = m.sb("pre", [P, 2, CT, D])
        h_ps = [m.ps(f"h_ps{r}", [P, FC, CH]) for r in range(2)]
        e_ps = [m.ps(f"e_ps{r}", [P, CH]) for r in range(2)]
        n_ps = [m.ps(f"n_ps{r}", [P, CT, D]) for r in range(2)]

        s_h = m.sem("h_ready")
        s_g = m.sem("h_gelu")
        s_eo = m.sem("eo_ready")
        s_ek = m.sem("eo_kept")
        s_n = m.sem("next_ready")
        s_nb = m.sem("next_biased")
        s_z = m.sem("z_ready")
        apart = keep["apart"]
        block = ctx.enter_context(nc.Block())

        def micro_batches(eng, body):
            with eng.Fori(0, 1) as k:
                body(k, False)
            body(1, True)

        @block.tensor
        def _(pe):
            def first(k, i):
                n, e = k * E1 + i, i % E1
                pe.wait_ge(s_g, FC * n + FC)
                for c in range(FC):
                    mm = pe.matmul(h_ps[i % 2][:, c, :], W1[:, e, c * P:(c + 1) * P], XA[:, bass.ds(n * CH, CH)],
                                   start=True, stop=True)
                mm.then_inc(s_h, 1)

            def second(k, i):
                n, e = k * E1 + i, i % E1
                pe.wait_ge(s_g, FC * n + 3 * FC)
                pe.wait_ge(s_ek, n + 1)
                for c in range(FC):
                    mm = pe.matmul(e_ps[i % 2][:, :], W2[:, e, c, :], hT[:, i % 2, c, :], start=(c == 0), stop=(c == FC - 1))
                mm.then_inc(s_eo, 1)

            def third(k, i):
                n = k * E1 + i
                pe.wait_ge(s_ek, n + 3)
                pe.wait_ge(s_nb, n + 1)
                for t in range(CT):
                    mm = pe.matmul(n_ps[i % 2][:, t, :], eoT[:, i % 2, t * P:(t + 1) * P], Wn[:, :], start=True, stop=True)
                mm.then_inc(s_n, 1)

            first(0, 0)
            first(0, 1)
            second(0, 0)

            def body(k, last):
                for i in range(E1):
                    if not (last and i + 2 >= E1):
                        first(k, i + 2)
                    if not (last and i + 1 >= E1):
                        second(k, i + 1)
                    third(k, i)

            micro_batches(pe, body)

        @block.scalar
        def _(act):
            def gelu(k, i):
                n, e = k * E1 + i, i % E1
                act.wait_ge(s_eo, n + 1)
                act.wait_ge(s_h, n + 1)
                for c in range(FC):
                    act.activation(hT[:, i % 2, c, :], h_ps[i % 2][:, c, :], ACT.Gelu, bias=b12[:, e, c:c + 1]).then_inc(s_g, 1)

            act.sem_inc(s_g, 2 * FC)
            act.sem_inc(s_z, 2)
            gelu(0, 0)
            gelu(0, 1)

            def body(k, last):
                for i in range(E1):
                    if not (last and i + 2 >= E1):
                        gelu(k, i + 2)
                    n = k * E1 + i
                    act.wait_ge(s_nb, n + 3)
                    act.sem_inc(apart["act"], 1)
                    act.activation(Z[:, bass.ds(n * CT, CT), :], pre[:, i % 2, :, :], ACT.Gelu).then_inc(s_z, 1)

            micro_batches(act, body)

        @block.vector
        def _(dve):
            def expert_bias(k, i):
                n, e = k * E1 + i, i % E1
                dve.wait_ge(s_n, n + 1)
                dve.wait_ge(s_eo, n + 3)
                dve.tensor_scalar(eoT[:, i % 2, :], e_ps[i % 2][:, :], b12[:, e, FC:FC + 1], None, ALU.add).then_inc(s_ek, 1)

            dve.sem_inc(s_eo, 2)
            dve.sem_inc(s_ek, 2)
            dve.sem_inc(s_n, 2)
            dve.sem_inc(s_nb, 2)
            expert_bias(0, 0)

            def body(k, last):
                for i in range(E1):
                    if not (last and i + 1 >= E1):
                        expert_bias(k, i + 1)
                    n = k * E1 + i
                    dve.wait_ge(s_z, n + 1)
                    dve.wait_ge(s_n, n + 3)
                    dve.tensor_tensor(pre[:, i % 2, :, :], n_ps[i % 2][:, :, :],
                                      bn[:, :].unsqueeze(1).broadcast_to([P, CT, D]), ALU.add).then_inc(s_nb, 1)

            micro_batches(dve, body)


def finish_rows(nc, io, keep):
    X, Z = keep["X"], keep["Z"]
    with ExitStack() as ctx:
        m = Scope(nc, ctx, "p10_")
        zn = m.sb("zn", [P, 2, TB, D])
        ln = [Moments(m, f"z{h}") for h in range(2)]
        s_ln = MomentSems(m)
        s_rt, s_zn = m.sem("rstd_ready"), m.sem("z_normed")
        s_x = [m.sem(f"x_updated{h}") for h in range(2)]
        s_out = m.sem("x_stored")
        apart = keep["apart"]["dve"]
        block = ctx.enter_context(nc.Block())

        @block.vector
        def _(dve):
            for h in range(2):
                dve.sem_inc(s_x[h], 1)
            with dve.Fori(0, B // 2) as p:
                for h in range(2):
                    moments(dve, s_ln, apart, ln[h], 2 * p + h, lambda t: row_tile(Z, 2 * p + h, t))
                for h in range(2):
                    dve.wait_ge(s_rt, 2 * p + h + 1)
                    dve.wait_ge(s_x[h], p + 1)
                    for t in range(TB):
                        dve.tensor_scalar(zn[:, h, t, :], row_tile(Z, 2 * p + h, t), ln[h].mv[:, t, 0:1],
                                          ln[h].rstd[:, t:t + 1], ALU.subtract, ALU.mult).then_inc(s_zn, 1)
                dve.wait_ge(s_zn, TB * (2 * p + 2))
                rows = X[:, bass.ds((2 * p + 1) * TB, TB), :]
                dve.tensor_tensor(rows, rows, zn[:, 1, :, :], ALU.add).then_inc(s_x[1], 1)

        @block.scalar
        def _(act):
            with act.Fori(0, B // 2) as p:
                for h in range(2):
                    act.wait_ge(s_ln.inv, 2 * p + h + 1)
                    act.activation(ln[h].rstd[:, :], ln[h].inv[:, :], ACT.Sqrt).then_inc(s_rt, 1)

        @block.gpsimd
        def _(pool):
            with pool.Fori(0, B // 2) as p:
                pool.wait_ge(s_zn, TB * (2 * p + 1))
                rows = X[:, bass.ds(2 * p * TB, TB), :]
                pool.tensor_tensor(rows, rows, zn[:, 0, :, :], ALU.add).then_inc(s_x[0], 1)
                pool.wait_ge(s_x[0], p + 2)

        @block.sync
        def _(sp):
            with sp.Fori(0, B // 2) as p:
                for h in range(2):
                    sp.wait_ge(s_x[h], p + 2)
                    sp.dma_start(io["out"][bass.ds(2 * p + h, 1), :, :].rearrange("b (t p) d -> p (b t) d", p=P),
                                 X[:, bass.ds((2 * p + h) * TB, TB), :]).then_inc(s_out, 16)
            sp.wait_ge(s_out, 16 * B)


def build(nc, io):
    with ExitStack() as ctx:
        m = Scope(nc, ctx)
        apart = {e: m.sem(f"{e}_apart") for e in ("act", "dve", "pool")}
        keep = {"apart": apart, "X": m.sb("X", [P, T, D]), "ident": m.sb("ident", [P, P])}
        with ExitStack() as attn:
            a = Scope(nc, attn)
            keep["tri"] = a.sb("tri", [P, 4 * P])
            keep["Q4"] = a.sb("q_operands", [P, G, GH, S], BF16)
            keep["K4"] = a.sb("k_operands", [P, G, GH, S], BF16)
            keep["Vg"] = a.sb("v_groups", [P, B * G, TB, GH * HD])
            keep["Vone"] = a.sb("v_with_ones", [P, 2, TB, GH, 32])
            keep["operands_loaded"] = [a.sem(f"operands_loaded{g}") for g in range(G)]
            project_heads(nc, io, keep)
            causal_attention(nc, io, keep)
        for name in ("qT", "kT"):
            keep[name] = m.sb(name, [P, B * S])
        keep["VP"] = m.sb("VP", [P, T, D])
        with ExitStack() as moe:
            a = Scope(nc, moe)
            for name, shape, dt in (("XN", [P, T, D], F32), ("XH", [P, T, D], F32), ("aff", [P, T, E0], F32),
                                    ("w1_all", [P, E0, F0], F32), ("w2_all", [P, E0, FC, D], F32),
                                    ("ln_b1", [P, E0, 2 + FC], F32), ("b2_rows", [P, E0, D], F32),
                                    ("gate", [P, T], F32), ("pos", [P, T], U32), ("tile_expert", [P, MAXTILES], I32)):
                keep[name] = a.sb(name, shape, dt)
            merge_heads(nc, io, keep)
            route(nc, io, keep)
            experts(nc, io, keep)
            combine_and_project(nc, io, keep)
        keep["Y"] = m.sb("Y", [P, T, D])
        for name, shape in (("f_w1", [P, E1, F0]), ("f_w2", [P, E1, FC, D]), ("next_w", [P, D]),
                            ("f_b12", [P, E1, FC + 1]), ("next_b_rows", [P, D])):
            keep[name] = m.sb(name, shape)
        banded_attention(nc, io, keep)
        keep["XA"] = m.sb("XA", [P, B * S])
        ffn_inputs(nc, io, keep)
        keep["Z"] = keep["Y"]
        static_experts(nc, io, keep)
        finish_rows(nc, io, keep)


def kernel(**inputs):
    import concourse.bacc as bacc
    from concourse.bass_utils import run_bass_kernel_spmd

    order = np.arange(D).reshape(G, GH, HD).transpose(0, 2, 1).reshape(-1)
    swap = order ^ 1
    turned = [np.asarray(inputs[f"L0_attn_W{k}"]).T for k in "qkvo"]
    Wq, Wk, Wv, Wo = turned
    arrays = {
        "x": np.asarray(inputs["L0_attn_x"]),
        "l0_w": np.stack([Wq[:, order], Wq[:, swap], Wk[:, order], Wk[:, swap], Wv, Wo], axis=1),
    }
    A = {k: np.asarray(v) for k, v in inputs.items()}
    per_row = lambda w: w.reshape(E0, -1, P).transpose(2, 0, 1)
    arrays["centroids"] = A["L0_ffn_centroids"].T
    arrays["w1"] = A["L0_ffn_w1"].transpose(2, 0, 1)
    arrays["w2"] = A["L0_ffn_w2"].transpose(2, 0, 1).reshape(FC, P, E0, D).transpose(1, 2, 0, 3)
    arrays["small"] = np.concatenate([per_row(A["L0_ffn_ln_g"]), per_row(A["L0_ffn_ln_b"]), per_row(A["L0_ffn_b1"])], -1)
    arrays["b2"] = A["L0_ffn_b2"]
    qkv = A["L1_attn_W_qkv"]
    arrays["l1_w"] = np.stack([qkv[:, 0:D], qkv[:, D:2 * D], qkv[:, 2 * D:], A["L1_attn_W_proj"]], 1)
    arrays["b_qkv"] = A["L1_attn_b_qkv"].reshape(3, D).T
    arrays["b_proj"] = A["L1_attn_b_proj"]
    arrays["attn_w"] = A["L1_ffn_attn_w"].T
    arrays["ffn_vectors"] = np.stack([A["L1_ffn_ln_scale"], A["L1_ffn_ln_bias"], A["L1_ffn_attn_b"]], 1)
    arrays["f_w1"] = A["L1_ffn_w1"].transpose(1, 0, 2)
    arrays["f_w2"] = A["L1_ffn_w2"].reshape(E1, FC, P, D).transpose(2, 0, 1, 3)
    arrays["f_b12"] = np.concatenate([per_row(A["L1_ffn_b1"]), per_row(A["L1_ffn_b2"])], -1)
    arrays["next_w"] = A["L1_ffn_next_w"].T
    arrays["next_b"] = A["L1_ffn_next_b"]
    freq = (1.0 / 10000.0 ** (np.arange(0, HD, 2, dtype=np.float32) / HD)).astype(np.float32)
    angle = np.outer(np.arange(S, dtype=np.float32), freq)
    angle = np.concatenate([angle, angle], -1).T
    sign = np.where(np.arange(HD) % 2 == 0, -1.0, 1.0).astype(np.float32)[:, None]
    arrays["rope"] = np.stack([np.tile(np.cos(angle), (H, 1))[order], np.tile(np.sin(angle) * sign, (H, 1))[order]], 1).astype(np.float32)

    nc = bacc.Bacc("TRN2", target_bir_lowering=False, num_devices=1)
    io, feed = {}, {}
    for name, a in arrays.items():
        feed["in_" + name] = np.ascontiguousarray(a)
        io[name] = nc.dram_tensor("in_" + name, a.shape, mybir.dt.from_np(a.dtype), kind="ExternalInput").ap()
    io["q_parts"] = nc.dram_tensor("q_parts", (3, B, D, S), BF16, kind="Internal").ap()
    io["k_parts"] = nc.dram_tensor("k_parts", (3, B, D, S), BF16, kind="Internal").ap()
    io["heads_out"] = nc.dram_tensor("heads_out", (B * G, P, S), F32, kind="Internal").ap()
    io["inv_sums"] = nc.dram_tensor("inv_sums", (B * H, S), F32, kind="Internal").ap()
    io["sorted_in"] = nc.dram_tensor("sorted_in", (MAXTILES * P, D), F32, kind="Internal").ap()
    io["sorted_out"] = nc.dram_tensor("sorted_out", (MAXTILES * P, D), F32, kind="Internal").ap()
    io["out"] = nc.dram_tensor("out_0", (B, S, D), F32, kind="ExternalOutput").ap()
    build(nc, io)
    return run_bass_kernel_spmd(nc, [feed], core_ids=[0]).results[0]["out_0"]
```
